# Optimizing a Trainium2 kernel written in Bass

```python
import numpy as np
import jax
import jax.numpy as jnp

def _softmax(x, axis=-1):
    return jax.nn.softmax(x, axis=axis)

def _gelu(x):
    return jax.nn.gelu(x, approximate=True)

def _silu(x):
    return jax.nn.silu(x)

def _sigmoid(x):
    return jax.nn.sigmoid(x)

def _layernorm(x, axis=-1, eps=1e-05):
    m = jnp.mean(x, axis=axis, keepdims=True)
    v = jnp.var(x, axis=axis, keepdims=True)
    return (x - m) / jnp.sqrt(v + eps)

def _scatter_add(tgt, idx, src, axis=0):
    return tgt.at[idx].add(src)

def _segment_sum(src, seg, n):
    return jax.ops.segment_sum(src, seg, n)
kernel_name = 'mk_gnn_preln_d4_gnn_r8_237f89'

def setup_inputs(seed: int=0):
    np.random.seed(seed)
    _w = jnp.asarray

    def _rec_inputs():
        import jax
        import jax.numpy as jnp
        _gk = jax.random.key(seed)
        x = -0.0003713 + 1 * jax.random.normal(jax.random.fold_in(_gk, 1), (6250, 128), jnp.float32)
        _s = jax.random.randint(jax.random.fold_in(_gk, 2), (50000,), 0, 6250, jnp.int32)
        _d = jax.random.randint(jax.random.fold_in(_gk, 3), (50000,), 0, 6250, jnp.int32)
        _loop = jnp.arange(6250, dtype=jnp.int32)
        src = jnp.concatenate([_s, _d, _loop])
        dst = jnp.concatenate([_d, _s, _loop])
        _o = jnp.argsort(dst, stable=True)
        src = src[_o]
        dst = dst[_o]
        edge_attr_128 = -8.16379e-05 + 0.999858 * jax.random.normal(jax.random.fold_in(_gk, 12), (106250, 128), jnp.float32)
        edge_type_7 = jax.random.randint(jax.random.fold_in(_gk, 14), (106250,), 0, 7, jnp.int32)
        node_type_4 = jax.random.randint(jax.random.fold_in(_gk, 15), (6250,), 0, 4, jnp.int32)
        return (x, src, dst, edge_attr_128, edge_type_7, node_type_4)
    x, src, dst, edge_attr_128, edge_type_7, node_type_4 = _rec_inputs()

    def _L0_gnn_setup():
        import jax, jax.numpy as jnp
        import numpy as np
        NEG_SLOPE = 0.2
        EPS = 1e-16
        key = jax.random.key(seed)
        k1, k2, k3, k4, k5 = jax.random.split(key, 5)
        N, E, IN, H, F = (12500, 100000, 128, 8, 16)
        x = jax.random.normal(k1, (N, IN), dtype=jnp.float32)
        edge_index = jax.random.randint(k2, (2, E), 0, N, dtype=jnp.int32)
        W_proj = jax.random.normal(k3, (IN, H * F), dtype=jnp.float32) * (1.0 / np.sqrt(IN))
        a_src = jax.random.normal(k4, (1, H, F), dtype=jnp.float32) * 0.1
        a_trg = jax.random.normal(k5, (1, H, F), dtype=jnp.float32) * 0.1
        bias = jnp.zeros((H * F,), dtype=jnp.float32)
        return {'x': x, 'edge_index': edge_index, 'W_proj': W_proj, 'a_src': a_src, 'a_trg': a_trg, 'bias': bias}
    _L0_gnn_all = _L0_gnn_setup()
    _L0_gnn_in = {k: v for k, v in _L0_gnn_all.items() if k in ('W_proj', 'a_src', 'a_trg', 'bias')}
    del _L0_gnn_all

    def _L1_gnn_setup():
        import jax, jax.numpy as jnp
        import numpy as np
        NUM_STEPS = 1

        def _seg_mean(vals, idx, num_nodes):
            s = jax.ops.segment_sum(vals, idx, num_segments=num_nodes)
            cnt = jax.ops.segment_sum(jnp.ones((vals.shape[0],), vals.dtype), idx, num_segments=num_nodes)
            return s / jnp.maximum(cnt, 1.0)[:, None]

        def _gru_cell(a, h, w_ih, w_hh, b_ih, b_hh):
            gi = a @ w_ih.T + b_ih
            gh = h @ w_hh.T + b_hh
            H = h.shape[1]
            i_r, i_z, i_n = (gi[:, :H], gi[:, H:2 * H], gi[:, 2 * H:])
            h_r, h_z, h_n = (gh[:, :H], gh[:, H:2 * H], gh[:, 2 * H:])
            r = jax.nn.sigmoid(i_r + h_r)
            z = jax.nn.sigmoid(i_z + h_z)
            n = jnp.tanh(i_n + r * h_n)
            return (1.0 - z) * n + z * h
        key = jax.random.key(seed)
        ks = jax.random.split(key, 8)
        N, E, H = (12500, 80000, 128)
        sc = 1.0 / np.sqrt(H)
        feat = jax.random.normal(ks[0], (N, H), jnp.float32)
        src = jax.random.randint(ks[1], (E,), 0, N, jnp.int32)
        dst = jax.random.randint(ks[2], (E,), 0, N, jnp.int32)
        W_in = jax.random.normal(ks[3], (H, H), jnp.float32) * sc
        W_out = jax.random.normal(ks[4], (H, H), jnp.float32) * sc
        w_ih = jax.random.normal(ks[5], (3 * H, 2 * H), jnp.float32) * sc
        w_hh = jax.random.normal(ks[6], (3 * H, H), jnp.float32) * sc
        return {'feat': feat, 'src': src, 'dst': dst, 'W_in': W_in, 'b_in': jnp.zeros((H,), jnp.float32), 'W_out': W_out, 'b_out': jnp.zeros((H,), jnp.float32), 'w_ih': w_ih, 'w_hh': w_hh, 'b_ih': jnp.zeros((3 * H,), jnp.float32), 'b_hh': jnp.zeros((3 * H,), jnp.float32)}
    _L1_gnn_all = _L1_gnn_setup()
    _L1_gnn_in = {k: v for k, v in _L1_gnn_all.items() if k in ('W_in', 'b_in', 'W_out', 'b_out', 'w_ih', 'w_hh', 'b_ih', 'b_hh')}
    del _L1_gnn_all

    def _L2_gnn_setup():
        import jax, jax.numpy as jnp
        import numpy as np
        N = 12500
        E = 200000
        C_IN = 128
        C_OUT = 128
        R = 7
        T = 4
        key = jax.random.key(seed)
        ks = jax.random.split(key, 7)
        x = jax.random.normal(ks[0], (N, C_IN), dtype=jnp.float32)
        edge_index = jax.random.randint(ks[1], (2, E), 0, N, dtype=jnp.int32)
        edge_type = jax.random.randint(ks[2], (E,), 0, R, dtype=jnp.int32)
        target_node_type = jax.random.randint(ks[3], (N,), 0, T, dtype=jnp.int32)
        rel_w = jax.random.normal(ks[4], (R, C_OUT, C_IN), dtype=jnp.float32) * (1.0 / np.sqrt(C_IN))
        root_w = jax.random.normal(ks[5], (T, C_OUT, C_IN), dtype=jnp.float32) * (1.0 / np.sqrt(C_IN))
        root_b = jax.random.normal(ks[6], (T, C_OUT), dtype=jnp.float32) * 0.01
        return {'x': x, 'edge_index': edge_index, 'edge_type': edge_type, 'target_node_type': target_node_type, 'rel_w': rel_w, 'root_w': root_w, 'root_b': root_b}
    _L2_gnn_all = _L2_gnn_setup()
    _L2_gnn_in = {k: v for k, v in _L2_gnn_all.items() if k in ('rel_w', 'root_w', 'root_b')}
    del _L2_gnn_all

    def _L3_gnn_setup():
        import jax, jax.numpy as jnp
        import numpy as np
        N_NODES = 6250
        N_EDGES = 100000
        D_FEAT = 128
        N_HEADS = 4
        HEAD_DIM = 32

        def mish(x):
            return x * jnp.tanh(jax.nn.softplus(x))
        key = jax.random.key(seed)
        ks = jax.random.split(key, 12)
        s = 1.0 / np.sqrt(D_FEAT)
        return {'nodes': jax.random.normal(ks[0], (N_NODES, D_FEAT), jnp.float32), 'edges': jax.random.normal(ks[1], (N_EDGES, D_FEAT), jnp.float32), 'Ws_k': jax.random.normal(ks[2], (D_FEAT, N_HEADS, HEAD_DIM), jnp.float32) * s, 'Ws_b': jnp.zeros((N_HEADS, HEAD_DIM), jnp.float32), 'Wr_k': jax.random.normal(ks[3], (D_FEAT, N_HEADS, HEAD_DIM), jnp.float32) * s, 'Wr_b': jnp.zeros((N_HEADS, HEAD_DIM), jnp.float32), 'We_k': jax.random.normal(ks[4], (D_FEAT, N_HEADS, HEAD_DIM), jnp.float32) * s, 'We_b': jnp.zeros((N_HEADS, HEAD_DIM), jnp.float32), 'attn_w': jax.random.normal(ks[5], (HEAD_DIM, 1), jnp.float32) / np.sqrt(HEAD_DIM), 'attn_b': jnp.zeros((1,), jnp.float32), 'senders': jax.random.randint(ks[6], (N_EDGES,), 0, N_NODES, jnp.int32), 'receivers': jax.random.randint(ks[7], (N_EDGES,), 0, N_NODES, jnp.int32)}
    _L3_gnn_all = _L3_gnn_setup()
    _L3_gnn_in = {k: v for k, v in _L3_gnn_all.items() if k in ('Ws_k', 'Ws_b', 'Wr_k', 'Wr_b', 'We_k', 'We_b', 'attn_w', 'attn_b')}
    del _L3_gnn_all
    return {'x': x, 'src': src, 'dst': dst, 'edge_attr_128': edge_attr_128, 'edge_type_7': edge_type_7, 'node_type_4': node_type_4, 'L0_gnn_W_proj': _L0_gnn_in['W_proj'], 'L0_gnn_a_src': _L0_gnn_in['a_src'], 'L0_gnn_a_trg': _L0_gnn_in['a_trg'], 'L0_gnn_bias': _L0_gnn_in['bias'], 'L1_gnn_W_in': _L1_gnn_in['W_in'], 'L1_gnn_b_in': _L1_gnn_in['b_in'], 'L1_gnn_W_out': _L1_gnn_in['W_out'], 'L1_gnn_b_out': _L1_gnn_in['b_out'], 'L1_gnn_w_ih': _L1_gnn_in['w_ih'], 'L1_gnn_w_hh': _L1_gnn_in['w_hh'], 'L1_gnn_b_ih': _L1_gnn_in['b_ih'], 'L1_gnn_b_hh': _L1_gnn_in['b_hh'], 'L2_gnn_rel_w': _L2_gnn_in['rel_w'], 'L2_gnn_root_w': _L2_gnn_in['root_w'], 'L2_gnn_root_b': _L2_gnn_in['root_b'], 'L3_gnn_Ws_k': _L3_gnn_in['Ws_k'], 'L3_gnn_Ws_b': _L3_gnn_in['Ws_b'], 'L3_gnn_Wr_k': _L3_gnn_in['Wr_k'], 'L3_gnn_Wr_b': _L3_gnn_in['Wr_b'], 'L3_gnn_We_k': _L3_gnn_in['We_k'], 'L3_gnn_We_b': _L3_gnn_in['We_b'], 'L3_gnn_attn_w': _L3_gnn_in['attn_w'], 'L3_gnn_attn_b': _L3_gnn_in['attn_b']}

def reference(x, src, dst, edge_attr_128, edge_type_7, node_type_4, L0_gnn_W_proj, L0_gnn_a_src, L0_gnn_a_trg, L0_gnn_bias, L1_gnn_W_in, L1_gnn_b_in, L1_gnn_W_out, L1_gnn_b_out, L1_gnn_w_ih, L1_gnn_w_hh, L1_gnn_b_ih, L1_gnn_b_hh, L2_gnn_rel_w, L2_gnn_root_w, L2_gnn_root_b, L3_gnn_Ws_k, L3_gnn_Ws_b, L3_gnn_Wr_k, L3_gnn_Wr_b, L3_gnn_We_k, L3_gnn_We_b, L3_gnn_attn_w, L3_gnn_attn_b):
    import jax
    import jax.numpy as jnp

    def _L0_gnn_ref(x, edge_index, W_proj, a_src, a_trg, bias):
        import jax, jax.numpy as jnp
        import numpy as np
        NEG_SLOPE = 0.2
        EPS = 1e-16
        N = x.shape[0]
        H, F = (a_src.shape[1], a_src.shape[2])
        h = (x @ W_proj).reshape(N, H, F)
        s_src = jnp.sum(h * a_src, axis=-1)
        s_trg = jnp.sum(h * a_trg, axis=-1)
        src, trg = (edge_index[0], edge_index[1])
        e = jax.nn.leaky_relu(s_src[src] + s_trg[trg], negative_slope=NEG_SLOPE)
        e = jnp.exp(e - jax.lax.stop_gradient(jnp.max(e)))
        denom = jax.ops.segment_sum(e, trg, num_segments=N)[trg]
        alpha = (e / (denom + EPS))[..., None]
        out = jax.ops.segment_sum(h[src] * alpha, trg, num_segments=N)
        out = out + h
        out = out.reshape(N, H * F) + bias
        return jax.nn.elu(out)

    def _L1_gnn_ref(feat, src, dst, W_in, b_in, W_out, b_out, w_ih, w_hh, b_ih, b_hh):
        import jax, jax.numpy as jnp
        import numpy as np
        NUM_STEPS = 1

        def _seg_mean(vals, idx, num_nodes):
            s = jax.ops.segment_sum(vals, idx, num_segments=num_nodes)
            cnt = jax.ops.segment_sum(jnp.ones((vals.shape[0],), vals.dtype), idx, num_segments=num_nodes)
            return s / jnp.maximum(cnt, 1.0)[:, None]

        def _gru_cell(a, h, w_ih, w_hh, b_ih, b_hh):
            gi = a @ w_ih.T + b_ih
            gh = h @ w_hh.T + b_hh
            H = h.shape[1]
            i_r, i_z, i_n = (gi[:, :H], gi[:, H:2 * H], gi[:, 2 * H:])
            h_r, h_z, h_n = (gh[:, :H], gh[:, H:2 * H], gh[:, 2 * H:])
            r = jax.nn.sigmoid(i_r + h_r)
            z = jax.nn.sigmoid(i_z + h_z)
            n = jnp.tanh(i_n + r * h_n)
            return (1.0 - z) * n + z * h
        N = feat.shape[0]
        h = feat
        for _ in range(NUM_STEPS):
            feat_in = h @ W_in.T + b_in
            feat_out = h @ W_out.T + b_out
            a_in = _seg_mean(feat_in[src], dst, N)
            a_out = _seg_mean(feat_out[dst], src, N)
            a = jnp.concatenate((a_in, a_out), axis=1)
            h = _gru_cell(a, h, w_ih, w_hh, b_ih, b_hh)
        return h

    def _L2_gnn_ref(x, edge_index, edge_type, target_node_type, rel_w, root_w, root_b):
        import jax, jax.numpy as jnp
        import numpy as np
        N = 12500
        E = 200000
        C_IN = 128
        C_OUT = 128
        R = 7
        T = 4
        n = x.shape[0]
        src, dst = (edge_index[0], edge_index[1])
        x_j = x[src]
        seg = dst.astype(jnp.int32) * R + edge_type
        sums = jax.ops.segment_sum(x_j, seg, num_segments=n * R).reshape(n, R, C_IN)
        cnt = jax.ops.segment_sum(jnp.ones((x_j.shape[0],), x.dtype), seg, num_segments=n * R).reshape(n, R)
        means = sums / jnp.maximum(cnt, 1.0)[:, :, None]
        out = jnp.einsum('nrc,roc->no', means, rel_w)
        for t in range(T):
            m = (target_node_type == t).astype(x.dtype)[:, None]
            out = out + m * (x @ root_w[t].T + root_b[t])
        return out

    def _L3_gnn_ref(nodes, edges, Ws_k, Ws_b, Wr_k, Wr_b, We_k, We_b, attn_w, attn_b, senders, receivers):
        import jax, jax.numpy as jnp
        import numpy as np
        N_NODES = 6250
        N_EDGES = 100000
        D_FEAT = 128
        N_HEADS = 4
        HEAD_DIM = 32

        def mish(x):
            return x * jnp.tanh(jax.nn.softplus(x))
        n = nodes.shape[0]
        sent = jnp.einsum('ef,fhd->ehd', nodes[senders], Ws_k) + Ws_b
        e_att = sent + jnp.einsum('ef,fhd->ehd', edges, We_k) + We_b
        recv = jnp.einsum('ef,fhd->ehd', nodes[receivers], Wr_k) + Wr_b
        logits = jnp.einsum('ehd,do->eho', mish(e_att + recv), attn_w) + attn_b
        seg_max = jax.ops.segment_max(logits, receivers, num_segments=n)
        w = jnp.exp(logits - seg_max[receivers])
        denom = jax.ops.segment_sum(w, receivers, num_segments=n)
        w = w / denom[receivers]
        msg = (w * e_att).reshape(e_att.shape[0], N_HEADS * HEAD_DIM)
        out_nodes = jax.ops.segment_sum(msg, receivers, num_segments=n)
        return out_nodes
    edge_index = jnp.stack([src, dst])
    h = jnp.maximum(_layernorm(x, axis=-1), 0.0)
    x = x + _L0_gnn_ref(h, edge_index, L0_gnn_W_proj, L0_gnn_a_src, L0_gnn_a_trg, L0_gnn_bias)
    h = jnp.maximum(_layernorm(x, axis=-1), 0.0)
    x = x + _L1_gnn_ref(h, src, dst, L1_gnn_W_in, L1_gnn_b_in, L1_gnn_W_out, L1_gnn_b_out, L1_gnn_w_ih, L1_gnn_w_hh, L1_gnn_b_ih, L1_gnn_b_hh)
    h = jnp.maximum(_layernorm(x, axis=-1), 0.0)
    x = x + _L2_gnn_ref(h, edge_index, edge_type_7, node_type_4, L2_gnn_rel_w, L2_gnn_root_w, L2_gnn_root_b)
    h = jnp.maximum(_layernorm(x, axis=-1), 0.0)
    x = x + _L3_gnn_ref(h, edge_attr_128, L3_gnn_Ws_k, L3_gnn_Ws_b, L3_gnn_Wr_k, L3_gnn_Wr_b, L3_gnn_We_k, L3_gnn_We_b, L3_gnn_attn_w, L3_gnn_attn_b, src, dst)
    return x

_drawn_inputs = setup_inputs


def setup_inputs(seed=0):
    import zlib

    import numpy as np

    out = dict(_drawn_inputs(seed))
    spreads = {'L0_gnn_bias': (0.0, 0.1),
     'L1_gnn_b_in': (0.0, 0.406),
     'L1_gnn_b_out': (0.0, 0.352),
     'L1_gnn_b_ih': (0.0, 0.305),
     'L1_gnn_b_hh': (0.0, 0.479),
     'L3_gnn_Ws_b': (0.0, 0.1),
     'L3_gnn_Wr_b': (0.0, 0.8),
     'L3_gnn_We_b': (0.0, 0.1)}
    factors = {'L0_gnn_a_trg': 39.985, 'L2_gnn_root_b': 8.0, 'L0_gnn_a_src': 2.967}
    for name, (base, spread) in spreads.items():
        noise = np.random.default_rng([zlib.crc32(name.encode()), seed]).standard_normal(out[name].shape)
        drawn = base * np.exp(spread * noise) if base else spread * noise
        out[name] = jnp.asarray(drawn.astype(out[name].dtype))
    for name, factor in factors.items():
        out[name] = (out[name] * factor).astype(out[name].dtype)
    return out
```

```python
from contextlib import ExitStack

import numpy as np

import concourse.bass as bass
from concourse import mybir

F32 = mybir.dt.float32
I32 = mybir.dt.int32
ALU = mybir.AluOpType
ACT = mybir.ActivationFunctionType
AX = mybir.AxisListType
DVE = mybir.EngineType.DVE
PE = mybir.EngineType.PE
SP = mybir.EngineType.SP

P = 128
D = 128
U = 8
RS = 4
TABLES = 8
BIG = 1e30
EPS_LN = 1e-5
SCAN_CHUNKS = 32


class Shape:
    def __init__(self, n, e, heads0, heads3, rels, types):
        self.n, self.e = n, e
        self.blocks = -(-n // P)
        self.nb = self.blocks + self.blocks % 2
        self.tiles = -(-e // P)
        self.steps = -(-(self.tiles + self.blocks - 1) // U) * U
        self.heads0, self.heads3, self.rels, self.node_types = heads0, heads3, rels, types
        self.ctiles = -(-self.tiles // SCAN_CHUNKS)
        self.stiles = self.ctiles * SCAN_CHUNKS


class Chain:

    def __init__(self, eng, sem, start=0):
        self.eng, self.sem, self.n = eng, sem, start

    def __call__(self, ins):
        self.n += 1
        ins.then_inc(self.sem, 1)
        self.eng.wait_ge(self.sem, self.n)


class Turn(Chain):

    def __init__(self, eng, sem, start, go):
        super().__init__(eng, sem)
        self.start, self.go = start, go

    def __call__(self, ins):
        self.n += 1
        ins.then_inc(self.sem, 1)
        hold(self.eng, self.sem, self.start + self.n, self.go)


def clear_ahead(pool, issued):
    pool.sem_inc(issued, 1)


def hold(eng, sem, value, go=None):
    if isinstance(value, int):
        if value > 0:
            eng.wait_ge(sem, value)
        return
    eng.wait_ge(sem, value)
    if go is not None:
        eng.wait_ge(go, 1)


def repeat(eng, n, turn):
    turn(0)
    if n > 1:
        with eng.Fori(1, n) as i:
            turn(i)


class Arena:

    def __init__(self, *arrays):
        self.parts = [[a[:].rearrange("p b d -> p (b d)"), 0] for a in arrays]

    def take(self, shape, dt=F32):
        n = int(np.prod(shape[1:]))
        n8 = -(-n // 16) * 16
        part = next(p for p in self.parts if p[1] + n8 <= p[0].shape[1])
        ap = part[0][0:shape[0], part[1]:part[1] + n]
        part[1] += n8
        if dt != F32:
            ap = ap.bitcast(dt)
        if len(shape) == 3:
            ap = ap.rearrange("p (a b) -> p a b", a=shape[1])
        if len(shape) == 4:
            ap = ap.rearrange("p (a b c) -> p a b c", a=shape[1], b=shape[2])
        return ap


class Program:
    def __init__(self, nc, shape, io):
        self.nc, self.s, self.io = nc, shape, io
        self.ctx = ExitStack()
        self.count = 0
        self.phase_sems = []

    def sb(self, name, shape, dt=F32, ctx=None):
        self.count += 1
        return (ctx or self.ctx).enter_context(self.nc.sbuf_tensor(f"{name}_{self.count}", shape, dt))

    def ps(self, name, ctx):
        return ctx.enter_context(self.nc.psum_tensor(name, [P, 512], F32))

    def sem(self, name):
        self.count += 1
        handle = self.nc.alloc_semaphore(f"{name}_{self.count}")
        self.phase_sems.append(handle)
        return handle

    def end_phase(self):
        self.nc.clear_and_free_semaphores(self.phase_sems)
        self.nc.all_engine_barrier()
        self.phase_sems = []

    def scratch(self, name, shape):
        return self.nc.dram_tensor(name, shape, F32, kind="Internal").ap()

    def regs(self, eng, row, i, top):
        _, v = self.nc.values_load_multi_w_load_instructions(
            row[0:1, bass.ds(i * U, U)], engines=[eng], min_val=0, max_val=top,
            skip_runtime_bounds_check_because="block and tile numbers are bounded when made")
        return v

    def bcast_row(self, ap, width):
        return ap.rearrange("(o w) -> o w", o=1).broadcast_to([P, width])

    def allocate(self):
        s = self.s
        nb, S = s.nb, s.steps
        self.x = self.sb("x_res", [P, nb, D])
        self.hn = self.sb("h_norm", [P, nb, D])
        self.acc = self.sb("acc", [P, nb, 136])
        self.aux = self.sb("aux", [P, nb, D])
        self.aux2 = self.sb("aux2", [P, nb, 136])
        self.wts = self.sb("edge_w", [P, max(S * 8, nb * 136)])
        self.w8 = self.wts[:, 0:S * 8].rearrange("p (s h) -> p s h", h=8)
        self.rel = self.sb("rel_dst", [P, S + U])
        self.srcf = self.sb("src_f", [P, S + U])
        self.src = self.sb("src_i", [P, S + U], I32)
        self.typ = self.sb("type_f", [P, S + U])
        self.blk = self.sb("step_block", [1, S], I32)
        self.til = self.sb("step_tile", [1, S + U], I32)
        self.strg = self.sb("target_scores", [P, nb, s.heads0])
        self.ahead = self.wts[:, 0:S + U]
        self.sidx = self.sb("scatter_rows", [P, S + U], I32)
        self.gidx = self.sb("relation_rows", [P, S + U], I32)
        self.w2 = self.sb("relation_weight", [P, S + U])
        self.inv = self.sb("inverse_counts", [P, nb, 8])
        self.gin = self.sb("has_in_edges", [P, nb])
        self.gout = self.sb("has_out_edges", [P, nb])
        self.mask = self.sb("mask", [P, S + U])
        self.iota = self.sb("iota_row", [P, P])
        self.ident = self.sb("ident", [P, P])
        self.pidx = self.sb("partition_index", [P, 1])
        self.ones = self.sb("ones", [P, P])
        self.issued = self.nc.alloc_semaphore("indirect_issued")
        self.setup_done = self.nc.alloc_semaphore("setup_done")
        rows = nb * P
        self.t_gat = self.scratch("t_gat", (rows, 136))
        self.t_h = self.scratch("t_h", (rows, D))
        self.t_rel = self.scratch("t_rel", (rows, s.rels, D))
        self.t_sent = self.scratch("t_sent", (rows, D))
        self.t_rows = self.scratch("t_rows", (S, P, D))
        self.t_out = [self.scratch(f"t_out{k}", (rows + P, 136)) for k in range(TABLES)]
        self.t_seq = self.scratch("t_seq", (s.stiles, s.heads3, P))
        self.t_max = self.scratch("t_max", (s.stiles, s.heads3, P))

    def prepare(self):
        nc, s, io = self.nc, self.s, self.io
        T, S, NF = s.tiles, s.steps, s.blocks - 1
        with ExitStack() as c:
            at = Arena(self.x, self.hn, self.acc)
            raw = at.take([P, T], I32)
            rawt = at.take([P, T], I32)
            dstf = at.take([P, S + U], F32)
            base = at.take([P, S + U], F32)
            on = at.take([P, S + U], F32)
            junk = at.take([P, S + U], F32)
            below = at.take([P, NF], F32)
            bi = at.take([P, S + U], I32)
            ti = at.take([P, S + U], I32)
            fi = at.take([P, NF], I32)
            io_i = at.take([P, P], I32)
            io_p = at.take([P, 1], I32)
            io_t = at.take([P, S + U], I32)
            row0 = at.take([P, P], F32)
            thr = at.take([P, NF], F32)
            thi = at.take([P, NF], I32)
            psA = [self.ps(f"p_first{k}", c) for k in range(-(-T // 512))]
            psB = self.ps("p_below", c)
            loaded, made, seq = self.sem("loaded"), self.sem("iotas"), self.sem("seq")
            rows_ready, counted, summed = self.sem("dst_ready"), self.sem("counted"), self.sem("summed")
            moved = self.sem("moved")
            block = c.enter_context(nc.Block())

            @block.sync
            def _(sp):
                sp.dma_start(raw[:], io["dst_t"]).then_inc(loaded, 16)
                sp.dma_start(rawt[:], io["type_t"]).then_inc(loaded, 16)
                sp.dma_start(self.src[:, 0:T], io["src_t"]).then_inc(loaded, 16)

            @block.gpsimd
            def _(pool):
                nc.gpsimd.iota(io_i[:], pattern=[[1, P]], base=0, channel_multiplier=0).then_inc(made, 1)
                nc.gpsimd.iota(io_p[:], pattern=[[0, 1]], base=0, channel_multiplier=1).then_inc(made, 1)
                nc.gpsimd.iota(io_t[:], pattern=[[1, S + U]], base=0, channel_multiplier=0).then_inc(made, 1)
                nc.gpsimd.iota(thi[:], pattern=[[P, NF]], base=P, channel_multiplier=0).then_inc(made, 1)

            @block.tensor
            def _(pe):
                pe.wait_ge(rows_ready, 1)
                for k, p in enumerate(psA):
                    w = min(512, T - 512 * k)
                    nc.tensor.matmul(p[:, 0:w], row0[:], dstf[:, 512 * k:512 * k + w],
                                     start=True, stop=True).then_inc(summed, 1)
                pe.wait_ge(counted, 1)
                nc.tensor.matmul(psB[:, 0:NF], self.ones[:], below[:], start=True, stop=True).then_inc(summed, 1)

            @block.vector
            def _(dve):
                v = nc.vector
                do = Chain(dve, seq)
                do(v.memset(self.ones[:], 1.0))
                do(v.memset(dstf[:], float((s.blocks + 1) * P)))
                do(v.memset(self.typ[:], 0.0))
                do(v.memset(self.srcf[:], 0.0))
                do(v.memset(on[:], 0.0))
                do(v.memset(on[:, 0:T], 1.0))
                do(v.memset(base[:], 0.0))
                do(v.memset(bi[:], 0))
                do(v.memset(self.rel[:], 0.0))
                dve.wait_ge(made, 4)
                do(v.tensor_copy(self.iota[:], io_i[:]))
                do(v.tensor_copy(self.pidx[:], io_p[:]))
                do(v.tensor_copy(thr[:], thi[:]))
                do(v.tensor_copy(ti[:], io_t[:]))
                do(v.tensor_scalar(self.ident[:], self.iota[:], self.pidx[:, 0:1], None, ALU.is_equal))
                do(v.memset(row0[:], 0.0))
                do(v.memset(row0[0:1, :], 1.0))
                dve.wait_ge(loaded, 48)
                do(v.tensor_copy(self.typ[:, 0:T], rawt[:]))
                do(v.tensor_copy(self.srcf[:, 0:T], self.src[:, 0:T]))
                v.tensor_copy(dstf[:, 0:T], raw[:]).then_inc(rows_ready, 1)
                dve.wait_ge(rows_ready, 1)
                def turn(k):
                    hold(dve, moved, k)
                    v.tensor_scalar(junk[:, 0:T], dstf[:, 0:T], thr[:, bass.ds(k, 1)], 0.0,
                                    ALU.is_lt, ALU.add, accum_out=below[:, bass.ds(k, 1)]).then_inc(moved, 1)
                repeat(dve, NF, turn)
                dve.wait_ge(moved, NF)
                do(v.tensor_copy(junk[:, 0:NF], below[:]))
                v.tensor_copy(below[:], junk[:, 0:NF]).then_inc(counted, 1)
                dve.wait_ge(counted, 1)
                dve.wait_ge(summed, len(psA) + 1)
                for k, p in enumerate(psA):
                    w = min(512, T - 512 * k)
                    do(v.tensor_copy(bi[:, 512 * k:512 * k + w], p[:, 0:w]))
                do(v.tensor_single_scalar(bi[:, 0:T], bi[:, 0:T], 7, ALU.arith_shift_right))
                do(v.tensor_single_scalar(bi[:, 0:T], bi[:, 0:T], 7, ALU.logical_shift_left))
                do(v.tensor_copy(base[:, 0:T], bi[:, 0:T]))
                do(v.tensor_single_scalar(bi[:, 0:T], bi[:, 0:T], 7, ALU.arith_shift_right))
                do(v.tensor_copy(fi[:], psB[:, 0:NF]))
                do(v.tensor_single_scalar(ti[:, T:T + NF], fi[:], 7, ALU.arith_shift_right))
                do(v.tensor_single_scalar(fi[:], fi[:], P - 1, ALU.bitwise_and))
                do(v.tensor_copy(junk[:, 0:NF], fi[:]))
                do(v.tensor_scalar(on[:, T:T + NF], junk[:, 0:NF], 0.0, None, ALU.is_gt))
                do(v.tensor_copy(junk[:, 0:NF], ti[:, T:T + NF]))
                do(v.tensor_scalar(junk[:, 0:NF], junk[:, 0:NF], float(T - 1), None, ALU.min))
                do(v.tensor_copy(ti[:, T:T + NF], junk[:, 0:NF]))
                do(v.memset(ti[:, T + NF:S + U], 0))
                do(v.tensor_copy(base[:, T:T + NF], thr[:]))
                do(v.tensor_copy(bi[:, T:T + NF], io_t[:, 1:NF + 1]))
                do(v.tensor_copy(self.blk[:], bi[0:1, 0:S]))
                do(v.tensor_copy(self.til[:], ti[0:1, :]))
                def turn(k):
                    t = dve.value_load(self.til[0:1, bass.ds(k + T, 1)], min_val=0, max_val=T - 1)
                    for a in (dstf, self.srcf, self.typ):
                        v.tensor_copy(a[:, bass.ds(k + T, 1)], a[:, bass.ds(t, 1)]).then_inc(moved, 1)
                repeat(dve, NF, turn)
                dve.wait_ge(moved, 4 * NF)
                do(v.tensor_copy(self.src[:], self.srcf[:]))
                do(v.tensor_scalar(on[:], on[:], 1.0, -1e6, ALU.subtract, ALU.mult))
                do(v.tensor_tensor(junk[:], dstf[:], base[:], ALU.subtract))
                do(v.tensor_tensor(self.rel[:], junk[:], on[:], ALU.add))
                do(v.tensor_scalar(junk[:], self.rel[:], 0.0, None, ALU.is_ge))
                do(v.tensor_scalar(self.mask[:], self.rel[:], float(P), None, ALU.is_lt))
                do(v.tensor_tensor(self.mask[:], self.mask[:], junk[:], ALU.mult))
                dve.sem_inc(self.setup_done, 1)

    def norm_vector(self, dve, do, sums, rstd, ask, done):
        v, nb = self.nc.vector, self.s.nb
        wide = lambda a: a[:].rearrange("p (b o) -> p b o", o=1).broadcast_to([P, nb, D])
        do(v.tensor_reduce(sums[:], self.x[:], AX.X, ALU.add))
        do(v.tensor_scalar(sums[:], sums[:], 1.0 / D, None, ALU.mult))
        do(v.tensor_tensor(self.hn[:], self.x[:], wide(sums), ALU.subtract))
        do(v.tensor_tensor(self.acc[:, :, 0:D], self.hn[:], self.hn[:], ALU.mult))
        do(v.tensor_reduce(sums[:], self.acc[:, :, 0:D], AX.X, ALU.add))
        v.tensor_scalar(sums[:], sums[:], 1.0 / D, EPS_LN, ALU.mult, ALU.add).then_inc(ask, 1)
        dve.wait_ge(done, 1)
        do(v.reciprocal(rstd[:], rstd[:]))
        do(v.tensor_tensor(self.hn[:], self.hn[:], wide(rstd), ALU.mult))
        do(v.tensor_scalar(self.hn[:], self.hn[:], 0.0, None, ALU.max))

    def norm_scalar(self, act, sums, rstd, ask, done):
        act.wait_ge(ask, 1)
        self.nc.scalar.activation(rstd[:], sums[:], ACT.Sqrt).then_inc(done, 1)

    def product_sems(self, name):
        return {k: self.sem(f"{name}_{k}") for k in
                ("loaded", "staged", "turned_ps", "turned", "product", "finished", "seq", "stored0", "stored1")}

    def product_memory(self, name, c, k, width, at=None):
        take = at.take if at else lambda shape: self.sb(name, shape, F32, c)
        return (take([P, k, width]), take([P, 2, k, D]), take([P, 2, k, D]),
                [self.ps(f"{name}_pt{j}", c) for j in range(2)], [self.ps(f"{name}_po{j}", c) for j in range(2)])

    def product_scalar(self, act, i, q, arrays, stage, turned, psT):
        go, K = self.setup_done, len(arrays)
        for j in range(2):
            hold(act, q["turned_ps"], (2 * i + j - 1) * K, go)
            for k in range(K):
                self.nc.scalar.activation(stage[:, j, k, :], arrays[k][:, bass.ds(2 * i + j, 1), 0:D],
                                          ACT.Copy).then_inc(q["staged"], 1)
        for j in range(2):
            hold(act, q["product"], 2 * i + j - 1, go)
            hold(act, q["turned_ps"], (2 * i + j) * K + K, go)
            for k in range(K):
                self.nc.scalar.activation(turned[:, j, k, :], psT[j][:, k * D:k * D + D],
                                          ACT.Copy).then_inc(q["turned"], 1)

    def product_tensor(self, pe, q, w, width, stage, turned, psT, psO, loads, blocks_used):
        nc, go, K = self.nc, self.setup_done, w.shape[1]
        pe.wait_ge(q["loaded"], 16 * loads)
        def turn(i):
            for j in range(2):
                hold(pe, q["turned"], (2 * i + j - 1) * K, go)
                for k in range(K):
                    hold(pe, q["staged"], (2 * i + j) * K + k + 1, go)
                    nc.tensor.transpose(psT[j][:, k * D:k * D + D], stage[:, j, k, :],
                                        self.ident[:]).then_inc(q["turned_ps"], 1)
            for j in range(2):
                hold(pe, q["turned"], (2 * i + j) * K + K, go)
                hold(pe, q["finished"], 2 * i + j - 1, go)
                for k in range(K):
                    m = nc.tensor.matmul(psO[j][:, 0:width], turned[:, j, k, :], w[:, k, :],
                                         start=(k == 0), stop=(k == K - 1))
                m.then_inc(q["product"], 1)
        repeat(pe, self.s.nb // 2, turn)

    def gat_nodes(self):
        nc, s, io, go = self.nc, self.s, self.io, self.setup_done
        H = s.heads0
        F = D // H
        q = self.product_sems("gat")
        load_x, ask, root = self.sem("load_x"), self.sem("ask"), self.sem("root")
        normed, seq = self.sem("normed"), self.sem("seq")
        with ExitStack() as c:
            w, stage, turned, psT, psO = self.product_memory("gat", c, 1, D)
            a_src = self.sb("a_src", [P, D], F32, c)
            a_trg = self.sb("a_trg", [P, D], F32, c)
            rows = self.sb("gat_rows", [P, 2, 136], F32, c)
            scaled = self.sb("scaled", [P, 2, D], F32, c)
            sums, rstd = self.sb("sums", [P, s.nb], F32, c), self.sb("rstd", [P, s.nb], F32, c)
            block = c.enter_context(nc.Block())

            @block.sync
            def _(sp):
                sp.dma_start(self.x[:], io["x"].rearrange("(b p) d -> p b d", p=P)).then_inc(load_x, 16)
                sp.dma_start(w[:, 0, :], io["W_proj"]).then_inc(q["loaded"], 16)
                sp.dma_start(a_src[:], self.bcast_row(io["a_src"], D)).then_inc(q["loaded"], 16)
                sp.dma_start(a_trg[:], self.bcast_row(io["a_trg"], D)).then_inc(q["loaded"], 16)
                table = self.t_gat.rearrange("(b p) d -> b p d", p=P)
                def turn(i):
                    for j in range(2):
                        hold(sp, q["finished"], 2 * i + j + 1, go)
                        sp.dma_start(table[bass.ds(2 * i + j, 1), :, :].rearrange("o p d -> p (o d)"),
                                     rows[:, j, :]).then_inc(q[f"stored{j}"], 16)
                repeat(sp, s.nb // 2, turn)
                for j in range(2):
                    sp.wait_ge(q[f"stored{j}"], 16 * (s.nb // 2))

            @block.scalar
            def _(act):
                self.norm_scalar(act, sums, rstd, ask, root)
                act.wait_ge(normed, 1)
                def turn(i):
                    self.product_scalar(act, i, q, [self.hn], stage, turned, psT)
                repeat(act, s.nb // 2, turn)

            @block.tensor
            def _(pe):
                self.product_tensor(pe, q, w, D, stage, turned, psT, psO, 3, None)

            @block.vector
            def _(dve):
                v = nc.vector
                do = Chain(dve, seq)
                dve.wait_ge(load_x, 16)
                self.norm_vector(dve, do, sums, rstd, ask, root)
                dve.sem_inc(normed, 1)
                dve.wait_ge(q["loaded"], 48)
                def turn(i):
                    for j in range(2):
                        hold(dve, q["product"], 2 * i + j + 1, go)
                        hold(dve, q[f"stored{j}"], i * 16, go)
                        then = Turn(dve, q["seq"], (2 * i + j) * 5, go)
                        then(v.tensor_copy(rows[:, j, 0:D], psO[j][:, 0:D]))
                        then(v.tensor_copy(self.aux[:, bass.ds(2 * i + j, 1), :], psO[j][:, 0:D]))
                        then(v.tensor_tensor(scaled[:, 0, :], rows[:, j, 0:D], a_src[:], ALU.mult))
                        then(v.tensor_tensor(scaled[:, 1, :], rows[:, j, 0:D], a_trg[:], ALU.mult))
                        then(v.tensor_reduce(self.strg[:, bass.ds(2 * i + j, 1), :],
                                             scaled[:, 1, :].rearrange("p (h f) -> p h f", f=F), AX.X, ALU.add))
                        v.tensor_reduce(rows[:, j, D:D + H], scaled[:, 0, :].rearrange("p (h f) -> p h f", f=F),
                                        AX.X, ALU.add).then_inc(q["finished"], 1)
                repeat(dve, s.nb // 2, turn)

    def plain_product(self, name, arrays, weights, bias, width, out=None, table=None, cols=0, gate=None, bias2=None):
        nc, s, go = self.nc, self.s, self.setup_done
        K = len(arrays)
        q = self.product_sems(name)
        with ExitStack() as c:
            w, stage, turned, psT, psO = self.product_memory(name, c, K, width)
            b = self.sb(f"{name}_bias", [P, width], F32, c)
            gb = self.sb(f"{name}_gated", [P, 2, width], F32, c) if gate is not None else None
            rows = self.sb(f"{name}_rows", [P, 2, width], F32, c) if table is not None else None
            block = c.enter_context(nc.Block())
            b2 = self.sb(f"{name}_bias2", [P, width], F32, c) if bias2 is not None else None
            loads = K + len(bias) + (bias2 is not None)

            @block.sync
            def _(sp):
                for k in range(K):
                    sp.dma_start(w[:, k, :], weights[k]).then_inc(q["loaded"], 16)
                at = 0
                for part in bias:
                    n = part.shape[0]
                    sp.dma_start(b[:, at:at + n], self.bcast_row(part, n)).then_inc(q["loaded"], 16)
                    at += n
                if bias2 is not None:
                    sp.dma_start(b2[:], self.bcast_row(bias2, width)).then_inc(q["loaded"], 16)
                if table is not None:
                    tab = table.rearrange("(b p) d -> b p d", p=P)
                    def turn(i):
                        for j in range(2):
                            hold(sp, q["finished"], 2 * i + j + 1, go)
                            sp.dma_start(tab[bass.ds(2 * i + j, 1), :, cols:cols + width]
                                         .rearrange("o p d -> p (o d)"), rows[:, j, :]).then_inc(q[f"stored{j}"], 16)
                    repeat(sp, s.nb // 2, turn)
                    for j in range(2):
                        sp.wait_ge(q[f"stored{j}"], 16 * (s.nb // 2))

            @block.scalar
            def _(act):
                def turn(i):
                    self.product_scalar(act, i, q, arrays, stage, turned, psT)
                repeat(act, s.nb // 2, turn)

            @block.tensor
            def _(pe):
                self.product_tensor(pe, q, w, width, stage, turned, psT, psO, loads, None)

            @block.vector
            def _(dve):
                v = nc.vector
                dve.wait_ge(q["loaded"], 16 * loads)
                do = Chain(dve, q["seq"])
                if not bias:
                    do(v.memset(b[:], 0.0))
                if bias2 is not None:
                    do(v.tensor_tensor(b[:], b[:], b2[:], ALU.add))
                first = do.n
                def turn(i):
                    for j in range(2):
                        hold(dve, q["product"], 2 * i + j + 1, go)
                        plus = b[:]
                        if gate is not None:
                            then = Turn(dve, q["seq"], 2 * i + j + first, go)
                            then(v.tensor_scalar(gb[:, j, :], b[:], gate[:, bass.ds(2 * i + j, 1)], None, ALU.mult))
                            plus = gb[:, j, :]
                        if table is not None:
                            hold(dve, q[f"stored{j}"], i * 16, go)
                            dst = rows[:, j, :]
                        else:
                            dst = out[:, bass.ds(2 * i + j, 1), 0:width].rearrange("p o d -> p (o d)")
                        v.tensor_tensor(dst, psO[j][:, 0:width], plus, ALU.add).then_inc(q["finished"], 1)
                repeat(dve, s.nb // 2, turn)

    def refill(self, dve, i, r, idx, source, idx_ready):
        self.nc.vector.tensor_copy(idx[:, r:r + 1], source[:, bass.ds(i * U + r + U, 1)]).then_inc(idx_ready, 1)

    def zero(self, arrays):
        with self.nc.Block() as block:
            @block.vector
            def _(dve):
                for a in arrays:
                    self.nc.vector.memset(a, 0.0)

    def expand_tensor(self, pe, i, r, q, sel, psT):
        go = self.setup_done
        hold(pe, q["sel"], i * U + r + 1, go)
        hold(pe, q["selT"], i * U + r - 1, go)
        self.nc.tensor.transpose(psT[r % 2][:, 0:P], sel[:, r % RS, :], self.ident[:]).then_inc(q["turned"], 1)

    def expand_scalar(self, act, q, psT, selT, pace):
        go = self.setup_done
        def turn(i):
            for r in range(U):
                hold(act, q["turned"], i * U + r + 1, go)
                hold(act, pace, i * U + r - 1, go)
                self.nc.scalar.activation(selT[:, r % 2, :], psT[r % 2][:, 0:P], ACT.Copy).then_inc(q["selT"], 1)
        repeat(act, self.s.steps // U, turn)

    def select(self, dve, i, r, q, sel, used, weight=None):
        hold(dve, used, i * U + r + 1 - RS, self.setup_done)
        col = bass.ds(i * U + r, 1)
        if weight is None:
            m = self.nc.vector.tensor_scalar(sel[:, r % RS, :], self.iota[:], self.rel[:, col], None, ALU.is_equal)
        else:
            m = self.nc.vector.tensor_scalar(sel[:, r % RS, :], self.iota[:], self.rel[:, col], weight[:, col],
                                             ALU.is_equal, ALU.mult)
        m.then_inc(q["sel"], 1)

    def order(self, front, back, lag=1):
        for r in range(U + lag):
            if r < U:
                front(r)
            if r >= lag:
                back(r - lag)

    def gat_gather(self):
        nc, s, go = self.nc, self.s, self.setup_done
        H, turns = s.heads0, s.steps // U
        q = {k: self.sem(f"gg_{k}") for k in ("idx", "sel", "turned", "selT", "target", "logit")}
        gathered = [self.sem(f"gg_gathered{r}") for r in range(U)]
        stored = [self.sem(f"gg_stored{r}") for r in range(U)]
        with ExitStack() as c:
            rows = self.sb("gg_rows", [P, U, 136], F32, c)
            idx = self.sb("gg_idx", [P, U], I32, c)
            sel = self.sb("gg_sel", [P, RS, P], F32, c)
            selT = self.sb("gg_selT", [P, 2, P], F32, c)
            psT = [self.ps(f"gg_pt{j}", c) for j in range(2)]
            psE = [self.ps(f"gg_pe{j}", c) for j in range(2)]
            block = c.enter_context(nc.Block())

            @block.gpsimd
            def _(pool):
                issued = self.issued
                def turn(i):
                    for r in range(U):
                        hold(pool, q["idx"], i * U + r + 1)
                        hold(pool, q["logit"], i * U + r + 1 - U)
                        hold(pool, stored[r], i * 16)
                        clear_ahead(pool, issued)
                        nc.gpsimd.indirect_dma_start(rows[:, r, :], None, self.t_gat,
                                                     bass.IndirectOffsetOnAxis(idx[:, r:r + 1], 0))\
                            .then_inc(gathered[r], 16)
                repeat(pool, turns, turn)

            @block.sync
            def _(sp):
                def turn(i):
                    for r in range(U):
                        hold(sp, gathered[r], i * 16 + 16, go)
                        sp.dma_start(self.t_rows[bass.ds(i * U + r, 1), :, :].rearrange("o p d -> p (o d)"),
                                     rows[:, r, 0:D]).then_inc(stored[r], 16)
                repeat(sp, turns, turn)
                for r in range(U):
                    sp.wait_ge(stored[r], 16 * turns)

            @block.scalar
            def _(act):
                self.expand_scalar(act, q, psT, selT, q["target"])

            @block.tensor
            def _(pe):
                def turn(i):
                    b = self.regs(PE, self.blk, i, s.nb - 1)

                    def target(r):
                        hold(pe, q["selT"], i * U + r + 1, go)
                        hold(pe, q["logit"], i * U + r - 1, go)
                        nc.tensor.matmul(psE[r % 2][:, 0:H], selT[:, r % 2, :], self.strg[:, bass.ds(b[r], 1), :],
                                         start=True, stop=True).then_inc(q["target"], 1)
                    self.order(lambda r: self.expand_tensor(pe, i, r, q, sel, psT), target)
                repeat(pe, turns, turn)

            @block.vector
            def _(dve):
                v = nc.vector
                v.tensor_copy(idx[:], self.src[:, 0:U]).then_inc(q["idx"], U)
                def turn(i):
                    def logit(r):
                        hold(dve, gathered[r], i * 16 + 16, go)
                        self.refill(dve, i, r, idx, self.src, q["idx"])
                        hold(dve, q["target"], i * U + r + 1, go)
                        v.tensor_tensor(self.w8[:, bass.ds(i * U + r, 1), 0:H].rearrange("p o h -> p (o h)"),
                                        rows[:, r, D:D + H], psE[r % 2][:, 0:H], ALU.add).then_inc(q["logit"], 1)
                    self.order(lambda r: self.select(dve, i, r, q, sel, q["turned"]), logit)
                repeat(dve, turns, turn)

    def gat_softmax(self):
        nc, s = self.nc, self.s
        S, H = s.steps, s.heads0
        seq, ready, turned, top = (self.sem(f"gs_{k}") for k in ("seq", "ready", "turned", "top"))
        with ExitStack() as c:
            off = self.sb("off", [P, S], F32, c)
            part = self.sb("part_max", [P, 1], F32, c)
            tops = self.sb("tops", [1, P], F32, c)
            one = self.sb("one_max", [1, 1], F32, c)
            low = self.sb("minus_max", [P, 1], F32, c)
            ps = self.ps("gs_ps", c)
            block = c.enter_context(nc.Block())
            w = self.w8[:, :, 0:H]

            @block.tensor
            def _(pe):
                pe.wait_ge(ready, 1)
                nc.tensor.transpose(ps[0:1, 0:P], part[:], self.ident[:]).then_inc(turned, 1)
                pe.wait_ge(ready, 2)
                nc.tensor.matmul(ps[:, P:P + 1], self.ones[0:1, :], one[:], start=True, stop=True).then_inc(turned, 1)

            @block.scalar
            def _(act):
                act.wait_ge(top, 1)
                nc.scalar.activation(w, w, ACT.Exp, bias=low[:, 0:1])

            @block.vector
            def _(dve):
                v = nc.vector
                do = Chain(dve, seq)
                wide = lambda a: a[:, 0:S].rearrange("p (s o) -> p s o", o=1).broadcast_to([P, S, H])
                do(v.scalar_tensor_tensor(w, w, 0.2, w, ALU.mult, ALU.max))
                do(v.tensor_scalar(off[:], self.mask[:, 0:S], 1.0, BIG, ALU.subtract, ALU.mult))
                do(v.tensor_tensor(w, w, wide(self.mask), ALU.mult))
                do(v.tensor_tensor(w, w, wide(off), ALU.add))
                v.tensor_reduce(part[:], w, AX.XY, ALU.max).then_inc(ready, 1)
                dve.wait_ge(turned, 1)
                do(v.tensor_copy(tops[:], ps[0:1, 0:P]))
                v.tensor_reduce(one[:], tops[:], AX.X, ALU.max).then_inc(ready, 1)
                dve.wait_ge(turned, 2)
                v.tensor_scalar(low[:], ps[:, P:P + 1], -1.0, None, ALU.mult).then_inc(top, 1)

    def weighted_sum(self, name, H):
        nc, s, go = self.nc, self.s, self.setup_done
        turns = s.steps // U
        q = {k: self.sem(f"{name}_{k}") for k in ("sel", "scaled", "summed", "added", "cleared")}
        loaded = [self.sem(f"{name}_loaded{r}") for r in range(U)]
        with ExitStack() as c:
            rows = self.sb(f"{name}_rows", [P, U, D], F32, c)
            vals = self.sb(f"{name}_vals", [P, RS, D], F32, c)
            sel = self.sb(f"{name}_sel", [P, RS, P], F32, c)
            psO = [self.ps(f"{name}_po{j}", c) for j in range(2)]
            block = c.enter_context(nc.Block())

            @block.sync
            def _(sp):
                def turn(i):
                    for r in range(U):
                        hold(sp, q["scaled"], i * U + r + 1 - U, go)
                        sp.dma_start(rows[:, r, :], self.t_rows[bass.ds(i * U + r, 1), :, :]
                                     .rearrange("o p d -> p (o d)")).then_inc(loaded[r], 16)
                repeat(sp, turns, turn)

            @block.tensor
            def _(pe):
                def turn(i):
                    for r in range(U):
                        hold(pe, q["sel"], i * U + r + 1, go)
                        hold(pe, q["scaled"], i * U + r + 1, go)
                        hold(pe, q["added"], i * U + r - 1, go)
                        nc.tensor.matmul(psO[r % 2][:, 0:D], sel[:, r % RS, :], vals[:, r % RS, :],
                                         start=True, stop=True)
                        nc.tensor.matmul(psO[r % 2][:, D:D + H], sel[:, r % RS, :],
                                         self.w8[:, bass.ds(i * U + r, 1), 0:H], start=True, stop=True)\
                            .then_inc(q["summed"], 1)
                repeat(pe, turns, turn)

            @block.vector
            def _(dve):
                v = nc.vector
                v.memset(self.acc[:], 0.0).then_inc(q["cleared"], 1)
                dve.wait_ge(q["cleared"], 1)
                def turn(i):
                    b = self.regs(DVE, self.blk, i, s.nb - 1)

                    def scale(r):
                        self.select(dve, i, r, q, sel, q["summed"])
                        hold(dve, loaded[r], i * 16 + 16, go)
                        w = self.w8[:, bass.ds(i * U + r, 1), 0:H].rearrange("p o h -> p (o h)")\
                            .rearrange("p (h o) -> p h o", o=1).broadcast_to([P, H, D // H])
                        v.tensor_tensor(vals[:, r % RS, :].rearrange("p (h f) -> p h f", h=H),
                                        rows[:, r, :].rearrange("p (h f) -> p h f", h=H), w, ALU.mult)\
                            .then_inc(q["scaled"], 1)
                    self.order(scale, lambda r: self.add_sum(dve, i, r, b[r], q, psO, D + H))
                repeat(dve, turns, turn)

    def add_sum(self, dve, i, r, b, q, psO, width):
        hold(dve, q["summed"], i * U + r + 1, self.setup_done)
        hold(dve, q["added"], i * U + r, self.setup_done)
        a = self.acc[:, bass.ds(b, 1), 0:width].rearrange("p o d -> p (o d)")
        self.nc.vector.tensor_tensor(a, a, psO[r % 2][:, 0:width], ALU.add).then_inc(q["added"], 1)

    def gat_output(self):
        nc, s, io = self.nc, self.s, self.io
        nb, H = s.nb, s.heads0
        seq, loaded, lowered, raised, ask, root = (
            self.sem(f"go_{k}") for k in ("seq", "loaded", "lowered", "raised", "ask", "root"))
        with ExitStack() as c:
            bias = self.sb("gat_bias", [P, D], F32, c)
            den = self.sb("gat_den", [P, nb, H], F32, c)
            sums, rstd = self.sb("sums", [P, nb], F32, c), self.sb("rstd", [P, nb], F32, c)
            block = c.enter_context(nc.Block())
            neg = self.aux2[:, :, 0:D]

            @block.sync
            def _(sp):
                sp.dma_start(bias[:], self.bcast_row(io["gat_bias"], D)).then_inc(loaded, 16)

            @block.scalar
            def _(act):
                act.wait_ge(lowered, 1)
                nc.scalar.activation(neg, neg, ACT.Exp).then_inc(raised, 1)
                self.norm_scalar(act, sums, rstd, ask, root)

            @block.vector
            def _(dve):
                v = nc.vector
                do = Chain(dve, seq)
                do(v.tensor_scalar(den[:], self.acc[:, :, D:D + H], 1e-16, None, ALU.add))
                do(v.reciprocal(den[:], den[:]))
                for h in range(H):
                    a = self.acc[:, :, h * (D // H):(h + 1) * (D // H)]
                    do(v.tensor_tensor(a, a, den[:, :, h:h + 1].broadcast_to([P, nb, D // H]), ALU.mult))
                out = self.acc[:, :, 0:D]
                do(v.tensor_tensor(out, out, self.aux[:], ALU.add))
                dve.wait_ge(loaded, 16)
                do(v.tensor_tensor(out, out, bias[:].rearrange("p (o d) -> p o d", o=1)
                                   .broadcast_to([P, nb, D]), ALU.add))
                v.tensor_scalar(neg, out, 0.0, None, ALU.min).then_inc(lowered, 1)
                do(v.tensor_scalar(out, out, 0.0, -1.0, ALU.max, ALU.add))
                dve.wait_ge(raised, 1)
                do(v.tensor_tensor(out, out, neg, ALU.add))
                do(v.tensor_tensor(self.x[:], self.x[:], out, ALU.add))
                self.norm_vector(dve, do, sums, rstd, ask, root)

    def keep_h(self):
        sent = self.sem("kh_sent")
        with self.nc.Block() as block:
            @block.sync
            def _(sp):
                sp.dma_start(self.t_h.rearrange("(b p) d -> p b d", p=P), self.hn[:]).then_inc(sent, 16)
                sp.wait_ge(sent, 16)

    def gather_sum(self, name, table, source, types=False, weight=None):
        nc, s, go = self.nc, self.s, self.setup_done
        R, turns = s.rels, s.steps // U
        q = {k: self.sem(f"{name}_{k}") for k in
             ("idx", "sel", "summed", "added", "cleared", "onehot", "diag", "spread", "same", "ahead")}
        gathered = [self.sem(f"{name}_gathered{r}") for r in range(U)]
        width = D + R if types else D
        with ExitStack() as c:
            at = Arena(self.aux)
            rows = at.take([P, U, D], F32)
            idx = at.take([P, U], I32)
            sel = at.take([P, RS, P], F32)
            hot = at.take([P, RS, 8], F32)
            diag = at.take([P, 2, P], F32)
            same = at.take([P, 2, P], F32)
            lower = at.take([P, P], F32)
            psO = [self.ps(f"{name}_po{j}", c) for j in range(2)]
            psB = [self.ps(f"{name}_pb{j}", c) for j in range(2)]
            block = c.enter_context(nc.Block())

            @block.gpsimd
            def _(pool):
                issued = self.issued
                def turn(i):
                    for r in range(U):
                        hold(pool, q["idx"], i * U + r + 1)
                        hold(pool, q["summed"], i * U + r + 1 - U)
                        clear_ahead(pool, issued)
                        nc.gpsimd.indirect_dma_start(rows[:, r, :], None, table,
                                                     bass.IndirectOffsetOnAxis(idx[:, r:r + 1], 0))\
                            .then_inc(gathered[r], 16)
                repeat(pool, turns, turn)

            @block.tensor
            def _(pe):
                def turn(i):
                    def spread(r):
                        if types:
                            hold(pe, q["diag"], i * U + r + 1, go)
                            hold(pe, q["same"], i * U + r - 1, go)
                            nc.tensor.matmul(psB[r % 2][:, 0:P], self.ones[:], diag[:, r % 2, :],
                                             start=True, stop=True).then_inc(q["spread"], 1)

                    def total(r):
                        hold(pe, q["sel"], i * U + r + 1, go)
                        hold(pe, gathered[r], i * 16 + 16, go)
                        hold(pe, q["added"], i * U + r - 1, go)
                        m = nc.tensor.matmul(psO[r % 2][:, 0:D], sel[:, r % RS, :], rows[:, r, :],
                                             start=True, stop=True)
                        if types:
                            hold(pe, q["onehot"], i * U + r + 1, go)
                            m = nc.tensor.matmul(psO[r % 2][:, D:D + R], sel[:, r % RS, :], hot[:, r % RS, 0:R],
                                                 start=True, stop=True)
                        m.then_inc(q["summed"], 1)
                    self.order(spread, total)
                repeat(pe, turns, turn)

            @block.vector
            def _(dve):
                v = nc.vector
                v.tensor_copy(idx[:], source[:, 0:U]).then_inc(q["idx"], U)
                v.memset(self.acc[:], 0.0).then_inc(q["cleared"], 1)
                if types:
                    v.tensor_scalar(lower[:], self.iota[:], self.pidx[:, 0:1], None, ALU.is_lt)\
                        .then_inc(q["cleared"], 1)
                    dve.wait_ge(q["cleared"], 2)
                dve.wait_ge(q["cleared"], 1)
                def turn(i):
                    b = self.regs(DVE, self.blk, i, s.nb - 1)

                    def front(r):
                        self.select(dve, i, r, q, sel, q["summed"], weight)
                        if types:
                            col = bass.ds(i * U + r, 1)
                            v.tensor_scalar(hot[:, r % RS, :], self.iota[:, 0:8], self.typ[:, col], None,
                                            ALU.is_equal).then_inc(q["onehot"], 1)
                            hold(dve, q["spread"], i * U + r - 1, go)
                            v.tensor_scalar(diag[:, r % 2, :], self.ident[:], self.srcf[:, col], None,
                                            ALU.mult).then_inc(q["diag"], 1)

                    def back(r):
                        if types:
                            col = bass.ds(i * U + r, 1)
                            hold(dve, q["spread"], i * U + r + 1, go)
                            hold(dve, q["ahead"], i * U + r - 1, go)
                            v.tensor_scalar(same[:, r % 2, :], psB[r % 2][:, 0:P], self.srcf[:, col], None,
                                            ALU.is_equal).then_inc(q["same"], 1)
                            hold(dve, q["same"], i * U + r + 1, go)
                            v.scalar_tensor_tensor(same[:, r % 2, :], same[:, r % 2, :], 1.0, lower[:], ALU.mult,
                                                   ALU.mult, accum_out=self.ahead[:, col]).then_inc(q["ahead"], 1)
                        self.add_sum(dve, i, r, b[r], q, psO, width)
                        hold(dve, gathered[r], i * 16 + 16, go)
                        self.refill(dve, i, r, idx, source, q["idx"])
                    self.order(front, back)
                repeat(dve, turns, turn)

    def mean_in(self):
        nc, s = self.nc, self.s
        nb, R, S = s.nb, s.rels, s.steps + U
        seq, zeroed, cleared = self.sem("mi_seq"), self.sem("mi_zeroed"), self.sem("mi_cleared")
        with ExitStack() as c:
            at = Arena(self.aux)
            cnt = at.take([P, nb], F32)
            inv = at.take([P, nb], F32)
            dump = at.take([P, 1], F32)
            t = at.take([P, S], F32)
            f = at.take([P, S], F32)
            block = c.enter_context(nc.Block())

            @block.sync
            def _(sp):
                sp.wait_ge(zeroed, 1)
                for k in range(TABLES):
                    sp.dma_start(self.t_out[k][0:nb * P, :].rearrange("(b p) d -> p b d", p=P), self.aux2[:])\
                        .then_inc(cleared, 16)
                    sp.dma_start(self.t_out[k][nb * P:nb * P + P, :], self.aux2[:, 0, :]).then_inc(cleared, 16)
                sp.wait_ge(cleared, 32 * TABLES)

            @block.vector
            def _(dve):
                v = nc.vector
                do = Chain(dve, seq)
                v.memset(self.aux2[:], 0.0).then_inc(zeroed, 1)
                do(v.tensor_scalar(self.inv[:, :, 0:R], self.acc[:, :, D:D + R], 1.0, None, ALU.max))
                do(v.reciprocal(self.inv[:, :, 0:R], self.inv[:, :, 0:R]))
                do(v.memset(self.inv[:, :, R:8], 1.0))
                do(v.tensor_reduce(cnt[:], self.acc[:, :, D:D + R], AX.X, ALU.add))
                do(v.tensor_scalar(self.gin[:], cnt[:], 1.0, None, ALU.min))
                do(v.tensor_scalar(cnt[:], cnt[:], 1.0, None, ALU.max))
                do(v.reciprocal(inv[:], cnt[:]))
                a = self.acc[:, :, 0:D]
                do(v.tensor_tensor(a, a, inv[:].rearrange("p (b o) -> p b o", o=1).broadcast_to([P, nb, D]), ALU.mult))
                do(v.tensor_scalar(dump[:], self.pidx[:], float(nb * P), None, ALU.add))
                do(v.tensor_scalar(f[:, 0:s.steps], self.ahead[:, 0:s.steps], 0.0, None, ALU.is_equal))
                do(v.tensor_scalar(t[:, 0:s.steps], self.srcf[:, 0:s.steps], dump[:, 0:1], None, ALU.subtract))
                do(v.tensor_tensor(t[:, 0:s.steps], t[:, 0:s.steps], f[:, 0:s.steps], ALU.mult))
                do(v.tensor_scalar(t[:, 0:s.steps], t[:, 0:s.steps], dump[:, 0:1], None, ALU.add))
                do(v.tensor_copy(self.sidx[:, 0:s.steps], t[:, 0:s.steps]))
                do(v.tensor_scalar(t[:], self.srcf[:], float(R), None, ALU.mult))
                do(v.tensor_tensor(t[:], t[:], self.typ[:], ALU.add))
                do(v.tensor_copy(self.gidx[:], t[:]))

    def scatter_out(self):
        nc, s, go = self.nc, self.s, self.setup_done
        turns = s.steps // U
        q = {k: self.sem(f"so_{k}") for k in ("idx", "sel", "turned", "selT", "diag", "spread", "same",
                                              "taken", "vals", "invs", "joined", "sums")}
        scattered = [self.sem(f"so_scattered{r}") for r in range(U)]
        with ExitStack() as c:
            at = Arena(self.aux)
            idx = at.take([P, U], I32)
            sel = at.take([P, RS, P], F32)
            selT = at.take([P, 2, P], F32)
            diag = at.take([P, 2, P], F32)
            same = at.take([P, 2, P], F32)
            vals = at.take([P, 2, 136], F32)
            sums = at.take([P, U, 136], F32)
            psT = [self.ps(f"so_pt{j}", c) for j in range(2)]
            psB = [self.ps(f"so_pb{j}", c) for j in range(2)]
            psE = [self.ps(f"so_pe{j}", c) for j in range(2)]
            psC = [self.ps(f"so_pc{j}", c) for j in range(2)]
            block = c.enter_context(nc.Block())

            @block.gpsimd
            def _(pool):
                issued = self.issued
                def turn(i):
                    for r in range(U):
                        hold(pool, q["idx"], i * U + r + 1)
                        hold(pool, q["sums"], i * U + r + 1)
                        hold(pool, scattered[r], i * 16)
                        clear_ahead(pool, issued)
                        nc.gpsimd.indirect_dma_start(self.t_out[r], bass.IndirectOffsetOnAxis(idx[:, r:r + 1], 0),
                                                     sums[:, r, :], None, compute_op=ALU.add)\
                            .then_inc(scattered[r], 16)
                repeat(pool, turns, turn)
                for r in range(U):
                    pool.wait_ge(scattered[r], 16 * turns)

            @block.scalar
            def _(act):
                a = nc.scalar
                def turn(i):
                    def turned(r):
                        hold(act, q["turned"], i * U + r + 1, go)
                        hold(act, q["taken"], i * U + r - 1, go)
                        a.activation(selT[:, r % 2, :], psT[r % 2][:, 0:P], ACT.Copy).then_inc(q["selT"], 1)

                    def taken(r):
                        hold(act, q["taken"], i * U + r + 1, go)
                        hold(act, q["joined"], i * U + r - 1, go)
                        hold(act, q["invs"], i * U + r - 1, go)
                        a.activation(vals[:, r % 2, :], psE[r % 2][:, 0:136], ACT.Copy).then_inc(q["vals"], 1)

                    def joined(r):
                        hold(act, q["joined"], i * U + r + 1, go)
                        hold(act, scattered[r], i * 16, go)
                        a.activation(sums[:, r, :], psC[r % 2][:, 0:136], ACT.Copy).then_inc(q["sums"], 1)
                    for r in range(U + 2):
                        if r < U:
                            turned(r)
                        if 1 <= r < U + 1:
                            taken(r - 1)
                        if r >= 2:
                            joined(r - 2)
                repeat(act, turns, turn)

            @block.tensor
            def _(pe):
                def turn(i):
                    b = self.regs(PE, self.blk, i, s.nb - 1)

                    def first(r):
                        self.expand_tensor(pe, i, r, q, sel, psT)
                        hold(pe, q["diag"], i * U + r + 1, go)
                        hold(pe, q["same"], i * U + r - 1, go)
                        nc.tensor.matmul(psB[r % 2][:, 0:P], self.ones[:], diag[:, r % 2, :],
                                         start=True, stop=True).then_inc(q["spread"], 1)

                    def take(r):
                        hold(pe, q["selT"], i * U + r + 1, go)
                        hold(pe, q["vals"], i * U + r - 1, go)
                        nc.tensor.matmul(psE[r % 2][:, 0:D], selT[:, r % 2, :],
                                         self.hn[:, bass.ds(b[r], 1), :], start=True, stop=True)
                        nc.tensor.matmul(psE[r % 2][:, D:D + 8], selT[:, r % 2, :],
                                         self.inv[:, bass.ds(b[r], 1), :], start=True, stop=True)\
                            .then_inc(q["taken"], 1)

                    def join(r):
                        hold(pe, q["vals"], i * U + r + 1, go)
                        hold(pe, q["same"], i * U + r + 1, go)
                        hold(pe, q["sums"], i * U + r - 1, go)
                        nc.tensor.matmul(psC[r % 2][:, 0:136], same[:, r % 2, :], vals[:, r % 2, :],
                                         start=True, stop=True).then_inc(q["joined"], 1)
                    for r in range(U + 2):
                        if r < U:
                            first(r)
                        if 1 <= r < U + 1:
                            take(r - 1)
                        if r >= 2:
                            join(r - 2)
                repeat(pe, turns, turn)

            @block.vector
            def _(dve):
                v = nc.vector
                def turn(i):
                    def front(r):
                        col = bass.ds(i * U + r, 1)
                        hold(dve, scattered[r], i * 16, go)
                        v.tensor_copy(idx[:, r:r + 1], self.sidx[:, col]).then_inc(q["idx"], 1)
                        self.select(dve, i, r, q, sel, q["turned"])
                        hold(dve, q["spread"], i * U + r - 1, go)
                        v.tensor_scalar(diag[:, r % 2, :], self.ident[:], self.srcf[:, col], None,
                                        ALU.mult).then_inc(q["diag"], 1)

                    def back(r):
                        hold(dve, q["spread"], i * U + r + 1, go)
                        hold(dve, q["joined"], i * U + r - 1, go)
                        v.tensor_scalar(same[:, r % 2, :], psB[r % 2][:, 0:P], self.srcf[:, bass.ds(i * U + r, 1)],
                                        None, ALU.is_equal).then_inc(q["same"], 1)
                        hold(dve, q["vals"], i * U + r + 1, go)
                        v.tensor_copy(self.w8[:, bass.ds(i * U + r, 1), :].rearrange("p o h -> p (o h)"),
                                      vals[:, r % 2, D:D + 8]).then_inc(q["invs"], 1)
                    self.order(front, back)
                repeat(dve, turns, turn)

    def mean_out(self):
        nc, s = self.nc, self.s
        nb, R, S = s.nb, s.rels, s.steps
        half = nb // 2
        seq, weighed = self.sem("mo_seq"), self.sem("mo_weighed")
        loaded = [self.sem(f"mo_loaded{j}") for j in range(2)]
        added = [self.sem(f"mo_added{j}") for j in range(2)]
        buf = self.wts[:, 0:nb * 136].rearrange("p (b d) -> p b d", d=136)
        with ExitStack() as c:
            at = Arena(self.aux)
            hot = at.take([P, S], F32)
            cnt = at.take([P, nb], F32)
            block = c.enter_context(nc.Block())

            @block.sync
            def _(sp):
                sp.wait_ge(weighed, 1)
                for k in range(TABLES):
                    for j in range(2):
                        if k:
                            sp.wait_ge(added[j], k)
                        sp.dma_start(buf[:, j * half:(j + 1) * half, :],
                                     self.t_out[k][j * half * P:(j + 1) * half * P, :]
                                     .rearrange("(b p) d -> p b d", p=P)).then_inc(loaded[j], 16)

            @block.vector
            def _(dve):
                v = nc.vector
                do = Chain(dve, seq)
                do(v.memset(self.w2[:], 0.0))
                for r in range(R):
                    do(v.tensor_scalar(hot[:], self.typ[:, 0:S], float(r), None, ALU.is_equal))
                    do(v.tensor_tensor(hot[:], hot[:], self.w8[:, :, r:r + 1].rearrange("p s o -> p (s o)"), ALU.mult))
                    do(v.tensor_tensor(self.w2[:, 0:S], self.w2[:, 0:S], hot[:], ALU.add))
                dve.sem_inc(weighed, 1)
                for k in range(TABLES):
                    for j in range(2):
                        a = self.aux2[:, j * half:(j + 1) * half, :]
                        dve.wait_ge(loaded[j], 16 * (k + 1))
                        if k:
                            dve.wait_ge(added[j], k)
                        v.tensor_tensor(a, a, buf[:, j * half:(j + 1) * half, :], ALU.add).then_inc(added[j], 1)
                for j in range(2):
                    dve.wait_ge(added[j], TABLES)
                flag = self.aux2[:, :, 135:136].rearrange("p b o -> p (b o)")
                do(v.tensor_scalar(self.gout[:], flag, 1.0, None, ALU.min))
                do(v.tensor_scalar(cnt[:], flag, 1.0, None, ALU.max))
                do(v.reciprocal(cnt[:], cnt[:]))
                a = self.aux2[:, :, 0:D]
                do(v.tensor_tensor(a, a, cnt[:].rearrange("p (b o) -> p b o", o=1).broadcast_to([P, nb, D]), ALU.mult))

    def gru(self):
        nc, s, io, go = self.nc, self.s, self.io, self.setup_done
        q = self.product_sems("gru")
        arrays = [self.aux, self.aux2, self.hn]
        blank = self.sem("gru_blank")
        biased = {k: self.sem(f"gru_{k}") for k in ("biased", "gates", "asked", "n")}
        OPS = 5
        with ExitStack() as c:
            at = Arena(self.acc)
            w, stage, turned, psT, psO = self.product_memory("gru", c, 3, 4 * D, at)
            bi = at.take([P, 4 * D], F32)
            bh = at.take([P, 4 * D], F32)
            g = at.take([P, 2, 4 * D], F32)
            rz = at.take([P, 2, 2 * D], F32)
            t = at.take([P, 2, D], F32)
            n = at.take([P, 2, D], F32)
            block = c.enter_context(nc.Block())

            @block.sync
            def _(sp):
                wi, wh = io["w_ih_t"], io["w_hh_t"]
                sp.wait_ge(blank, 1)
                for k in range(2):
                    sp.dma_start(w[:, k, 0:3 * D], wi[k * D:(k + 1) * D, :]).then_inc(q["loaded"], 16)
                sp.dma_start(w[:, 2, 0:2 * D], wh[:, 0:2 * D]).then_inc(q["loaded"], 16)
                sp.dma_start(w[:, 2, 3 * D:4 * D], wh[:, 2 * D:3 * D]).then_inc(q["loaded"], 16)
                sp.dma_start(bi[:, 0:3 * D], self.bcast_row(io["b_ih"], 3 * D)).then_inc(q["loaded"], 16)
                sp.dma_start(bh[:, 0:2 * D], self.bcast_row(io["b_hh"][0:2 * D], 2 * D)).then_inc(q["loaded"], 16)
                sp.dma_start(bh[:, 3 * D:4 * D], self.bcast_row(io["b_hh"][2 * D:3 * D], D)).then_inc(q["loaded"], 16)

            @block.scalar
            def _(act):
                a = nc.scalar
                def turn(i):
                    self.product_scalar(act, i, q, arrays, stage, turned, psT)
                    for j in range(2):
                        hold(act, biased["biased"], 2 * i + j + 1, go)
                        a.activation(rz[:, j, :], g[:, j, 0:2 * D], ACT.Sigmoid).then_inc(biased["gates"], 1)
                    for j in range(2):
                        hold(act, biased["asked"], 2 * i + j + 1, go)
                        a.activation(n[:, j, :], t[:, j, :], ACT.Tanh).then_inc(biased["n"], 1)
                repeat(act, s.nb // 2, turn)

            @block.tensor
            def _(pe):
                self.product_tensor(pe, q, w, 4 * D, stage, turned, psT, psO, 7, None)

            @block.vector
            def _(dve):
                v = nc.vector
                do = Chain(dve, q["seq"])
                do(v.memset(bi[:], 0.0))
                do(v.memset(bh[:], 0.0))
                v.memset(w[:], 0.0).then_inc(blank, 1)
                dve.wait_ge(q["loaded"], 16 * 7)
                do(v.tensor_tensor(bi[:], bi[:], bh[:], ALU.add))
                def turn(i):
                    for j in range(2):
                        hold(dve, q["product"], 2 * i + j + 1, go)
                        v.tensor_tensor(g[:, j, :], psO[j][:], bi[:], ALU.add).then_inc(biased["biased"], 1)
                    for j in range(2):
                        hold(dve, biased["gates"], 2 * i + j + 1, go)
                        then = Turn(dve, q["seq"], (2 * i + j) * OPS + 3, go)
                        then(v.tensor_tensor(t[:, j, :], rz[:, j, 0:D], g[:, j, 3 * D:4 * D], ALU.mult))
                        v.tensor_tensor(t[:, j, :], t[:, j, :], g[:, j, 2 * D:3 * D], ALU.add)\
                            .then_inc(biased["asked"], 1)
                        hold(dve, biased["n"], 2 * i + j + 1, go)
                        one = bass.ds(2 * i + j, 1)
                        h = self.hn[:, one, :].rearrange("p o d -> p (o d)")
                        x = self.x[:, one, :].rearrange("p o d -> p (o d)")
                        then(v.tensor_tensor(t[:, j, :], h, n[:, j, :], ALU.subtract))
                        then(v.tensor_tensor(t[:, j, :], t[:, j, :], rz[:, j, D:2 * D], ALU.mult))
                        then(v.tensor_tensor(t[:, j, :], t[:, j, :], n[:, j, :], ALU.add))
                        then(v.tensor_tensor(x, x, t[:, j, :], ALU.add))
                        assert then.n == OPS
                        dve.sem_inc(q["finished"], 1)
                repeat(dve, s.nb // 2, turn)

    def norm(self, name, plus=None):
        nc, s = self.nc, self.s
        seq, ask, root = (self.sem(f"{name}_{k}") for k in ("seq", "ask", "root"))
        with ExitStack() as c:
            sums, rstd = self.sb("sums", [P, s.nb], F32, c), self.sb("rstd", [P, s.nb], F32, c)
            block = c.enter_context(nc.Block())

            @block.scalar
            def _(act):
                self.norm_scalar(act, sums, rstd, ask, root)

            @block.vector
            def _(dve):
                do = Chain(dve, seq)
                if plus is not None:
                    do(nc.vector.tensor_tensor(self.x[:], self.x[:], plus, ALU.add))
                self.norm_vector(dve, do, sums, rstd, ask, root)

    def root_nodes(self):
        nc, s, io, go = self.nc, self.s, self.io, self.setup_done
        K, W = s.node_types, s.node_types * D
        q = self.product_sems("root")
        OPS = 1 + K
        with ExitStack() as c:
            w, stage, turned, psT, psO = self.product_memory("root", c, 1, W)
            b = self.sb("root_bias", [P, W], F32, c)
            g = self.sb("root_g", [P, 2, W], F32, c)
            typ = self.sb("node_type", [P, s.nb], I32, c)
            own = self.sb("own_type", [P, K, s.nb], F32, c)
            block = c.enter_context(nc.Block())

            @block.sync
            def _(sp):
                sp.dma_start(w[:, 0, :], io["root_w_t"]).then_inc(q["loaded"], 16)
                sp.dma_start(b[:], self.bcast_row(io["root_b"], W)).then_inc(q["loaded"], 16)
                sp.dma_start(typ[:], io["node_type_t"]).then_inc(q["loaded"], 16)

            @block.scalar
            def _(act):
                def turn(i):
                    self.product_scalar(act, i, q, [self.hn], stage, turned, psT)
                repeat(act, s.nb // 2, turn)

            @block.tensor
            def _(pe):
                self.product_tensor(pe, q, w, W, stage, turned, psT, psO, 3, None)

            @block.vector
            def _(dve):
                v = nc.vector
                do = Chain(dve, q["seq"])
                dve.wait_ge(q["loaded"], 48)
                for k in range(K):
                    do(v.tensor_scalar(own[:, k, :], typ[:], float(k), None, ALU.is_equal))
                def turn(i):
                    for j in range(2):
                        at = bass.ds(2 * i + j, 1)
                        x = self.x[:, at, :].rearrange("p o d -> p (o d)")
                        hold(dve, q["product"], 2 * i + j + 1, go)
                        then = Turn(dve, q["seq"], (2 * i + j) * OPS + K, go)
                        then(v.tensor_tensor(g[:, j, :], psO[j][:, 0:W], b[:], ALU.add))
                        for k in range(K):
                            then(v.scalar_tensor_tensor(x, g[:, j, k * D:(k + 1) * D], own[:, k, at], x,
                                                        ALU.mult, ALU.add))
                        assert then.n == OPS
                        dve.sem_inc(q["finished"], 1)
                repeat(dve, s.nb // 2, turn)

    def edge_rows(self):
        nc, s, io, go = self.nc, self.s, self.io, self.setup_done
        H, turns = s.heads3, s.steps // U
        B = U // 2
        q = {k: self.sem(f"er_{k}") for k in ("idx", "sel", "turned", "selT", "projected", "target", "z", "capped",
                                              "raised", "polynomial", "logits", "seq", "consts", "att")}
        gathered = [self.sem(f"er_gathered{r}") for r in range(U)]
        stored = [self.sem(f"er_stored{r}") for r in range(U)]
        loaded = [self.sem(f"er_loaded{r}") for r in range(U)]
        with ExitStack() as c:
            at = Arena(self.hn, self.acc, self.aux2)
            rows = at.take([P, U, D], F32)
            att = at.take([P, U, D], F32)
            ea = at.take([P, U, D], F32)
            idx = at.take([P, U], I32)
            sel = at.take([P, RS, P], F32)
            selT = at.take([P, 2, P], F32)
            z = at.take([P, 2, B * D], F32)
            u = at.take([P, 2, B * D], F32)
            m = at.take([P, 2, B * D], F32)
            we = at.take([P, D], F32)
            attn = at.take([P, D // H], F32)
            attn_b = at.take([P, 1], F32)
            psT = [self.ps(f"er_pt{j}", c) for j in range(2)]
            psA = [self.ps(f"er_pa{j}", c) for j in range(2)]
            psE = [self.ps(f"er_pe{j}", c) for j in range(2)]
            block = c.enter_context(nc.Block())

            @block.gpsimd
            def _(pool):
                issued = self.issued
                def turn(i):
                    for r in range(U):
                        hold(pool, q["idx"], i * U + r + 1)
                        hold(pool, q["att"], i * U + r + 1 - U)
                        clear_ahead(pool, issued)
                        nc.gpsimd.indirect_dma_start(rows[:, r, :], None, self.t_sent,
                                                     bass.IndirectOffsetOnAxis(idx[:, r:r + 1], 0))\
                            .then_inc(gathered[r], 16)
                repeat(pool, turns, turn)

            @block.sync
            def _(sp):
                sp.dma_start(we[:], io["We"]).then_inc(q["consts"], 16)
                sp.dma_start(attn[:], self.bcast_row(io["attn_w"], D // H)).then_inc(q["consts"], 16)
                sp.dma_start(attn_b[:], self.bcast_row(io["attn_b"], 1)).then_inc(q["consts"], 16)
                def turn(i):
                    t = self.regs(SP, self.til, i, s.tiles - 1)
                    for r in range(U):
                        hold(sp, q["projected"], i * U + r + 1 - U, go)
                        sp.dma_start(ea[:, r, :], io["edge_t"][bass.ds(t[r], 1), :, :]
                                     .rearrange("o p d -> p (o d)")).then_inc(loaded[r], 16)
                repeat(sp, turns, turn)

            @block.scalar
            def _(act):
                a = nc.scalar
                def turn(i):
                    for r in range(U):
                        hold(act, q["turned"], i * U + r + 1, go)
                        hold(act, q["target"], i * U + r - 1, go)
                        a.activation(selT[:, r % 2, :], psT[r % 2][:, 0:P], ACT.Copy).then_inc(q["selT"], 1)
                        if r >= 2:
                            self.send(act, i, r - 2, q, att, stored)
                        if r == B + 1:
                            self.raise_e(act, i, 0, q, u)
                    for r in (U - 2, U - 1):
                        self.send(act, i, r, q, att, stored)
                    self.raise_e(act, i, 1, q, u)
                repeat(act, turns, turn)
                for r in range(U):
                    act.wait_ge(stored[r], 16 * turns)

            @block.tensor
            def _(pe):
                pe.wait_ge(q["consts"], 48)
                def turn(i):
                    b = self.regs(PE, self.blk, i, s.nb - 1)

                    def project(r):
                        self.expand_tensor(pe, i, r, q, sel, psT)
                        hold(pe, loaded[r], i * 16 + 16, go)
                        hold(pe, q["att"], i * U + r - 1, go)
                        nc.tensor.matmul(psA[r % 2][:, 0:D], ea[:, r, :], we[:], start=True, stop=True)\
                            .then_inc(q["projected"], 1)

                    def target(r):
                        hold(pe, q["selT"], i * U + r + 1, go)
                        hold(pe, q["z"], i * U + r - 1, go)
                        nc.tensor.matmul(psE[r % 2][:, 0:D], selT[:, r % 2, :],
                                         self.aux[:, bass.ds(b[r], 1), :], start=True, stop=True)\
                            .then_inc(q["target"], 1)
                    self.order(project, target)
                repeat(pe, turns, turn)

            @block.vector
            def _(dve):
                v = nc.vector
                v.tensor_copy(idx[:], self.src[:, 0:U]).then_inc(q["idx"], U)
                dve.wait_ge(q["consts"], 48)
                def turn(i):
                    def add(r):
                        hold(dve, gathered[r], i * 16 + 16, go)
                        self.refill(dve, i, r, idx, self.src, q["idx"])
                        hold(dve, q["projected"], i * U + r + 1, go)
                        hold(dve, stored[r], i * 16, go)
                        v.tensor_tensor(att[:, r, :], rows[:, r, :], psA[r % 2][:, 0:D], ALU.add)\
                            .then_inc(q["att"], 1)
                        hold(dve, q["target"], i * U + r + 1, go)
                        hold(dve, q["att"], i * U + r + 1, go)
                        v.tensor_tensor(z[:, r // B, (r % B) * D:(r % B + 1) * D], att[:, r, :],
                                        psE[r % 2][:, 0:D], ALU.add).then_inc(q["z"], 1)

                    def cap(k):
                        hold(dve, q["z"], i * U + (k + 1) * B, go)
                        v.tensor_scalar(u[:, k, :], z[:, k, :], 20.0, None, ALU.min).then_inc(q["capped"], 1)

                    def mish(k):
                        hold(dve, q["raised"], 2 * i + k + 1, go)
                        then = Turn(dve, q["seq"], (2 * i + k) * 7, go)
                        then(v.scalar_tensor_tensor(m[:, k, :], u[:, k, :], 2.0, u[:, k, :], ALU.add, ALU.mult))
                        then(v.tensor_scalar(u[:, k, :], m[:, k, :], 2.0, None, ALU.add))
                        then(v.reciprocal(u[:, k, :], u[:, k, :]))
                        then(v.tensor_tensor(m[:, k, :], m[:, k, :], u[:, k, :], ALU.mult))
                        then(v.tensor_tensor(m[:, k, :], m[:, k, :], z[:, k, :], ALU.mult))
                        parts = m[:, k, :].rearrange("p (b f) -> p b f", f=D // H)
                        then(v.tensor_tensor(parts, parts, attn[:].rearrange("p (o f) -> p o f", o=1)
                                             .broadcast_to([P, B * H, D // H]), ALU.mult))
                        then(v.tensor_reduce(self.w8[:, bass.ds(i * U + k * B, B), 0:H],
                                             m[:, k, :].rearrange("p (b h f) -> p b h f", h=H, f=D // H),
                                             AX.X, ALU.add))
                        assert then.n == 7
                    self.front = lambda r: self.select(dve, i, r, q, sel, q["turned"])
                    for r in range(U + 1):
                        if r < U:
                            self.front(r)
                        if r >= 1:
                            add(r - 1)
                        if r == B:
                            cap(0)
                        if r == B + 2:
                            mish(0)
                    cap(1)
                    mish(1)
                repeat(dve, turns, turn)
                v.tensor_scalar(self.w8[:, :, 0:H], self.w8[:, :, 0:H], attn_b[:, 0:1], None, ALU.add)\
                    .then_inc(q["logits"], 1)
                dve.wait_ge(q["logits"], 1)

    def send(self, act, i, r, q, att, stored):
        hold(act, q["att"], i * U + r + 1, self.setup_done)
        act.dma_start(self.t_rows[bass.ds(i * U + r, 1), :, :].rearrange("o p d -> p (o d)"), att[:, r, :])\
            .then_inc(stored[r], 16)

    def raise_e(self, act, i, k, q, u):
        hold(act, q["capped"], 2 * i + k + 1, self.setup_done)
        self.nc.scalar.activation(u[:, k, :], u[:, k, :], ACT.Exp).then_inc(q["raised"], 1)

    def merge_logits(self):
        nc, s, go = self.nc, self.s, self.setup_done
        T, NF, S, H = s.tiles, s.blocks - 1, s.steps, s.heads3
        seq, moved = self.sem("ml_seq"), self.sem("ml_moved")
        with nc.Block() as block:
            @block.vector
            def _(dve):
                v = nc.vector
                do = Chain(dve, seq)
                w = self.w8[:, :, 0:H]
                do(v.tensor_tensor(w, w, self.mask[:, 0:S].rearrange("p (s o) -> p s o", o=1)
                                   .broadcast_to([P, S, H]), ALU.mult))
                def turn(k):
                    t = dve.value_load(self.til[0:1, bass.ds(k + T, 1)], min_val=0, max_val=T - 1)
                    a = self.w8[:, bass.ds(t, 1), 0:H]
                    hold(dve, moved, k, go)
                    v.tensor_tensor(a, a, self.w8[:, bass.ds(k + T, 1), 0:H], ALU.add).then_inc(moved, 1)
                repeat(dve, NF, turn)
                dve.wait_ge(moved, NF)

    def edge_softmax(self):
        nc, s, go = self.nc, self.s, self.setup_done
        T, H, C, CT, ST = s.tiles, s.heads3, SCAN_CHUNKS, s.ctiles, s.stiles
        L, NF = CT * P, s.blocks - 1
        per = P // H
        groups = -(-ST // per)
        names = ("seq", "compact", "turned", "copied", "written", "loaded", "rows", "rowcopy", "carry",
                 "carried", "back", "backin", "backturned", "sub", "exped", "moved")
        q = {k: self.sem(f"es_{k}") for k in names}
        stage_free = [self.sem(f"es_stage{j}") for j in range(2)]
        arrived = [self.sem(f"es_arrived{j}") for j in range(2)]
        flat = lambda a: a[:].rearrange("p b d -> p (b d)")
        accf, auxf, aux2f, hnf = flat(self.acc), flat(self.aux), flat(self.aux2), flat(self.hn)
        assert 2 * L <= self.s.nb * 136 and L <= self.s.nb * D and ST * H <= L and H * C == P
        logits = accf[:, 0:ST * H]
        run = accf[:, L:2 * L]
        seqd = aux2f[:, 0:L]
        here, other = aux2f[:, L:2 * L].bitcast(I32), hnf[:, 0:L].bitcast(I32)
        reset = auxf[:, 0:L]
        with ExitStack() as c:
            stage = self.sb("es_stage", [P, 2, P], F32, c)
            edge = self.sb("es_edge", [P, 2], F32, c)
            row = self.sb("es_row", [1, 2 * P], F32, c)
            chain = self.sb("es_chain", [1, H * (C + 1)], F32, c)
            first = self.sb("es_first", [1, P], F32, c)
            start = self.sb("es_start", [P, 1], F32, c)
            ps = [self.ps(f"es_ps{j}", c) for j in range(2)]
            psR = self.ps("es_pr", c)
            psB = [self.ps(f"es_pb{j}", c) for j in range(2)]
            block = c.enter_context(nc.Block())
            dseq = io_seq = self.io["dst_seq"]
            tseq = self.t_seq.rearrange("t h e -> (t h) e")
            tmax = self.t_max.rearrange("t h e -> (t h) e")

            def chunked(t, h):
                return t[:, h, :].rearrange("(c j) e -> c j e", c=C)

            @block.sync
            def _(sp):
                for h in range(H):
                    for off, dst in ((1, here), (0, other)):
                        sp.dma_start(dst[h * C:(h + 1) * C, :], dseq[off:off + C * L].rearrange("(c l) -> c l", c=C))\
                            .then_inc(q["loaded"], 16)
                for g in range(groups):
                    sp.wait_ge(q["copied"], g + 1)
                    sp.dma_start(tseq[g * P:(g + 1) * P, :], stage[:, g % 2, :]).then_inc(stage_free[g % 2], 16)
                for j in range(2):
                    sp.wait_ge(stage_free[j], 16 * len(range(j, groups, 2)))
                for h in range(H):
                    sp.dma_start(seqd[h * C:(h + 1) * C, :].rearrange("p (j e) -> p j e", e=P), chunked(self.t_seq, h))\
                        .then_inc(q["written"], 16)
                sp.wait_ge(q["carry"], 5)
                for h in range(H):
                    sp.dma_start(other[h * C:(h + 1) * C, :], dseq[2:2 + C * L].rearrange("(c l) -> c l", c=C))\
                        .then_inc(q["loaded"], 16)
                sp.wait_ge(q["carry"], 10)
                for h in range(H):
                    sp.dma_start(chunked(self.t_max, h), run[h * C:(h + 1) * C, :].rearrange("p (j e) -> p j e", e=P))\
                        .then_inc(q["back"], 16)
                sp.wait_ge(q["back"], 16 * H)
                for g in range(groups):
                    if g >= 2:
                        sp.wait_ge(q["backturned"], g - 1)
                    sp.dma_start(stage[:, g % 2, :], tmax[g * P:(g + 1) * P, :]).then_inc(arrived[g % 2], 16)

            @block.tensor
            def _(pe):
                pe.wait_ge(q["compact"], 1)
                for g in range(groups):
                    if g >= 2:
                        pe.wait_ge(q["copied"], g - 1)
                    nc.tensor.transpose(ps[g % 2][:, 0:P], logits[:, g * P:(g + 1) * P], self.ident[:])\
                        .then_inc(q["turned"], 1)
                for d in range(2):
                    pe.wait_ge(q["carry"], 5 * d + 1)
                    for k in range(2):
                        nc.tensor.transpose(psR[0:1, k * P:(k + 1) * P], edge[:, k:k + 1], self.ident[:])\
                            .then_inc(q["rows"], 1)
                    pe.wait_ge(q["carry"], 5 * d + 4)
                    nc.tensor.matmul(psR[:, 2 * P:2 * P + 1], first[:], self.ones[0:1, 0:1], start=True, stop=True)\
                        .then_inc(q["rows"], 1)
                for g in range(groups):
                    pe.wait_ge(arrived[g % 2], 16 * (g // 2 + 1))
                    if g >= 2:
                        pe.wait_ge(q["sub"], g - 1)
                    nc.tensor.transpose(psB[g % 2][:, 0:P], stage[:, g % 2, :], self.ident[:])\
                        .then_inc(q["backturned"], 1)

            @block.scalar
            def _(act):
                for g in range(groups):
                    act.wait_ge(q["turned"], g + 1)
                    if g >= 2:
                        act.wait_ge(stage_free[g % 2], 16 * (g // 2))
                    nc.scalar.activation(stage[:, g % 2, :], ps[g % 2][:, 0:P], ACT.Copy).then_inc(q["copied"], 1)
                act.wait_ge(q["sub"], groups)
                nc.scalar.activation(self.w8[:, 0:T, 0:H], self.w8[:, 0:T, 0:H], ACT.Exp).then_inc(q["exped"], 1)

            @block.vector
            def _(dve):
                v = nc.vector
                do = Chain(dve, q["seq"])
                do(v.memset(logits, 0.0))
                v.tensor_copy(logits[:, 0:T * H].rearrange("p (t h) -> p t h", h=H), self.w8[:, 0:T, 0:H])\
                    .then_inc(q["compact"], 1)
                dve.wait_ge(q["loaded"], 32 * H)
                for d in range(2):
                    if d == 1:
                        dve.wait_ge(q["loaded"], 48 * H)
                    do(v.tensor_tensor(reset, here, other, ALU.not_equal))
                    do(v.tensor_scalar(reset, reset, -BIG, None, ALU.mult))
                    if d == 0:
                        dve.wait_ge(q["written"], 16 * H)
                    way = (lambda a: a) if d == 0 else (lambda a: a[:, ::-1])
                    data = seqd if d == 0 else run
                    out = run if d == 0 else seqd
                    do(v.tensor_tensor_scan(way(out), way(reset), way(data), -BIG, ALU.add, ALU.max))
                    end = L - 1 if d == 0 else 0
                    do(v.tensor_copy(edge[:, 0:1], out[:, end:end + 1]))
                    do(v.memset(chain[:], -BIG))
                    v.tensor_reduce(edge[:, 1:2], reset, AX.X, ALU.min).then_inc(q["carry"], 1)
                    dve.wait_ge(q["rows"], 3 * d + 2)
                    v.tensor_copy(row[:], psR[0:1, 0:2 * P]).then_inc(q["carry"], 1)
                    dve.wait_ge(q["carry"], 5 * d + 2)
                    for h in range(H):
                        a = row[0:1, h * C:(h + 1) * C]
                        r = row[0:1, P + h * C:P + (h + 1) * C]
                        at = h * (C + 1)
                        if d == 0:
                            o = chain[0:1, at + 1:at + 1 + C]
                        else:
                            a, r, o = a[:, ::-1], r[:, ::-1], chain[0:1, at:at + C][:, ::-1]
                        do(v.tensor_tensor_scan(o, r, a, -BIG, ALU.add, ALU.max))
                    dve.sem_inc(q["carry"], 1)
                    off = 0 if d == 0 else 1
                    v.tensor_copy(first[:].rearrange("p (h c) -> p h c", h=H),
                                  chain[:].rearrange("p (h c) -> p h c", h=H)[:, :, off:off + C])\
                        .then_inc(q["carry"], 1)
                    dve.wait_ge(q["rows"], 3 * d + 3)
                    do(v.tensor_copy(start[:], psR[:, 2 * P:2 * P + 1]))
                    final = run
                    v.tensor_tensor_scan(way(final), way(reset), way(data), start[:, 0:1], ALU.add, ALU.max)\
                        .then_inc(q["carry"], 1)
                    dve.wait_ge(q["carry"], 5 * d + 5)
                for g in range(groups):
                    n = min(per, T - g * per)
                    dve.wait_ge(q["backturned"], g + 1)
                    if n > 0:
                        w = self.w8[:, g * per:g * per + n, 0:H]
                        m = v.tensor_tensor(w, w, psB[g % 2][:, 0:n * H].rearrange("p (t h) -> p t h", h=H), ALU.subtract)
                    else:
                        m = v.memset(edge[:], 0.0)
                    m.then_inc(q["sub"], 1)
                dve.wait_ge(q["exped"], 1)
                def turn(k):
                    t = dve.value_load(self.til[0:1, bass.ds(k + T, 1)], min_val=0, max_val=T - 1)
                    v.tensor_copy(self.w8[:, bass.ds(k + T, 1), 0:H], self.w8[:, bass.ds(t, 1), 0:H])\
                        .then_inc(q["moved"], 1)
                repeat(dve, NF, turn)
                dve.wait_ge(q["moved"], NF)

    def output(self):
        nc, s, io = self.nc, self.s, self.io
        nb, H = s.nb, s.heads3
        seq, done, sent = self.sem("ou_seq"), self.sem("ou_done"), self.sem("ou_sent")
        with ExitStack() as c:
            den = self.sb("ou_den", [P, nb, H], F32, c)
            block = c.enter_context(nc.Block())

            @block.vector
            def _(dve):
                v = nc.vector
                do = Chain(dve, seq)
                do(v.tensor_scalar(den[:], self.acc[:, :, D:D + H], 1e-30, None, ALU.max))
                do(v.reciprocal(den[:], den[:]))
                for h in range(H):
                    a = self.acc[:, :, h * (D // H):(h + 1) * (D // H)]
                    do(v.tensor_tensor(a, a, den[:, :, h:h + 1].broadcast_to([P, nb, D // H]), ALU.mult))
                v.tensor_tensor(self.x[:], self.x[:], self.acc[:, :, 0:D], ALU.add).then_inc(done, 1)

            @block.sync
            def _(sp):
                sp.wait_ge(done, 1)
                sp.dma_start(io["out"].rearrange("(b p) d -> p b d", p=P), self.x[:]).then_inc(sent, 16)
                sp.wait_ge(sent, 16)

    def build(self):
        s, io = self.s, self.io
        with self.ctx:
            self.allocate()
            self.prepare()
            self.end_phase()
            self.gat_nodes()
            self.end_phase()
            self.gat_gather()
            self.end_phase()
            self.gat_softmax()
            self.end_phase()
            self.weighted_sum("gat_sum", s.heads0)
            self.end_phase()
            self.gat_output()
            self.end_phase()
            self.keep_h()
            self.end_phase()
            self.gather_sum("in_sum", self.t_h, self.src, types=True)
            self.end_phase()
            self.mean_in()
            self.end_phase()
            self.scatter_out()
            self.end_phase()
            self.mean_out()
            self.end_phase()
            self.plain_product("a_in", [self.acc], [io["W_in_t"]], [io["b_in"]], D, out=self.aux, gate=self.gin)
            self.end_phase()
            self.plain_product("a_out", [self.aux2], [io["W_out_t"]], [io["b_out"]], D, out=self.aux2, gate=self.gout)
            self.end_phase()
            self.gru()
            self.end_phase()
            self.norm("norm2")
            self.end_phase()
            W = s.rels * D // 2
            for k in range(2):
                self.plain_product(f"rel{k}", [self.hn], [io["rel_w_t"][:, k * W:(k + 1) * W]], [], W,
                                   table=self.t_rel.rearrange("n r d -> n (r d)"), cols=k * W)
                self.end_phase()
            self.root_nodes()
            self.end_phase()
            self.gather_sum("rel_sum", self.t_rel.rearrange("n r d -> (n r) d"), self.gidx, weight=self.w2)
            self.end_phase()
            self.norm("norm3", plus=self.acc[:, :, 0:D])
            self.end_phase()
            self.plain_product("sent", [self.hn], [io["Ws"]], [io["Ws_b"]], D, table=self.t_sent,
                               bias2=io["We_b"])
            self.end_phase()
            self.plain_product("recv", [self.hn], [io["Wr"]], [io["Wr_b"]], D, out=self.aux)
            self.end_phase()
            self.edge_rows()
            self.end_phase()
            self.merge_logits()
            self.end_phase()
            self.edge_softmax()
            self.end_phase()
            self.weighted_sum("att_sum", s.heads3)
            self.end_phase()
            self.output()
            self.end_phase()



def kernel(x, src, dst, edge_attr_128, edge_type_7, node_type_4, **w):
    import concourse.bacc as bacc
    from concourse.bass_utils import run_bass_kernel_spmd

    x, src, dst, ea, et, nt = (np.asarray(a) for a in (x, src, dst, edge_attr_128, edge_type_7, node_type_4))
    w = {k: np.asarray(a) for k, a in w.items()}
    n, e = x.shape[0], src.shape[0]
    s = Shape(n, e, w["L0_gnn_a_src"].shape[1], w["L3_gnn_Ws_k"].shape[1], w["L2_gnn_rel_w"].shape[0],
              w["L2_gnn_root_w"].shape[0])
    far = (s.blocks + 1) * P

    def by_tile(a, fill):
        return np.ascontiguousarray(np.pad(a, (0, s.tiles * P - e), constant_values=fill).reshape(s.tiles, P).T)

    flat = lambda a: np.ascontiguousarray(a.reshape(-1))
    mat = lambda a: np.ascontiguousarray(a.reshape(D, -1))
    arrays = {
        "x": np.pad(x, ((0, s.nb * P - n), (0, 0))),
        "src_t": by_tile(src, 0), "dst_t": by_tile(dst, far), "type_t": by_tile(et, 0),
        "dst_seq": np.pad(dst, (1, s.stiles * P - e + 1), constant_values=(-1, far)),
        "edge_t": np.ascontiguousarray(
            np.pad(ea, ((0, s.tiles * P - e), (0, 0))).reshape(s.tiles, P, D).transpose(0, 2, 1)),
        "node_type_t": np.ascontiguousarray(np.pad(nt, (0, s.nb * P - n)).reshape(s.nb, P).T),
        "W_proj": w["L0_gnn_W_proj"], "a_src": flat(w["L0_gnn_a_src"]), "a_trg": flat(w["L0_gnn_a_trg"]),
        "gat_bias": w["L0_gnn_bias"],
        "W_in_t": w["L1_gnn_W_in"].T, "b_in": w["L1_gnn_b_in"],
        "W_out_t": w["L1_gnn_W_out"].T, "b_out": w["L1_gnn_b_out"],
        "w_ih_t": w["L1_gnn_w_ih"].T, "w_hh_t": w["L1_gnn_w_hh"].T,
        "b_ih": w["L1_gnn_b_ih"], "b_hh": w["L1_gnn_b_hh"],
        "rel_w_t": w["L2_gnn_rel_w"].transpose(2, 0, 1).reshape(D, -1),
        "root_w_t": w["L2_gnn_root_w"].transpose(2, 0, 1).reshape(D, -1), "root_b": flat(w["L2_gnn_root_b"]),
        "Ws": mat(w["L3_gnn_Ws_k"]), "Wr": mat(w["L3_gnn_Wr_k"]), "We": mat(w["L3_gnn_We_k"]),
        "Ws_b": flat(w["L3_gnn_Ws_b"]), "Wr_b": flat(w["L3_gnn_Wr_b"]), "We_b": flat(w["L3_gnn_We_b"]),
        "attn_w": flat(w["L3_gnn_attn_w"]), "attn_b": w["L3_gnn_attn_b"],
    }
    arrays = {k: np.ascontiguousarray(a) for k, a in arrays.items()}
    nc = bacc.Bacc("TRN2", target_bir_lowering=False, num_devices=1)
    io = {k: nc.dram_tensor(f"in_{k}", a.shape, mybir.dt.from_np(a.dtype), kind="ExternalInput").ap()
          for k, a in arrays.items()}
    io["out"] = nc.dram_tensor("out", (s.nb * P, D), F32, kind="ExternalOutput").ap()
    Program(nc, s, io).build()
    r = run_bass_kernel_spmd(nc, [{f"in_{k}": a for k, a in arrays.items()}], core_ids=[0])
    return r.results[0]["out"][:n]
```

```python
from contextlib import ExitStack

import numpy as np

import concourse.bass as bass
from concourse import mybir

F32 = mybir.dt.float32
I32 = mybir.dt.int32
ALU = mybir.AluOpType
ACT = mybir.ActivationFunctionType
AX = mybir.AxisListType
DVE = mybir.EngineType.DVE
PE = mybir.EngineType.PE
SP = mybir.EngineType.SP

P = 128
D = 128
U = 8
HALF = U // 2
RS = 4
TABLES = 8
BIG = 1e30
EPS_LN = 1e-5
SCAN_CHUNKS = 32


class Shape:
    def __init__(self, n, e, heads0, heads3, rels, types):
        self.n, self.e = n, e
        self.blocks = -(-n // P)
        self.nb = self.blocks + self.blocks % 2
        self.tiles = -(-e // P)
        self.steps = -(-(self.tiles + self.blocks - 1) // U) * U
        self.heads0, self.heads3, self.rels, self.node_types = heads0, heads3, rels, types
        self.ctiles = -(-self.tiles // SCAN_CHUNKS)
        self.stiles = self.ctiles * SCAN_CHUNKS


class Chain:

    def __init__(self, eng, sem, start=0):
        self.eng, self.sem, self.n = eng, sem, start

    def __call__(self, ins):
        self.n += 1
        ins.then_inc(self.sem, 1)
        self.eng.wait_ge(self.sem, self.n)


class Turn(Chain):

    def __init__(self, eng, sem, start, go):
        super().__init__(eng, sem)
        self.start, self.go = start, go

    def __call__(self, ins):
        self.n += 1
        ins.then_inc(self.sem, 1)
        hold(self.eng, self.sem, self.start + self.n, self.go)


def clear_ahead(pool, issued):
    pool.sem_inc(issued, 1)


def hold(eng, sem, value, go=None):
    if isinstance(value, int):
        if value > 0:
            eng.wait_ge(sem, value)
        return
    eng.wait_ge(sem, value)
    if go is not None:
        eng.wait_ge(go, 1)


def repeat(eng, n, turn):
    turn(0)
    if n > 1:
        with eng.Fori(1, n) as i:
            turn(i)


class Arena:

    def __init__(self, *arrays):
        self.parts = [[a[:].rearrange("p b d -> p (b d)"), 0] for a in arrays]

    def take(self, shape, dt=F32):
        n = int(np.prod(shape[1:]))
        n8 = -(-n // 16) * 16
        part = next(p for p in self.parts if p[1] + n8 <= p[0].shape[1])
        ap = part[0][0:shape[0], part[1]:part[1] + n]
        part[1] += n8
        if dt != F32:
            ap = ap.bitcast(dt)
        if len(shape) == 3:
            ap = ap.rearrange("p (a b) -> p a b", a=shape[1])
        if len(shape) == 4:
            ap = ap.rearrange("p (a b c) -> p a b c", a=shape[1], b=shape[2])
        return ap


class Program:
    def __init__(self, nc, shape, io):
        self.nc, self.s, self.io = nc, shape, io
        self.ctx = ExitStack()
        self.count = 0
        self.phase_sems = []

    def sb(self, name, shape, dt=F32, ctx=None):
        self.count += 1
        return (ctx or self.ctx).enter_context(self.nc.sbuf_tensor(f"{name}_{self.count}", shape, dt))

    def ps(self, name, ctx):
        return ctx.enter_context(self.nc.psum_tensor(name, [P, 512], F32))

    def sem(self, name):
        self.count += 1
        handle = self.nc.alloc_semaphore(f"{name}_{self.count}")
        self.phase_sems.append(handle)
        return handle

    def end_phase(self):
        self.nc.clear_and_free_semaphores(self.phase_sems)
        self.nc.all_engine_barrier()
        self.phase_sems = []

    def scratch(self, name, shape):
        return self.nc.dram_tensor(name, shape, F32, kind="Internal").ap()

    def bcast_row(self, ap, width):
        return ap.rearrange("(o w) -> o w", o=1).broadcast_to([P, width])

    def allocate(self):
        s = self.s
        nb, S = s.nb, s.steps
        self.x = self.sb("x_res", [P, nb, D])
        self.hn = self.sb("h_norm", [P, nb, D])
        self.acc = self.sb("acc", [P, nb, 136])
        self.aux = self.sb("aux", [P, nb, D])
        self.aux2 = self.sb("aux2", [P, nb, 136])
        self.wts = self.sb("edge_w", [P, max(S * 8, nb * 136)])
        self.w8 = self.wts[:, 0:S * 8].rearrange("p (s h) -> p s h", h=8)
        self.rel = self.sb("rel_dst", [P, S + U])
        self.srcf = self.sb("src_f", [P, S + U])
        self.src = self.sb("src_i", [P, S + U], I32)
        self.typ = self.sb("type_f", [P, S + U])
        self.blk = self.sb("step_block", [1, U + S + U], I32)
        self.til = self.sb("step_tile", [1, U + S + U], I32)
        self.strg = self.sb("target_scores", [P, nb, s.heads0])
        self.ahead = self.wts[:, 0:S + U]
        self.sidx = self.sb("scatter_rows", [P, S + U], I32)
        self.gidx = self.sb("relation_rows", [P, S + U], I32)
        self.w2 = self.sb("relation_weight", [P, S + U])
        self.inv = self.sb("inverse_counts", [P, nb, 8])
        self.gin = self.sb("has_in_edges", [P, nb])
        self.gout = self.sb("has_out_edges", [P, nb])
        self.mask = self.sb("mask", [P, S + U])
        self.iota = self.sb("iota_row", [P, P])
        self.ident = self.sb("ident", [P, P])
        self.pidx = self.sb("partition_index", [P, 1])
        self.ones = self.sb("ones", [P, P])
        self.issued = self.nc.alloc_semaphore("indirect_issued")
        self.setup_done = self.nc.alloc_semaphore("setup_done")
        rows = nb * P
        self.t_gat = self.scratch("t_gat", (rows, 136))
        self.t_h = self.scratch("t_h", (rows, D))
        self.t_rel = self.scratch("t_rel", (rows, s.rels, D))
        self.t_sent = self.scratch("t_sent", (rows, D))
        self.t_rows = self.scratch("t_rows", (S, P, D))
        self.t_out = [self.scratch(f"t_out{k}", (rows + P, 136)) for k in range(TABLES)]
        self.t_relrow = self.scratch("t_relrow", (S * P,))
        self.t_srcrow = self.scratch("t_srcrow", (S * P,))
        self.t_seq = self.scratch("t_seq", (s.stiles, s.heads3, P))
        self.t_max = self.scratch("t_max", (s.stiles, s.heads3, P))

    def prepare(self):
        nc, s, io = self.nc, self.s, self.io
        T, S, NF = s.tiles, s.steps, s.blocks - 1
        with ExitStack() as c:
            at = Arena(self.x, self.hn, self.acc)
            raw = at.take([P, T], I32)
            rawt = at.take([P, T], I32)
            dstf = at.take([P, S + U], F32)
            base = at.take([P, S + U], F32)
            on = at.take([P, S + U], F32)
            junk = at.take([P, S + U], F32)
            below = at.take([P, NF], F32)
            bi = at.take([P, S + U], I32)
            ti = at.take([P, S + U], I32)
            fi = at.take([P, NF], I32)
            io_i = at.take([P, P], I32)
            io_p = at.take([P, 1], I32)
            io_t = at.take([P, S + U], I32)
            row0 = at.take([P, P], F32)
            thr = at.take([P, NF], F32)
            thi = at.take([P, NF], I32)
            psA = [self.ps(f"p_first{k}", c) for k in range(-(-T // 512))]
            psB = self.ps("p_below", c)
            psT = [self.ps(f"p_turned{j}", c) for j in range(2)]
            line = at.take([P, 4, P], F32)
            turned_rows, lined = self.sem("turned_rows"), self.sem("lined")
            ready = self.sem("ready")
            written = [self.sem(f"written{j}") for j in range(4)]
            parts = [(a, dst, k, min(P, S - k)) for a, dst in ((self.rel, self.t_relrow), (self.srcf, self.t_srcrow))
                     for k in range(0, S, P)]
            loaded, made, seq = self.sem("loaded"), self.sem("iotas"), self.sem("seq")
            rows_ready, counted, summed = self.sem("dst_ready"), self.sem("counted"), self.sem("summed")
            moved = self.sem("moved")
            block = c.enter_context(nc.Block())

            @block.sync
            def _(sp):
                sp.dma_start(raw[:], io["dst_t"]).then_inc(loaded, 16)
                sp.dma_start(rawt[:], io["type_t"]).then_inc(loaded, 16)
                sp.dma_start(self.src[:, 0:T], io["src_t"]).then_inc(loaded, 16)
                for g, (_, dst, k, n) in enumerate(parts):
                    sp.wait_ge(lined, g + 1)
                    sp.dma_start(dst[k * P:(k + n) * P].rearrange("(s e) -> s e", e=P), line[0:n, g % 4, :])\
                        .then_inc(written[g % 4], 16)
                for j in range(4):
                    sp.wait_ge(written[j], 16 * len(parts[j::4]))

            @block.gpsimd
            def _(pool):
                nc.gpsimd.iota(io_i[:], pattern=[[1, P]], base=0, channel_multiplier=0).then_inc(made, 1)
                nc.gpsimd.iota(io_p[:], pattern=[[0, 1]], base=0, channel_multiplier=1).then_inc(made, 1)
                nc.gpsimd.iota(io_t[:], pattern=[[1, S + U]], base=0, channel_multiplier=0).then_inc(made, 1)
                nc.gpsimd.iota(thi[:], pattern=[[P, NF]], base=P, channel_multiplier=0).then_inc(made, 1)

            @block.tensor
            def _(pe):
                pe.wait_ge(rows_ready, 1)
                for k, p in enumerate(psA):
                    w = min(512, T - 512 * k)
                    nc.tensor.matmul(p[:, 0:w], row0[:], dstf[:, 512 * k:512 * k + w],
                                     start=True, stop=True).then_inc(summed, 1)
                pe.wait_ge(counted, 1)
                nc.tensor.matmul(psB[:, 0:NF], self.ones[:], below[:], start=True, stop=True).then_inc(summed, 1)
                pe.wait_ge(ready, 1)
                for g, (a, _, k, n) in enumerate(parts):
                    if g >= 2:
                        pe.wait_ge(lined, g - 1)
                    nc.tensor.transpose(psT[g % 2][0:n, 0:P], a[:, k:k + n], self.ident[:]).then_inc(turned_rows, 1)

            @block.vector
            def _(dve):
                v = nc.vector
                do = Chain(dve, seq)
                do(v.memset(self.ones[:], 1.0))
                do(v.memset(dstf[:], float((s.blocks + 1) * P)))
                do(v.memset(self.typ[:], 0.0))
                do(v.memset(self.srcf[:], 0.0))
                do(v.memset(on[:], 0.0))
                do(v.memset(on[:, 0:T], 1.0))
                do(v.memset(base[:], 0.0))
                do(v.memset(bi[:], 0))
                do(v.memset(self.rel[:], 0.0))
                dve.wait_ge(made, 4)
                do(v.tensor_copy(self.iota[:], io_i[:]))
                do(v.tensor_copy(self.pidx[:], io_p[:]))
                do(v.tensor_copy(thr[:], thi[:]))
                do(v.tensor_copy(ti[:], io_t[:]))
                do(v.tensor_scalar(self.ident[:], self.iota[:], self.pidx[:, 0:1], None, ALU.is_equal))
                do(v.memset(row0[:], 0.0))
                do(v.memset(row0[0:1, :], 1.0))
                dve.wait_ge(loaded, 48)
                do(v.tensor_copy(self.typ[:, 0:T], rawt[:]))
                do(v.tensor_copy(self.srcf[:, 0:T], self.src[:, 0:T]))
                v.tensor_copy(dstf[:, 0:T], raw[:]).then_inc(rows_ready, 1)
                dve.wait_ge(rows_ready, 1)
                def turn(k):
                    hold(dve, moved, k)
                    v.tensor_scalar(junk[:, 0:T], dstf[:, 0:T], thr[:, bass.ds(k, 1)], 0.0,
                                    ALU.is_lt, ALU.add, accum_out=below[:, bass.ds(k, 1)]).then_inc(moved, 1)
                repeat(dve, NF, turn)
                dve.wait_ge(moved, NF)
                do(v.tensor_copy(junk[:, 0:NF], below[:]))
                v.tensor_copy(below[:], junk[:, 0:NF]).then_inc(counted, 1)
                dve.wait_ge(counted, 1)
                dve.wait_ge(summed, len(psA) + 1)
                for k, p in enumerate(psA):
                    w = min(512, T - 512 * k)
                    do(v.tensor_copy(bi[:, 512 * k:512 * k + w], p[:, 0:w]))
                do(v.tensor_single_scalar(bi[:, 0:T], bi[:, 0:T], 7, ALU.arith_shift_right))
                do(v.tensor_single_scalar(bi[:, 0:T], bi[:, 0:T], 7, ALU.logical_shift_left))
                do(v.tensor_copy(base[:, 0:T], bi[:, 0:T]))
                do(v.tensor_single_scalar(bi[:, 0:T], bi[:, 0:T], 7, ALU.arith_shift_right))
                do(v.tensor_copy(fi[:], psB[:, 0:NF]))
                do(v.tensor_single_scalar(ti[:, T:T + NF], fi[:], 7, ALU.arith_shift_right))
                do(v.tensor_single_scalar(fi[:], fi[:], P - 1, ALU.bitwise_and))
                do(v.tensor_copy(junk[:, 0:NF], fi[:]))
                do(v.tensor_scalar(on[:, T:T + NF], junk[:, 0:NF], 0.0, None, ALU.is_gt))
                do(v.tensor_copy(junk[:, 0:NF], ti[:, T:T + NF]))
                do(v.tensor_scalar(junk[:, 0:NF], junk[:, 0:NF], float(T - 1), None, ALU.min))
                do(v.tensor_copy(ti[:, T:T + NF], junk[:, 0:NF]))
                do(v.memset(ti[:, T + NF:S + U], 0))
                do(v.tensor_copy(base[:, T:T + NF], thr[:]))
                do(v.tensor_copy(bi[:, T:T + NF], io_t[:, 1:NF + 1]))
                do(v.memset(self.blk[:], 0))
                do(v.memset(self.til[:], 0))
                do(v.tensor_copy(self.blk[:, U:], bi[0:1, :]))
                do(v.tensor_copy(self.til[:, U:], ti[0:1, :]))
                def turn(k):
                    t = dve.value_load(self.til[0:1, bass.ds(k + (T + U), 1)], min_val=0, max_val=T - 1)
                    for a in (dstf, self.srcf, self.typ):
                        v.tensor_copy(a[:, bass.ds(k + T, 1)], a[:, bass.ds(t, 1)]).then_inc(moved, 1)
                repeat(dve, NF, turn)
                dve.wait_ge(moved, 4 * NF)
                do(v.tensor_copy(self.src[:], self.srcf[:]))
                do(v.tensor_scalar(on[:], on[:], 1.0, -1e6, ALU.subtract, ALU.mult))
                do(v.tensor_tensor(junk[:], dstf[:], base[:], ALU.subtract))
                do(v.tensor_tensor(self.rel[:], junk[:], on[:], ALU.add))
                do(v.tensor_scalar(junk[:], self.rel[:], 0.0, None, ALU.is_ge))
                do(v.tensor_scalar(self.mask[:], self.rel[:], float(P), None, ALU.is_lt))
                do(v.tensor_tensor(self.mask[:], self.mask[:], junk[:], ALU.mult))
                dve.sem_inc(self.setup_done, 1)
                dve.sem_inc(ready, 1)
                for g, (_, _, _, n) in enumerate(parts):
                    dve.wait_ge(turned_rows, g + 1)
                    if g >= 4:
                        dve.wait_ge(written[g % 4], 16 * (g // 4))
                    v.tensor_copy(line[0:n, g % 4, :], psT[g % 2][0:n, 0:P]).then_inc(lined, 1)

    def norm_vector(self, dve, do, sums, rstd, ask, done):
        v, nb = self.nc.vector, self.s.nb
        wide = lambda a: a[:].rearrange("p (b o) -> p b o", o=1).broadcast_to([P, nb, D])
        do(v.tensor_reduce(sums[:], self.x[:], AX.X, ALU.add))
        do(v.tensor_scalar(sums[:], sums[:], 1.0 / D, None, ALU.mult))
        do(v.tensor_tensor(self.hn[:], self.x[:], wide(sums), ALU.subtract))
        do(v.tensor_tensor(self.acc[:, :, 0:D], self.hn[:], self.hn[:], ALU.mult))
        do(v.tensor_reduce(sums[:], self.acc[:, :, 0:D], AX.X, ALU.add))
        v.tensor_scalar(sums[:], sums[:], 1.0 / D, EPS_LN, ALU.mult, ALU.add).then_inc(ask, 1)
        dve.wait_ge(done, 1)
        do(v.reciprocal(rstd[:], rstd[:]))
        do(v.tensor_tensor(self.hn[:], self.hn[:], wide(rstd), ALU.mult))
        do(v.tensor_scalar(self.hn[:], self.hn[:], 0.0, None, ALU.max))

    def norm_scalar(self, act, sums, rstd, ask, done):
        act.wait_ge(ask, 1)
        self.nc.scalar.activation(rstd[:], sums[:], ACT.Sqrt).then_inc(done, 1)

    def product_sems(self, name):
        return {k: self.sem(f"{name}_{k}") for k in
                ("loaded", "staged", "turned_ps", "turned", "product", "finished", "seq", "stored0", "stored1")}

    def product_memory(self, name, c, k, width, at=None):
        take = at.take if at else lambda shape: self.sb(name, shape, F32, c)
        return (take([P, k, width]), take([P, 2, k, D]), take([P, 2, k, D]),
                [self.ps(f"{name}_pt{j}", c) for j in range(2)], [self.ps(f"{name}_po{j}", c) for j in range(2)])

    def product_scalar(self, act, i, q, arrays, stage, turned, psT):
        go, K = self.setup_done, len(arrays)
        for j in range(2):
            hold(act, q["turned_ps"], (2 * i + j - 1) * K, go)
            for k in range(K):
                self.nc.scalar.activation(stage[:, j, k, :], arrays[k][:, bass.ds(2 * i + j, 1), 0:D],
                                          ACT.Copy).then_inc(q["staged"], 1)
        for j in range(2):
            hold(act, q["product"], 2 * i + j - 1, go)
            hold(act, q["turned_ps"], (2 * i + j) * K + K, go)
            for k in range(K):
                self.nc.scalar.activation(turned[:, j, k, :], psT[j][:, k * D:k * D + D],
                                          ACT.Copy).then_inc(q["turned"], 1)

    def product_tensor(self, pe, q, w, width, stage, turned, psT, psO, loads, blocks_used):
        nc, go, K = self.nc, self.setup_done, w.shape[1]
        pe.wait_ge(q["loaded"], 16 * loads)
        def turn(i):
            for j in range(2):
                hold(pe, q["turned"], (2 * i + j - 1) * K, go)
                for k in range(K):
                    hold(pe, q["staged"], (2 * i + j) * K + k + 1, go)
                    nc.tensor.transpose(psT[j][:, k * D:k * D + D], stage[:, j, k, :],
                                        self.ident[:]).then_inc(q["turned_ps"], 1)
            for j in range(2):
                hold(pe, q["turned"], (2 * i + j) * K + K, go)
                hold(pe, q["finished"], 2 * i + j - 1, go)
                for k in range(K):
                    m = nc.tensor.matmul(psO[j][:, 0:width], turned[:, j, k, :], w[:, k, :],
                                         start=(k == 0), stop=(k == K - 1))
                m.then_inc(q["product"], 1)
        repeat(pe, self.s.nb // 2, turn)

    def gat_nodes(self):
        nc, s, io, go = self.nc, self.s, self.io, self.setup_done
        H = s.heads0
        F = D // H
        q = self.product_sems("gat")
        load_x, ask, root = self.sem("load_x"), self.sem("ask"), self.sem("root")
        normed, seq = self.sem("normed"), self.sem("seq")
        with ExitStack() as c:
            w, stage, turned, psT, psO = self.product_memory("gat", c, 1, D)
            a_src = self.sb("a_src", [P, D], F32, c)
            a_trg = self.sb("a_trg", [P, D], F32, c)
            rows = self.sb("gat_rows", [P, 2, 136], F32, c)
            scaled = self.sb("scaled", [P, 2, D], F32, c)
            sums, rstd = self.sb("sums", [P, s.nb], F32, c), self.sb("rstd", [P, s.nb], F32, c)
            block = c.enter_context(nc.Block())

            @block.sync
            def _(sp):
                sp.dma_start(self.x[:], io["x"].rearrange("(b p) d -> p b d", p=P)).then_inc(load_x, 16)
                sp.dma_start(w[:, 0, :], io["W_proj"]).then_inc(q["loaded"], 16)
                sp.dma_start(a_src[:], self.bcast_row(io["a_src"], D)).then_inc(q["loaded"], 16)
                sp.dma_start(a_trg[:], self.bcast_row(io["a_trg"], D)).then_inc(q["loaded"], 16)
                table = self.t_gat.rearrange("(b p) d -> b p d", p=P)
                def turn(i):
                    for j in range(2):
                        hold(sp, q["finished"], 2 * i + j + 1, go)
                        sp.dma_start(table[bass.ds(2 * i + j, 1), :, :].rearrange("o p d -> p (o d)"),
                                     rows[:, j, :]).then_inc(q[f"stored{j}"], 16)
                repeat(sp, s.nb // 2, turn)
                for j in range(2):
                    sp.wait_ge(q[f"stored{j}"], 16 * (s.nb // 2))

            @block.scalar
            def _(act):
                self.norm_scalar(act, sums, rstd, ask, root)
                act.wait_ge(normed, 1)
                def turn(i):
                    self.product_scalar(act, i, q, [self.hn], stage, turned, psT)
                repeat(act, s.nb // 2, turn)

            @block.tensor
            def _(pe):
                self.product_tensor(pe, q, w, D, stage, turned, psT, psO, 3, None)

            @block.vector
            def _(dve):
                v = nc.vector
                do = Chain(dve, seq)
                dve.wait_ge(load_x, 16)
                self.norm_vector(dve, do, sums, rstd, ask, root)
                dve.sem_inc(normed, 1)
                dve.wait_ge(q["loaded"], 48)
                def turn(i):
                    for j in range(2):
                        hold(dve, q["product"], 2 * i + j + 1, go)
                        hold(dve, q[f"stored{j}"], i * 16, go)
                        then = Turn(dve, q["seq"], (2 * i + j) * 5, go)
                        then(v.tensor_copy(rows[:, j, 0:D], psO[j][:, 0:D]))
                        then(v.tensor_copy(self.aux[:, bass.ds(2 * i + j, 1), :], psO[j][:, 0:D]))
                        then(v.tensor_tensor(scaled[:, 0, :], rows[:, j, 0:D], a_src[:], ALU.mult))
                        then(v.tensor_tensor(scaled[:, 1, :], rows[:, j, 0:D], a_trg[:], ALU.mult))
                        then(v.tensor_reduce(self.strg[:, bass.ds(2 * i + j, 1), :],
                                             scaled[:, 1, :].rearrange("p (h f) -> p h f", f=F), AX.X, ALU.add))
                        v.tensor_reduce(rows[:, j, D:D + H], scaled[:, 0, :].rearrange("p (h f) -> p h f", f=F),
                                        AX.X, ALU.add).then_inc(q["finished"], 1)
                repeat(dve, s.nb // 2, turn)

    def plain_product(self, name, arrays, weights, bias, width, out=None, table=None, cols=0, gate=None, bias2=None):
        nc, s, go = self.nc, self.s, self.setup_done
        K = len(arrays)
        q = self.product_sems(name)
        with ExitStack() as c:
            w, stage, turned, psT, psO = self.product_memory(name, c, K, width)
            b = self.sb(f"{name}_bias", [P, width], F32, c)
            gb = self.sb(f"{name}_gated", [P, 2, width], F32, c) if gate is not None else None
            rows = self.sb(f"{name}_rows", [P, 2, width], F32, c) if table is not None else None
            block = c.enter_context(nc.Block())
            b2 = self.sb(f"{name}_bias2", [P, width], F32, c) if bias2 is not None else None
            loads = K + len(bias) + (bias2 is not None)

            @block.sync
            def _(sp):
                for k in range(K):
                    sp.dma_start(w[:, k, :], weights[k]).then_inc(q["loaded"], 16)
                at = 0
                for part in bias:
                    n = part.shape[0]
                    sp.dma_start(b[:, at:at + n], self.bcast_row(part, n)).then_inc(q["loaded"], 16)
                    at += n
                if bias2 is not None:
                    sp.dma_start(b2[:], self.bcast_row(bias2, width)).then_inc(q["loaded"], 16)
                if table is not None:
                    tab = table.rearrange("(b p) d -> b p d", p=P)
                    def turn(i):
                        for j in range(2):
                            hold(sp, q["finished"], 2 * i + j + 1, go)
                            sp.dma_start(tab[bass.ds(2 * i + j, 1), :, cols:cols + width]
                                         .rearrange("o p d -> p (o d)"), rows[:, j, :]).then_inc(q[f"stored{j}"], 16)
                    repeat(sp, s.nb // 2, turn)
                    for j in range(2):
                        sp.wait_ge(q[f"stored{j}"], 16 * (s.nb // 2))

            @block.scalar
            def _(act):
                def turn(i):
                    self.product_scalar(act, i, q, arrays, stage, turned, psT)
                repeat(act, s.nb // 2, turn)

            @block.tensor
            def _(pe):
                self.product_tensor(pe, q, w, width, stage, turned, psT, psO, loads, None)

            @block.vector
            def _(dve):
                v = nc.vector
                dve.wait_ge(q["loaded"], 16 * loads)
                do = Chain(dve, q["seq"])
                if not bias:
                    do(v.memset(b[:], 0.0))
                if bias2 is not None:
                    do(v.tensor_tensor(b[:], b[:], b2[:], ALU.add))
                first = do.n
                def turn(i):
                    for j in range(2):
                        hold(dve, q["product"], 2 * i + j + 1, go)
                        plus = b[:]
                        if gate is not None:
                            then = Turn(dve, q["seq"], 2 * i + j + first, go)
                            then(v.tensor_scalar(gb[:, j, :], b[:], gate[:, bass.ds(2 * i + j, 1)], None, ALU.mult))
                            plus = gb[:, j, :]
                        if table is not None:
                            hold(dve, q[f"stored{j}"], i * 16, go)
                            dst = rows[:, j, :]
                        else:
                            dst = out[:, bass.ds(2 * i + j, 1), 0:width].rearrange("p o d -> p (o d)")
                        v.tensor_tensor(dst, psO[j][:, 0:width], plus, ALU.add).then_inc(q["finished"], 1)
                repeat(dve, s.nb // 2, turn)

    def refill(self, i, r, idx, source, idx_ready):
        self.nc.vector.tensor_copy(idx[:, r:r + 1], source[:, bass.ds(i * U + r + U, 1)]).then_inc(idx_ready, 1)

    def load_rows(self, sp, i, r, table, rows, used, landed):
        if r % HALF == 0:
            h = r // HALF
            hold(sp, used, i * U + r + HALF - U, self.setup_done)
            sp.dma_start(rows[:, h, :], table[bass.ds((i * U + r) * P, HALF * P)]
                         .rearrange("(o w) -> o w", o=1).broadcast_to([P, HALF * P])).then_inc(landed[h], 16)

    def select_turned(self, dve, i, r, rows, landed, selT, used, made):
        if r % HALF == 0:
            hold(dve, landed[r // HALF], i * 16 + 16, self.setup_done)
        hold(dve, used, i * U + r + 1 - RS, self.setup_done)
        self.nc.vector.tensor_scalar(selT[:, r % RS, :], rows[:, r // HALF, (r % HALF) * P:(r % HALF + 1) * P],
                                     self.pidx[:, 0:1], None, ALU.is_equal).then_inc(made, 1)

    def select(self, dve, i, r, q, sel, used, weight=None):
        hold(dve, used, i * U + r + 1 - RS, self.setup_done)
        col = bass.ds(i * U + r, 1)
        if weight is None:
            m = self.nc.vector.tensor_scalar(sel[:, r % RS, :], self.iota[:], self.rel[:, col], None, ALU.is_equal)
        else:
            m = self.nc.vector.tensor_scalar(sel[:, r % RS, :], self.iota[:], self.rel[:, col], weight[:, col],
                                             ALU.is_equal, ALU.mult)
        m.then_inc(q["sel"], 1)

    def flow(self, eng, parts, blocks_for=None, tiles_for=None):
        turns = self.s.steps // U

        def turn(i):
            last = isinstance(i, int) and i == turns
            numbers = {}
            for f, row, top in ((blocks_for, self.blk, self.s.nb - 1), (tiles_for, self.til, self.s.tiles - 1)):
                if f is not None:
                    lag = next(g for g, h in parts if h is f)
                    if not last or lag:
                        kind = {"PE": PE, "DVE": DVE, "SP": SP}[f.engine]
                        _, numbers[f] = self.nc.values_load_multi_w_load_instructions(
                            row[0:1, bass.ds(i * U + (U - lag), U)], engines=[kind], min_val=0, max_val=top,
                            skip_runtime_bounds_check_because="the numbers are bounded when made")
            for r in range(U):
                for lag, f in parts:
                    k, j = (r - lag, i) if r >= lag else (r - lag + U, i - 1)
                    if (isinstance(j, int) and j < 0) or (last and j is i):
                        continue
                    f(j, k, numbers[f][r] if f in numbers else None)

        for i in range(min(2, turns)):
            turn(i)
        if turns > 2:
            with eng.Fori(2, turns) as i:
                turn(i)
        turn(turns)

    def gat_gather(self):
        nc, s, go = self.nc, self.s, self.setup_done
        H, turns = s.heads0, s.steps // U
        q = {k: self.sem(f"gg_{k}") for k in ("idx", "selT", "target", "logit")}
        gathered = [self.sem(f"gg_gathered{r}") for r in range(U)]
        stored = [self.sem(f"gg_stored{r}") for r in range(U)]
        landed = [self.sem(f"gg_landed{h}") for h in range(2)]
        with ExitStack() as c:
            at = Arena(self.aux2)
            rows = at.take([P, U, 136])
            idx = at.take([P, U], I32)
            relrow = at.take([P, 2, HALF * P])
            selT = at.take([P, RS, P])
            psE = [self.ps(f"gg_pe{j}", c) for j in range(4)]
            block = c.enter_context(nc.Block())

            @block.gpsimd
            def _(pool):
                def gather(i, r, _):
                    hold(pool, q["idx"], i * U + r + 1)
                    hold(pool, q["logit"], i * U + r + 1 - U)
                    hold(pool, stored[r], i * 16)
                    clear_ahead(pool, self.issued)
                    nc.gpsimd.indirect_dma_start(rows[:, r, :], None, self.t_gat,
                                                 bass.IndirectOffsetOnAxis(idx[:, r:r + 1], 0))\
                        .then_inc(gathered[r], 16)
                self.flow(pool, [(0, gather)])

            @block.sync
            def _(sp):
                def rel(i, r, _):
                    self.load_rows(sp, i, r, self.t_relrow, relrow, q["selT"], landed)

                def store(i, r, _):
                    hold(sp, gathered[r], i * 16 + 16, go)
                    sp.dma_start(self.t_rows[bass.ds(i * U + r, 1), :, :].rearrange("o p d -> p (o d)"),
                                 rows[:, r, 0:D]).then_inc(stored[r], 16)
                self.flow(sp, [(0, rel), (4, store)])
                for r in range(U):
                    sp.wait_ge(stored[r], 16 * turns)

            @block.tensor
            def _(pe):
                def target(i, r, b):
                    hold(pe, q["selT"], i * U + r + 1, go)
                    hold(pe, q["logit"], i * U + r + 1 - 4, go)
                    nc.tensor.matmul(psE[r % 4][:, 0:H], selT[:, r % RS, :], self.strg[:, bass.ds(b, 1), :],
                                     start=True, stop=True).then_inc(q["target"], 1)
                target.engine = "PE"
                self.flow(pe, [(0, target)], blocks_for=target)

            @block.vector
            def _(dve):
                v = nc.vector
                v.tensor_copy(idx[:], self.src[:, 0:U]).then_inc(q["idx"], U)

                def select(i, r, _):
                    self.select_turned(dve, i, r, relrow, landed, selT, q["target"], q["selT"])

                def logit(i, r, _):
                    hold(dve, gathered[r], i * 16 + 16, go)
                    self.refill(i, r, idx, self.src, q["idx"])
                    hold(dve, q["target"], i * U + r + 1, go)
                    v.tensor_tensor(self.w8[:, bass.ds(i * U + r, 1), 0:H].rearrange("p o h -> p (o h)"),
                                    rows[:, r, D:D + H], psE[r % 4][:, 0:H], ALU.add).then_inc(q["logit"], 1)
                self.flow(dve, [(0, select), (2, logit)])

    def gat_softmax(self):
        nc, s = self.nc, self.s
        S, H = s.steps, s.heads0
        seq, ready, turned, top = (self.sem(f"gs_{k}") for k in ("seq", "ready", "turned", "top"))
        with ExitStack() as c:
            off = self.sb("off", [P, S], F32, c)
            part = self.sb("part_max", [P, 1], F32, c)
            tops = self.sb("tops", [1, P], F32, c)
            one = self.sb("one_max", [1, 1], F32, c)
            low = self.sb("minus_max", [P, 1], F32, c)
            ps = self.ps("gs_ps", c)
            block = c.enter_context(nc.Block())
            w = self.w8[:, :, 0:H]

            @block.tensor
            def _(pe):
                pe.wait_ge(ready, 1)
                nc.tensor.transpose(ps[0:1, 0:P], part[:], self.ident[:]).then_inc(turned, 1)
                pe.wait_ge(ready, 2)
                nc.tensor.matmul(ps[:, P:P + 1], self.ones[0:1, :], one[:], start=True, stop=True).then_inc(turned, 1)

            @block.scalar
            def _(act):
                act.wait_ge(top, 1)
                nc.scalar.activation(w, w, ACT.Exp, bias=low[:, 0:1])

            @block.vector
            def _(dve):
                v = nc.vector
                do = Chain(dve, seq)
                wide = lambda a: a[:, 0:S].rearrange("p (s o) -> p s o", o=1).broadcast_to([P, S, H])
                do(v.scalar_tensor_tensor(w, w, 0.2, w, ALU.mult, ALU.max))
                do(v.tensor_scalar(off[:], self.mask[:, 0:S], 1.0, BIG, ALU.subtract, ALU.mult))
                do(v.tensor_tensor(w, w, wide(self.mask), ALU.mult))
                do(v.tensor_tensor(w, w, wide(off), ALU.add))
                v.tensor_reduce(part[:], w, AX.XY, ALU.max).then_inc(ready, 1)
                dve.wait_ge(turned, 1)
                do(v.tensor_copy(tops[:], ps[0:1, 0:P]))
                v.tensor_reduce(one[:], tops[:], AX.X, ALU.max).then_inc(ready, 1)
                dve.wait_ge(turned, 2)
                v.tensor_scalar(low[:], ps[:, P:P + 1], -1.0, None, ALU.mult).then_inc(top, 1)

    def weighted_sum(self, name, H):
        nc, s, go = self.nc, self.s, self.setup_done
        q = {k: self.sem(f"{name}_{k}") for k in ("sel", "scaled", "summed", "added", "cleared")}
        loaded = [self.sem(f"{name}_loaded{r}") for r in range(U)]
        with ExitStack() as c:
            at = Arena(self.aux2)
            rows = at.take([P, U, D])
            vals = at.take([P, RS, D])
            sel = at.take([P, RS, P])
            psO = [self.ps(f"{name}_po{j}", c) for j in range(4)]
            block = c.enter_context(nc.Block())

            @block.sync
            def _(sp):
                def load(i, r, _):
                    hold(sp, q["scaled"], i * U + r + 1 - U, go)
                    sp.dma_start(rows[:, r, :], self.t_rows[bass.ds(i * U + r, 1), :, :]
                                 .rearrange("o p d -> p (o d)")).then_inc(loaded[r], 16)
                self.flow(sp, [(0, load)])

            @block.tensor
            def _(pe):
                def total(i, r, _):
                    hold(pe, q["sel"], i * U + r + 1, go)
                    hold(pe, q["scaled"], i * U + r + 1, go)
                    hold(pe, q["added"], i * U + r + 1 - 4, go)
                    nc.tensor.matmul(psO[r % 4][:, 0:D], sel[:, r % RS, :], vals[:, r % RS, :],
                                     start=True, stop=True)
                    nc.tensor.matmul(psO[r % 4][:, D:D + H], sel[:, r % RS, :],
                                     self.w8[:, bass.ds(i * U + r, 1), 0:H], start=True, stop=True)\
                        .then_inc(q["summed"], 1)
                self.flow(pe, [(0, total)])

            @block.vector
            def _(dve):
                v = nc.vector
                v.memset(self.acc[:], 0.0).then_inc(q["cleared"], 1)
                dve.wait_ge(q["cleared"], 1)

                def scale(i, r, _):
                    self.select(dve, i, r, q, sel, q["summed"])
                    hold(dve, loaded[r], i * 16 + 16, go)
                    w = self.w8[:, bass.ds(i * U + r, 1), 0:H].rearrange("p o h -> p (o h)")\
                        .rearrange("p (h o) -> p h o", o=1).broadcast_to([P, H, D // H])
                    v.tensor_tensor(vals[:, r % RS, :].rearrange("p (h f) -> p h f", h=H),
                                    rows[:, r, :].rearrange("p (h f) -> p h f", h=H), w, ALU.mult)\
                        .then_inc(q["scaled"], 1)

                def add(i, r, b):
                    self.add_sum(dve, i, r, b, q, psO, D + H)
                add.engine = "DVE"
                self.flow(dve, [(0, scale), (3, add)], blocks_for=add)

    def add_sum(self, dve, i, r, b, q, psO, width):
        hold(dve, q["summed"], i * U + r + 1, self.setup_done)
        hold(dve, q["added"], i * U + r, self.setup_done)
        a = self.acc[:, bass.ds(b, 1), 0:width].rearrange("p o d -> p (o d)")
        self.nc.vector.tensor_tensor(a, a, psO[r % 4][:, 0:width], ALU.add).then_inc(q["added"], 1)

    def gat_output(self):
        nc, s, io = self.nc, self.s, self.io
        nb, H = s.nb, s.heads0
        seq, loaded, lowered, raised, ask, root = (
            self.sem(f"go_{k}") for k in ("seq", "loaded", "lowered", "raised", "ask", "root"))
        with ExitStack() as c:
            bias = self.sb("gat_bias", [P, D], F32, c)
            den = self.sb("gat_den", [P, nb, H], F32, c)
            sums, rstd = self.sb("sums", [P, nb], F32, c), self.sb("rstd", [P, nb], F32, c)
            block = c.enter_context(nc.Block())
            neg = self.aux2[:, :, 0:D]

            @block.sync
            def _(sp):
                sp.dma_start(bias[:], self.bcast_row(io["gat_bias"], D)).then_inc(loaded, 16)

            @block.scalar
            def _(act):
                act.wait_ge(lowered, 1)
                nc.scalar.activation(neg, neg, ACT.Exp).then_inc(raised, 1)
                self.norm_scalar(act, sums, rstd, ask, root)

            @block.vector
            def _(dve):
                v = nc.vector
                do = Chain(dve, seq)
                do(v.tensor_scalar(den[:], self.acc[:, :, D:D + H], 1e-16, None, ALU.add))
                do(v.reciprocal(den[:], den[:]))
                for h in range(H):
                    a = self.acc[:, :, h * (D // H):(h + 1) * (D // H)]
                    do(v.tensor_tensor(a, a, den[:, :, h:h + 1].broadcast_to([P, nb, D // H]), ALU.mult))
                out = self.acc[:, :, 0:D]
                do(v.tensor_tensor(out, out, self.aux[:], ALU.add))
                dve.wait_ge(loaded, 16)
                do(v.tensor_tensor(out, out, bias[:].rearrange("p (o d) -> p o d", o=1)
                                   .broadcast_to([P, nb, D]), ALU.add))
                v.tensor_scalar(neg, out, 0.0, None, ALU.min).then_inc(lowered, 1)
                do(v.tensor_scalar(out, out, 0.0, -1.0, ALU.max, ALU.add))
                dve.wait_ge(raised, 1)
                do(v.tensor_tensor(out, out, neg, ALU.add))
                do(v.tensor_tensor(self.x[:], self.x[:], out, ALU.add))
                self.norm_vector(dve, do, sums, rstd, ask, root)

    def keep_h(self):
        sent = self.sem("kh_sent")
        with self.nc.Block() as block:
            @block.sync
            def _(sp):
                sp.dma_start(self.t_h.rearrange("(b p) d -> p b d", p=P), self.hn[:]).then_inc(sent, 16)
                sp.wait_ge(sent, 16)

    def gather_sum(self, name, table, source, kinds=False, weight=None):
        nc, s, go = self.nc, self.s, self.setup_done
        R = s.rels
        q = {k: self.sem(f"{name}_{k}") for k in
             ("idx", "sel", "summed", "added", "cleared", "onehot", "same", "ahead")}
        gathered = [self.sem(f"{name}_gathered{r}") for r in range(U)]
        landed = [self.sem(f"{name}_landed{h}") for h in range(2)]
        width = D + R if kinds else D
        with ExitStack() as c:
            at = Arena(self.aux)
            rows = at.take([P, U, D])
            idx = at.take([P, U], I32)
            sel = at.take([P, RS, P])
            hot = at.take([P, RS, 8])
            same = at.take([P, 2, P])
            lower = at.take([P, P])
            srcrow = at.take([P, 2, HALF * P])
            psO = [self.ps(f"{name}_po{j}", c) for j in range(4)]
            block = c.enter_context(nc.Block())

            @block.gpsimd
            def _(pool):
                def gather(i, r, _):
                    hold(pool, q["idx"], i * U + r + 1)
                    hold(pool, q["summed"], i * U + r + 1 - U)
                    clear_ahead(pool, self.issued)
                    nc.gpsimd.indirect_dma_start(rows[:, r, :], None, table,
                                                 bass.IndirectOffsetOnAxis(idx[:, r:r + 1], 0))\
                        .then_inc(gathered[r], 16)
                self.flow(pool, [(0, gather)])

            if kinds:
                @block.sync
                def _(sp):
                    def sources(i, r, _):
                        self.load_rows(sp, i, r, self.t_srcrow, srcrow, q["same"], landed)
                    self.flow(sp, [(0, sources)])

            @block.tensor
            def _(pe):
                def total(i, r, _):
                    hold(pe, q["sel"], i * U + r + 1, go)
                    hold(pe, gathered[r], i * 16 + 16, go)
                    hold(pe, q["added"], i * U + r + 1 - 4, go)
                    m = nc.tensor.matmul(psO[r % 4][:, 0:D], sel[:, r % RS, :], rows[:, r, :],
                                         start=True, stop=True)
                    if kinds:
                        hold(pe, q["onehot"], i * U + r + 1, go)
                        m = nc.tensor.matmul(psO[r % 4][:, D:D + R], sel[:, r % RS, :], hot[:, r % RS, 0:R],
                                             start=True, stop=True)
                    m.then_inc(q["summed"], 1)
                self.flow(pe, [(0, total)])

            @block.vector
            def _(dve):
                v = nc.vector
                v.tensor_copy(idx[:], source[:, 0:U]).then_inc(q["idx"], U)
                v.memset(self.acc[:], 0.0).then_inc(q["cleared"], 1)
                if kinds:
                    v.tensor_scalar(lower[:], self.iota[:], self.pidx[:, 0:1], None, ALU.is_lt)\
                        .then_inc(q["cleared"], 1)
                dve.wait_ge(q["cleared"], 2 if kinds else 1)

                def front(i, r, _):
                    self.select(dve, i, r, q, sel, q["summed"], weight)
                    if kinds:
                        col = bass.ds(i * U + r, 1)
                        v.tensor_scalar(hot[:, r % RS, :], self.iota[:, 0:8], self.typ[:, col], None,
                                        ALU.is_equal).then_inc(q["onehot"], 1)
                        if r % HALF == 0:
                            hold(dve, landed[r // HALF], i * 16 + 16, go)
                        hold(dve, q["ahead"], i * U + r - 1, go)
                        v.tensor_scalar(same[:, r % 2, :], srcrow[:, r // HALF, (r % HALF) * P:(r % HALF + 1) * P],
                                        self.srcf[:, col], None, ALU.is_equal).then_inc(q["same"], 1)

                def back(i, r, b):
                    if kinds:
                        hold(dve, q["same"], i * U + r + 1, go)
                        v.scalar_tensor_tensor(same[:, r % 2, :], same[:, r % 2, :], 1.0, lower[:], ALU.mult,
                                               ALU.mult, accum_out=self.ahead[:, bass.ds(i * U + r, 1)])\
                            .then_inc(q["ahead"], 1)

                def add(i, r, b):
                    self.add_sum(dve, i, r, b, q, psO, width)
                    hold(dve, gathered[r], i * 16 + 16, go)
                    self.refill(i, r, idx, source, q["idx"])
                add.engine = "DVE"
                self.flow(dve, [(0, front), (1, back), (2, add)], blocks_for=add)

    def mean_in(self):
        nc, s = self.nc, self.s
        nb, R, S = s.nb, s.rels, s.steps + U
        seq, zeroed, cleared = self.sem("mi_seq"), self.sem("mi_zeroed"), self.sem("mi_cleared")
        with ExitStack() as c:
            at = Arena(self.aux)
            cnt = at.take([P, nb], F32)
            inv = at.take([P, nb], F32)
            dump = at.take([P, 1], F32)
            t = at.take([P, S], F32)
            f = at.take([P, S], F32)
            block = c.enter_context(nc.Block())

            @block.sync
            def _(sp):
                sp.wait_ge(zeroed, 1)
                for k in range(TABLES):
                    sp.dma_start(self.t_out[k][0:nb * P, :].rearrange("(b p) d -> p b d", p=P), self.aux2[:])\
                        .then_inc(cleared, 16)
                    sp.dma_start(self.t_out[k][nb * P:nb * P + P, :], self.aux2[:, 0, :]).then_inc(cleared, 16)
                sp.wait_ge(cleared, 32 * TABLES)

            @block.vector
            def _(dve):
                v = nc.vector
                do = Chain(dve, seq)
                v.memset(self.aux2[:], 0.0).then_inc(zeroed, 1)
                do(v.tensor_scalar(self.inv[:, :, 0:R], self.acc[:, :, D:D + R], 1.0, None, ALU.max))
                do(v.reciprocal(self.inv[:, :, 0:R], self.inv[:, :, 0:R]))
                do(v.memset(self.inv[:, :, R:8], 1.0))
                do(v.tensor_reduce(cnt[:], self.acc[:, :, D:D + R], AX.X, ALU.add))
                do(v.tensor_scalar(self.gin[:], cnt[:], 1.0, None, ALU.min))
                do(v.tensor_scalar(cnt[:], cnt[:], 1.0, None, ALU.max))
                do(v.reciprocal(inv[:], cnt[:]))
                a = self.acc[:, :, 0:D]
                do(v.tensor_tensor(a, a, inv[:].rearrange("p (b o) -> p b o", o=1).broadcast_to([P, nb, D]), ALU.mult))
                do(v.tensor_scalar(dump[:], self.pidx[:], float(nb * P), None, ALU.add))
                do(v.tensor_scalar(f[:, 0:s.steps], self.ahead[:, 0:s.steps], 0.0, None, ALU.is_equal))
                do(v.tensor_scalar(t[:, 0:s.steps], self.srcf[:, 0:s.steps], dump[:, 0:1], None, ALU.subtract))
                do(v.tensor_tensor(t[:, 0:s.steps], t[:, 0:s.steps], f[:, 0:s.steps], ALU.mult))
                do(v.tensor_scalar(t[:, 0:s.steps], t[:, 0:s.steps], dump[:, 0:1], None, ALU.add))
                do(v.tensor_copy(self.sidx[:, 0:s.steps], t[:, 0:s.steps]))
                do(v.tensor_scalar(t[:], self.srcf[:], float(R), None, ALU.mult))
                do(v.tensor_tensor(t[:], t[:], self.typ[:], ALU.add))
                do(v.tensor_copy(self.gidx[:], t[:]))

    def scatter_out(self):
        nc, s, go = self.nc, self.s, self.setup_done
        turns = s.steps // U
        q = {k: self.sem(f"so_{k}") for k in ("idx", "selT", "same", "taken", "vals", "invs", "joined", "sums")}
        scattered = [self.sem(f"so_scattered{r}") for r in range(U)]
        landed = [self.sem(f"so_landed{h}") for h in range(2)]
        landed_src = [self.sem(f"so_landed_src{h}") for h in range(2)]
        with ExitStack() as c:
            at = Arena(self.aux)
            idx = at.take([P, U], I32)
            relrow = at.take([P, 2, HALF * P])
            srcrow = at.take([P, 2, HALF * P])
            selT = at.take([P, RS, P])
            same = at.take([P, RS, P])
            vals = at.take([P, 2, 136])
            sums = at.take([P, U, 136])
            psE = [self.ps(f"so_pe{j}", c) for j in range(4)]
            psC = [self.ps(f"so_pc{j}", c) for j in range(4)]
            block = c.enter_context(nc.Block())

            @block.gpsimd
            def _(pool):
                def scatter(i, r, _):
                    hold(pool, q["idx"], i * U + r + 1)
                    hold(pool, q["sums"], i * U + r + 1)
                    hold(pool, scattered[r], i * 16)
                    clear_ahead(pool, self.issued)
                    nc.gpsimd.indirect_dma_start(self.t_out[r], bass.IndirectOffsetOnAxis(idx[:, r:r + 1], 0),
                                                 sums[:, r, :], None, compute_op=ALU.add)\
                        .then_inc(scattered[r], 16)
                self.flow(pool, [(0, scatter)])
                for r in range(U):
                    pool.wait_ge(scattered[r], 16 * turns)

            @block.sync
            def _(sp):
                def rel(i, r, _):
                    self.load_rows(sp, i, r, self.t_relrow, relrow, q["selT"], landed)
                    self.load_rows(sp, i, r, self.t_srcrow, srcrow, q["same"], landed_src)
                self.flow(sp, [(0, rel)])

            @block.scalar
            def _(act):
                a = nc.scalar

                def taken(i, r, _):
                    hold(act, q["taken"], i * U + r + 1, go)
                    hold(act, q["joined"], i * U + r - 1, go)
                    hold(act, q["invs"], i * U + r - 1, go)
                    a.activation(vals[:, r % 2, :], psE[r % 4][:, 0:136], ACT.Copy).then_inc(q["vals"], 1)

                def joined(i, r, _):
                    hold(act, q["joined"], i * U + r + 1, go)
                    hold(act, scattered[r], i * 16, go)
                    a.activation(sums[:, r, :], psC[r % 4][:, 0:136], ACT.Copy).then_inc(q["sums"], 1)
                self.flow(act, [(0, taken), (1, joined)])

            @block.tensor
            def _(pe):
                def take(i, r, b):
                    hold(pe, q["selT"], i * U + r + 1, go)
                    hold(pe, q["vals"], i * U + r + 1 - 4, go)
                    nc.tensor.matmul(psE[r % 4][:, 0:D], selT[:, r % RS, :],
                                     self.hn[:, bass.ds(b, 1), :], start=True, stop=True)
                    nc.tensor.matmul(psE[r % 4][:, D:D + 8], selT[:, r % RS, :],
                                     self.inv[:, bass.ds(b, 1), :], start=True, stop=True)\
                        .then_inc(q["taken"], 1)
                take.engine = "PE"

                def join(i, r, _):
                    hold(pe, q["vals"], i * U + r + 1, go)
                    hold(pe, q["same"], i * U + r + 1, go)
                    hold(pe, q["sums"], i * U + r + 1 - 4, go)
                    nc.tensor.matmul(psC[r % 4][:, 0:136], same[:, r % RS, :], vals[:, r % 2, :],
                                     start=True, stop=True).then_inc(q["joined"], 1)
                self.flow(pe, [(0, take), (1, join)], blocks_for=take)

            @block.vector
            def _(dve):
                v = nc.vector

                def front(i, r, _):
                    col = bass.ds(i * U + r, 1)
                    self.select_turned(dve, i, r, relrow, landed, selT, q["taken"], q["selT"])
                    if r % HALF == 0:
                        hold(dve, landed_src[r // HALF], i * 16 + 16, go)
                    hold(dve, q["joined"], i * U + r + 1 - RS, go)
                    v.tensor_scalar(same[:, r % RS, :], srcrow[:, r // HALF, (r % HALF) * P:(r % HALF + 1) * P],
                                    self.srcf[:, col], None, ALU.is_equal).then_inc(q["same"], 1)

                def back(i, r, _):
                    col = bass.ds(i * U + r, 1)
                    hold(dve, scattered[r], i * 16, go)
                    v.tensor_copy(idx[:, r:r + 1], self.sidx[:, col]).then_inc(q["idx"], 1)
                    hold(dve, q["vals"], i * U + r + 1, go)
                    v.tensor_copy(self.w8[:, col, :].rearrange("p o h -> p (o h)"),
                                  vals[:, r % 2, D:D + 8]).then_inc(q["invs"], 1)
                self.flow(dve, [(0, front), (2, back)])

    def mean_out(self):
        nc, s = self.nc, self.s
        nb, R, S = s.nb, s.rels, s.steps
        half = nb // 2
        seq, weighed = self.sem("mo_seq"), self.sem("mo_weighed")
        loaded = [self.sem(f"mo_loaded{j}") for j in range(2)]
        added = [self.sem(f"mo_added{j}") for j in range(2)]
        buf = self.wts[:, 0:nb * 136].rearrange("p (b d) -> p b d", d=136)
        with ExitStack() as c:
            at = Arena(self.aux)
            hot = at.take([P, S], F32)
            cnt = at.take([P, nb], F32)
            block = c.enter_context(nc.Block())

            @block.sync
            def _(sp):
                sp.wait_ge(weighed, 1)
                for k in range(TABLES):
                    for j in range(2):
                        if k:
                            sp.wait_ge(added[j], k)
                        sp.dma_start(buf[:, j * half:(j + 1) * half, :],
                                     self.t_out[k][j * half * P:(j + 1) * half * P, :]
                                     .rearrange("(b p) d -> p b d", p=P)).then_inc(loaded[j], 16)

            @block.vector
            def _(dve):
                v = nc.vector
                do = Chain(dve, seq)
                do(v.memset(self.w2[:], 0.0))
                for r in range(R):
                    do(v.tensor_scalar(hot[:], self.typ[:, 0:S], float(r), None, ALU.is_equal))
                    do(v.tensor_tensor(hot[:], hot[:], self.w8[:, :, r:r + 1].rearrange("p s o -> p (s o)"), ALU.mult))
                    do(v.tensor_tensor(self.w2[:, 0:S], self.w2[:, 0:S], hot[:], ALU.add))
                dve.sem_inc(weighed, 1)
                for k in range(TABLES):
                    for j in range(2):
                        a = self.aux2[:, j * half:(j + 1) * half, :]
                        dve.wait_ge(loaded[j], 16 * (k + 1))
                        if k:
                            dve.wait_ge(added[j], k)
                        v.tensor_tensor(a, a, buf[:, j * half:(j + 1) * half, :], ALU.add).then_inc(added[j], 1)
                for j in range(2):
                    dve.wait_ge(added[j], TABLES)
                flag = self.aux2[:, :, 135:136].rearrange("p b o -> p (b o)")
                do(v.tensor_scalar(self.gout[:], flag, 1.0, None, ALU.min))
                do(v.tensor_scalar(cnt[:], flag, 1.0, None, ALU.max))
                do(v.reciprocal(cnt[:], cnt[:]))
                a = self.aux2[:, :, 0:D]
                do(v.tensor_tensor(a, a, cnt[:].rearrange("p (b o) -> p b o", o=1).broadcast_to([P, nb, D]), ALU.mult))

    def gru(self):
        nc, s, io, go = self.nc, self.s, self.io, self.setup_done
        q = self.product_sems("gru")
        arrays = [self.aux, self.aux2, self.hn]
        blank = self.sem("gru_blank")
        biased = {k: self.sem(f"gru_{k}") for k in ("biased", "gates", "asked", "n")}
        OPS = 5
        with ExitStack() as c:
            at = Arena(self.acc)
            w, stage, turned, psT, psO = self.product_memory("gru", c, 3, 4 * D, at)
            bi = at.take([P, 4 * D], F32)
            bh = at.take([P, 4 * D], F32)
            g = at.take([P, 2, 4 * D], F32)
            rz = at.take([P, 2, 2 * D], F32)
            t = at.take([P, 2, D], F32)
            n = at.take([P, 2, D], F32)
            block = c.enter_context(nc.Block())

            @block.sync
            def _(sp):
                wi, wh = io["w_ih_t"], io["w_hh_t"]
                sp.wait_ge(blank, 1)
                for k in range(2):
                    sp.dma_start(w[:, k, 0:3 * D], wi[k * D:(k + 1) * D, :]).then_inc(q["loaded"], 16)
                sp.dma_start(w[:, 2, 0:2 * D], wh[:, 0:2 * D]).then_inc(q["loaded"], 16)
                sp.dma_start(w[:, 2, 3 * D:4 * D], wh[:, 2 * D:3 * D]).then_inc(q["loaded"], 16)
                sp.dma_start(bi[:, 0:3 * D], self.bcast_row(io["b_ih"], 3 * D)).then_inc(q["loaded"], 16)
                sp.dma_start(bh[:, 0:2 * D], self.bcast_row(io["b_hh"][0:2 * D], 2 * D)).then_inc(q["loaded"], 16)
                sp.dma_start(bh[:, 3 * D:4 * D], self.bcast_row(io["b_hh"][2 * D:3 * D], D)).then_inc(q["loaded"], 16)

            @block.scalar
            def _(act):
                a = nc.scalar
                def turn(i):
                    self.product_scalar(act, i, q, arrays, stage, turned, psT)
                    for j in range(2):
                        hold(act, biased["biased"], 2 * i + j + 1, go)
                        a.activation(rz[:, j, :], g[:, j, 0:2 * D], ACT.Sigmoid).then_inc(biased["gates"], 1)
                    for j in range(2):
                        hold(act, biased["asked"], 2 * i + j + 1, go)
                        a.activation(n[:, j, :], t[:, j, :], ACT.Tanh).then_inc(biased["n"], 1)
                repeat(act, s.nb // 2, turn)

            @block.tensor
            def _(pe):
                self.product_tensor(pe, q, w, 4 * D, stage, turned, psT, psO, 7, None)

            @block.vector
            def _(dve):
                v = nc.vector
                do = Chain(dve, q["seq"])
                do(v.memset(bi[:], 0.0))
                do(v.memset(bh[:], 0.0))
                v.memset(w[:], 0.0).then_inc(blank, 1)
                dve.wait_ge(q["loaded"], 16 * 7)
                do(v.tensor_tensor(bi[:], bi[:], bh[:], ALU.add))
                def turn(i):
                    for j in range(2):
                        hold(dve, q["product"], 2 * i + j + 1, go)
                        v.tensor_tensor(g[:, j, :], psO[j][:], bi[:], ALU.add).then_inc(biased["biased"], 1)
                    for j in range(2):
                        hold(dve, biased["gates"], 2 * i + j + 1, go)
                        then = Turn(dve, q["seq"], (2 * i + j) * OPS + 3, go)
                        then(v.tensor_tensor(t[:, j, :], rz[:, j, 0:D], g[:, j, 3 * D:4 * D], ALU.mult))
                        v.tensor_tensor(t[:, j, :], t[:, j, :], g[:, j, 2 * D:3 * D], ALU.add)\
                            .then_inc(biased["asked"], 1)
                        hold(dve, biased["n"], 2 * i + j + 1, go)
                        one = bass.ds(2 * i + j, 1)
                        h = self.hn[:, one, :].rearrange("p o d -> p (o d)")
                        x = self.x[:, one, :].rearrange("p o d -> p (o d)")
                        then(v.tensor_tensor(t[:, j, :], h, n[:, j, :], ALU.subtract))
                        then(v.tensor_tensor(t[:, j, :], t[:, j, :], rz[:, j, D:2 * D], ALU.mult))
                        then(v.tensor_tensor(t[:, j, :], t[:, j, :], n[:, j, :], ALU.add))
                        then(v.tensor_tensor(x, x, t[:, j, :], ALU.add))
                        assert then.n == OPS
                        dve.sem_inc(q["finished"], 1)
                repeat(dve, s.nb // 2, turn)

    def norm(self, name, plus=None):
        nc, s = self.nc, self.s
        seq, ask, root = (self.sem(f"{name}_{k}") for k in ("seq", "ask", "root"))
        with ExitStack() as c:
            sums, rstd = self.sb("sums", [P, s.nb], F32, c), self.sb("rstd", [P, s.nb], F32, c)
            block = c.enter_context(nc.Block())

            @block.scalar
            def _(act):
                self.norm_scalar(act, sums, rstd, ask, root)

            @block.vector
            def _(dve):
                do = Chain(dve, seq)
                if plus is not None:
                    do(nc.vector.tensor_tensor(self.x[:], self.x[:], plus, ALU.add))
                self.norm_vector(dve, do, sums, rstd, ask, root)

    def root_nodes(self):
        nc, s, io, go = self.nc, self.s, self.io, self.setup_done
        K, W = s.node_types, s.node_types * D
        q = self.product_sems("root")
        OPS = 1 + K
        with ExitStack() as c:
            w, stage, turned, psT, psO = self.product_memory("root", c, 1, W)
            b = self.sb("root_bias", [P, W], F32, c)
            g = self.sb("root_g", [P, 2, W], F32, c)
            typ = self.sb("node_type", [P, s.nb], I32, c)
            own = self.sb("own_type", [P, K, s.nb], F32, c)
            block = c.enter_context(nc.Block())

            @block.sync
            def _(sp):
                sp.dma_start(w[:, 0, :], io["root_w_t"]).then_inc(q["loaded"], 16)
                sp.dma_start(b[:], self.bcast_row(io["root_b"], W)).then_inc(q["loaded"], 16)
                sp.dma_start(typ[:], io["node_type_t"]).then_inc(q["loaded"], 16)

            @block.scalar
            def _(act):
                def turn(i):
                    self.product_scalar(act, i, q, [self.hn], stage, turned, psT)
                repeat(act, s.nb // 2, turn)

            @block.tensor
            def _(pe):
                self.product_tensor(pe, q, w, W, stage, turned, psT, psO, 3, None)

            @block.vector
            def _(dve):
                v = nc.vector
                do = Chain(dve, q["seq"])
                dve.wait_ge(q["loaded"], 48)
                for k in range(K):
                    do(v.tensor_scalar(own[:, k, :], typ[:], float(k), None, ALU.is_equal))
                def turn(i):
                    for j in range(2):
                        at = bass.ds(2 * i + j, 1)
                        x = self.x[:, at, :].rearrange("p o d -> p (o d)")
                        hold(dve, q["product"], 2 * i + j + 1, go)
                        then = Turn(dve, q["seq"], (2 * i + j) * OPS + K, go)
                        then(v.tensor_tensor(g[:, j, :], psO[j][:, 0:W], b[:], ALU.add))
                        for k in range(K):
                            then(v.scalar_tensor_tensor(x, g[:, j, k * D:(k + 1) * D], own[:, k, at], x,
                                                        ALU.mult, ALU.add))
                        assert then.n == OPS
                        dve.sem_inc(q["finished"], 1)
                repeat(dve, s.nb // 2, turn)

    def edge_rows(self):
        nc, s, io, go = self.nc, self.s, self.io, self.setup_done
        H, turns = s.heads3, s.steps // U
        B = HALF
        q = {k: self.sem(f"er_{k}") for k in ("idx", "selT", "projected", "target", "z", "capped",
                                              "inverse", "weighed", "part", "part2", "reduced", "logits", "consts", "att")}
        gathered = [self.sem(f"er_gathered{r}") for r in range(U)]
        stored = [self.sem(f"er_stored{r}") for r in range(U)]
        loaded = [self.sem(f"er_loaded{r}") for r in range(U)]
        landed = [self.sem(f"er_landed{h}") for h in range(2)]
        with ExitStack() as c:
            at = Arena(self.hn, self.acc, self.aux2)
            rows = at.take([P, U, D])
            att = at.take([P, U, D])
            ea = at.take([P, U, D])
            idx = at.take([P, U], I32)
            relrow = at.take([P, 2, B * P])
            selT = at.take([P, RS, P])
            z = at.take([P, 2, B * D])
            u = at.take([P, 2, B * D])
            we = at.take([P, D])
            attn = at.take([P, D // H])
            attn4 = at.take([P, B * D])
            attn_b = at.take([P, 1])
            psA = [self.ps(f"er_pa{j}", c) for j in range(4)]
            psE = [self.ps(f"er_pe{j}", c) for j in range(4)]
            block = c.enter_context(nc.Block())

            @block.gpsimd
            def _(pool):
                def gather(i, r, _):
                    hold(pool, q["idx"], i * U + r + 1)
                    hold(pool, q["att"], i * U + r + 1 - U)
                    clear_ahead(pool, self.issued)
                    nc.gpsimd.indirect_dma_start(rows[:, r, :], None, self.t_sent,
                                                 bass.IndirectOffsetOnAxis(idx[:, r:r + 1], 0))\
                        .then_inc(gathered[r], 16)
                self.flow(pool, [(0, gather)])

            @block.sync
            def _(sp):
                sp.dma_start(we[:], io["We"]).then_inc(q["consts"], 16)
                sp.dma_start(attn[:], self.bcast_row(io["attn_w"], D // H)).then_inc(q["consts"], 16)
                sp.dma_start(attn_b[:], self.bcast_row(io["attn_b"], 1)).then_inc(q["consts"], 16)

                def load(i, r, t):
                    self.load_rows(sp, i, r, self.t_relrow, relrow, q["selT"], landed)
                    hold(sp, q["projected"], i * U + r + 1 - U, go)
                    sp.dma_start(ea[:, r, :], io["edge_t"][bass.ds(t, 1), :, :]
                                 .rearrange("o p d -> p (o d)")).then_inc(loaded[r], 16)
                load.engine = "SP"

                def send(i, r, _):
                    hold(sp, q["att"], i * U + r + 1, go)
                    sp.dma_start(self.t_rows[bass.ds(i * U + r, 1), :, :].rearrange("o p d -> p (o d)"),
                                 att[:, r, :]).then_inc(stored[r], 16)
                self.flow(sp, [(0, load), (6, send)], tiles_for=load)
                for r in range(U):
                    sp.wait_ge(stored[r], 16 * turns)

            @block.scalar
            def _(act):
                def inverse(i, r, _):
                    if r % B:
                        return
                    k = r // B
                    uk = u[:, k, :]
                    hold(act, q["capped"], 2 * i + k + 1, go)
                    then = Turn(act, q["part"], (2 * i + k) * 3, go)
                    then(nc.scalar.activation(uk, uk, ACT.Exp))
                    then(nc.scalar.activation(uk, uk, ACT.Square, bias=1.0))
                    then(nc.scalar.activation(uk, uk, ACT.Ln, bias=1.0))
                    nc.scalar.activation(uk, uk, ACT.Exp, scale=-1.0).then_inc(q["inverse"], 1)
                self.flow(act, [(0, inverse)])

            @block.tensor
            def _(pe):
                pe.wait_ge(q["consts"], 48)

                def project(i, r, _):
                    hold(pe, loaded[r], i * 16 + 16, go)
                    hold(pe, q["att"], i * U + r + 1 - 4, go)
                    nc.tensor.matmul(psA[r % 4][:, 0:D], ea[:, r, :], we[:], start=True, stop=True)\
                        .then_inc(q["projected"], 1)

                def target(i, r, b):
                    hold(pe, q["selT"], i * U + r + 1, go)
                    hold(pe, q["z"], i * U + r + 1 - 4, go)
                    nc.tensor.matmul(psE[r % 4][:, 0:D], selT[:, r % RS, :],
                                     self.aux[:, bass.ds(b, 1), :], start=True, stop=True)\
                        .then_inc(q["target"], 1)
                target.engine = "PE"
                self.flow(pe, [(0, project), (0, target)], blocks_for=target)

            @block.vector
            def _(dve):
                v = nc.vector
                v.tensor_copy(idx[:], self.src[:, 0:U]).then_inc(q["idx"], U)
                dve.wait_ge(q["consts"], 48)
                v.tensor_copy(attn4[:].rearrange("p (b f) -> p b f", f=D // H),
                              attn[:].rearrange("p (o f) -> p o f", o=1).broadcast_to([P, B * H, D // H]))\
                    .then_inc(q["consts"], 1)
                dve.wait_ge(q["consts"], 49)

                def select(i, r, _):
                    self.select_turned(dve, i, r, relrow, landed, selT, q["target"], q["selT"])

                def add(i, r, _):
                    hold(dve, gathered[r], i * 16 + 16, go)
                    self.refill(i, r, idx, self.src, q["idx"])
                    hold(dve, q["projected"], i * U + r + 1, go)
                    hold(dve, stored[r], i * 16, go)
                    v.tensor_tensor(att[:, r, :], rows[:, r, :], psA[r % 4][:, 0:D], ALU.add)\
                        .then_inc(q["att"], 1)

                def plus(i, r, _):
                    hold(dve, q["target"], i * U + r + 1, go)
                    hold(dve, q["att"], i * U + r + 1, go)
                    if r % B == 0:
                        hold(dve, q["reduced"], 2 * i + r // B - 1, go)
                    v.tensor_tensor(z[:, r // B, (r % B) * D:(r % B + 1) * D], att[:, r, :],
                                    psE[r % 4][:, 0:D], ALU.add).then_inc(q["z"], 1)

                def cap(i, r, _):
                    if r % B == B - 1:
                        k = r // B
                        hold(dve, q["z"], i * U + r + 1, go)
                        v.tensor_scalar(u[:, k, :], z[:, k, :], 20.0, None, ALU.min).then_inc(q["capped"], 1)
                        v.tensor_tensor(z[:, k, :], z[:, k, :], attn4[:], ALU.mult).then_inc(q["weighed"], 1)

                def mish(i, r, _):
                    if r % B:
                        return
                    k = r // B
                    hold(dve, q["inverse"], 2 * i + k + 1, go)
                    hold(dve, q["weighed"], 2 * i + k + 1, go)
                    v.scalar_tensor_tensor(z[:, k, :], u[:, k, :], 0.5, z[:, k, :], ALU.subtract, ALU.mult)\
                        .then_inc(q["part2"], 1)
                    hold(dve, q["part2"], 2 * i + k + 1, go)
                    v.tensor_reduce(self.w8[:, bass.ds(i * U + k * B, B), 0:H],
                                    z[:, k, :].rearrange("p (b h f) -> p b h f", h=H, f=D // H),
                                    AX.X, ALU.add).then_inc(q["reduced"], 1)
                self.flow(dve, [(0, select), (2, add), (2, plus), (2, cap), (U, mish)])
                dve.wait_ge(q["reduced"], 2 * turns)
                v.tensor_scalar(self.w8[:, :, 0:H], self.w8[:, :, 0:H], -2.0, attn_b[:, 0:1], ALU.mult, ALU.add)\
                    .then_inc(q["logits"], 1)
                dve.wait_ge(q["logits"], 1)

    def merge_logits(self):
        nc, s, go = self.nc, self.s, self.setup_done
        T, NF, S, H = s.tiles, s.blocks - 1, s.steps, s.heads3
        seq, moved = self.sem("ml_seq"), self.sem("ml_moved")
        with nc.Block() as block:
            @block.vector
            def _(dve):
                v = nc.vector
                do = Chain(dve, seq)
                w = self.w8[:, :, 0:H]
                do(v.tensor_tensor(w, w, self.mask[:, 0:S].rearrange("p (s o) -> p s o", o=1)
                                   .broadcast_to([P, S, H]), ALU.mult))
                def turn(k):
                    t = dve.value_load(self.til[0:1, bass.ds(k + (T + U), 1)], min_val=0, max_val=T - 1)
                    a = self.w8[:, bass.ds(t, 1), 0:H]
                    hold(dve, moved, k, go)
                    v.tensor_tensor(a, a, self.w8[:, bass.ds(k + T, 1), 0:H], ALU.add).then_inc(moved, 1)
                repeat(dve, NF, turn)
                dve.wait_ge(moved, NF)

    def edge_softmax(self):
        nc, s, go = self.nc, self.s, self.setup_done
        T, H, C, CT, ST = s.tiles, s.heads3, SCAN_CHUNKS, s.ctiles, s.stiles
        L, NF = CT * P, s.blocks - 1
        per = P // H
        groups = -(-ST // per)
        names = ("seq", "compact", "turned", "copied", "written", "loaded", "rows", "rowcopy", "carry",
                 "carried", "back", "backin", "backturned", "sub", "exped", "moved")
        q = {k: self.sem(f"es_{k}") for k in names}
        stage_free = [self.sem(f"es_stage{j}") for j in range(2)]
        arrived = [self.sem(f"es_arrived{j}") for j in range(2)]
        flat = lambda a: a[:].rearrange("p b d -> p (b d)")
        accf, auxf, aux2f, hnf = flat(self.acc), flat(self.aux), flat(self.aux2), flat(self.hn)
        assert 2 * L <= self.s.nb * 136 and L <= self.s.nb * D and ST * H <= L and H * C == P
        logits = accf[:, 0:ST * H]
        run = accf[:, L:2 * L]
        seqd = aux2f[:, 0:L]
        here, other = aux2f[:, L:2 * L].bitcast(I32), hnf[:, 0:L].bitcast(I32)
        reset = auxf[:, 0:L]
        with ExitStack() as c:
            stage = self.sb("es_stage", [P, 2, P], F32, c)
            edge = self.sb("es_edge", [P, 2], F32, c)
            row = self.sb("es_row", [1, 2 * P], F32, c)
            chain = self.sb("es_chain", [1, H * (C + 1)], F32, c)
            first = self.sb("es_first", [1, P], F32, c)
            start = self.sb("es_start", [P, 1], F32, c)
            ps = [self.ps(f"es_ps{j}", c) for j in range(2)]
            psR = self.ps("es_pr", c)
            psB = [self.ps(f"es_pb{j}", c) for j in range(2)]
            block = c.enter_context(nc.Block())
            dseq = io_seq = self.io["dst_seq"]
            tseq = self.t_seq.rearrange("t h e -> (t h) e")
            tmax = self.t_max.rearrange("t h e -> (t h) e")

            def chunked(t, h):
                return t[:, h, :].rearrange("(c j) e -> c j e", c=C)

            @block.sync
            def _(sp):
                for h in range(H):
                    for off, dst in ((1, here), (0, other)):
                        sp.dma_start(dst[h * C:(h + 1) * C, :], dseq[off:off + C * L].rearrange("(c l) -> c l", c=C))\
                            .then_inc(q["loaded"], 16)
                for g in range(groups):
                    sp.wait_ge(q["copied"], g + 1)
                    sp.dma_start(tseq[g * P:(g + 1) * P, :], stage[:, g % 2, :]).then_inc(stage_free[g % 2], 16)
                for j in range(2):
                    sp.wait_ge(stage_free[j], 16 * len(range(j, groups, 2)))
                for h in range(H):
                    sp.dma_start(seqd[h * C:(h + 1) * C, :].rearrange("p (j e) -> p j e", e=P), chunked(self.t_seq, h))\
                        .then_inc(q["written"], 16)
                sp.wait_ge(q["carry"], 5)
                for h in range(H):
                    sp.dma_start(other[h * C:(h + 1) * C, :], dseq[2:2 + C * L].rearrange("(c l) -> c l", c=C))\
                        .then_inc(q["loaded"], 16)
                sp.wait_ge(q["carry"], 10)
                for h in range(H):
                    sp.dma_start(chunked(self.t_max, h), run[h * C:(h + 1) * C, :].rearrange("p (j e) -> p j e", e=P))\
                        .then_inc(q["back"], 16)
                sp.wait_ge(q["back"], 16 * H)
                for g in range(groups):
                    if g >= 2:
                        sp.wait_ge(q["backturned"], g - 1)
                    sp.dma_start(stage[:, g % 2, :], tmax[g * P:(g + 1) * P, :]).then_inc(arrived[g % 2], 16)

            @block.tensor
            def _(pe):
                pe.wait_ge(q["compact"], 1)
                for g in range(groups):
                    if g >= 2:
                        pe.wait_ge(q["copied"], g - 1)
                    nc.tensor.transpose(ps[g % 2][:, 0:P], logits[:, g * P:(g + 1) * P], self.ident[:])\
                        .then_inc(q["turned"], 1)
                for d in range(2):
                    pe.wait_ge(q["carry"], 5 * d + 1)
                    for k in range(2):
                        nc.tensor.transpose(psR[0:1, k * P:(k + 1) * P], edge[:, k:k + 1], self.ident[:])\
                            .then_inc(q["rows"], 1)
                    pe.wait_ge(q["carry"], 5 * d + 4)
                    nc.tensor.matmul(psR[:, 2 * P:2 * P + 1], first[:], self.ones[0:1, 0:1], start=True, stop=True)\
                        .then_inc(q["rows"], 1)
                for g in range(groups):
                    pe.wait_ge(arrived[g % 2], 16 * (g // 2 + 1))
                    if g >= 2:
                        pe.wait_ge(q["sub"], g - 1)
                    nc.tensor.transpose(psB[g % 2][:, 0:P], stage[:, g % 2, :], self.ident[:])\
                        .then_inc(q["backturned"], 1)

            @block.scalar
            def _(act):
                for g in range(groups):
                    act.wait_ge(q["turned"], g + 1)
                    if g >= 2:
                        act.wait_ge(stage_free[g % 2], 16 * (g // 2))
                    nc.scalar.activation(stage[:, g % 2, :], ps[g % 2][:, 0:P], ACT.Copy).then_inc(q["copied"], 1)
                act.wait_ge(q["sub"], groups)
                nc.scalar.activation(self.w8[:, 0:T, 0:H], self.w8[:, 0:T, 0:H], ACT.Exp).then_inc(q["exped"], 1)

            @block.vector
            def _(dve):
                v = nc.vector
                do = Chain(dve, q["seq"])
                do(v.memset(logits, 0.0))
                v.tensor_copy(logits[:, 0:T * H].rearrange("p (t h) -> p t h", h=H), self.w8[:, 0:T, 0:H])\
                    .then_inc(q["compact"], 1)
                dve.wait_ge(q["loaded"], 32 * H)
                for d in range(2):
                    if d == 1:
                        dve.wait_ge(q["loaded"], 48 * H)
                    do(v.tensor_tensor(reset, here, other, ALU.not_equal))
                    do(v.tensor_scalar(reset, reset, -BIG, None, ALU.mult))
                    if d == 0:
                        dve.wait_ge(q["written"], 16 * H)
                    way = (lambda a: a) if d == 0 else (lambda a: a[:, ::-1])
                    data = seqd if d == 0 else run
                    out = run if d == 0 else seqd
                    do(v.tensor_tensor_scan(way(out), way(reset), way(data), -BIG, ALU.add, ALU.max))
                    end = L - 1 if d == 0 else 0
                    do(v.tensor_copy(edge[:, 0:1], out[:, end:end + 1]))
                    do(v.memset(chain[:], -BIG))
                    v.tensor_reduce(edge[:, 1:2], reset, AX.X, ALU.min).then_inc(q["carry"], 1)
                    dve.wait_ge(q["rows"], 3 * d + 2)
                    v.tensor_copy(row[:], psR[0:1, 0:2 * P]).then_inc(q["carry"], 1)
                    dve.wait_ge(q["carry"], 5 * d + 2)
                    for h in range(H):
                        a = row[0:1, h * C:(h + 1) * C]
                        r = row[0:1, P + h * C:P + (h + 1) * C]
                        at = h * (C + 1)
                        if d == 0:
                            o = chain[0:1, at + 1:at + 1 + C]
                        else:
                            a, r, o = a[:, ::-1], r[:, ::-1], chain[0:1, at:at + C][:, ::-1]
                        do(v.tensor_tensor_scan(o, r, a, -BIG, ALU.add, ALU.max))
                    dve.sem_inc(q["carry"], 1)
                    off = 0 if d == 0 else 1
                    v.tensor_copy(first[:].rearrange("p (h c) -> p h c", h=H),
                                  chain[:].rearrange("p (h c) -> p h c", h=H)[:, :, off:off + C])\
                        .then_inc(q["carry"], 1)
                    dve.wait_ge(q["rows"], 3 * d + 3)
                    do(v.tensor_copy(start[:], psR[:, 2 * P:2 * P + 1]))
                    final = run
                    v.tensor_tensor_scan(way(final), way(reset), way(data), start[:, 0:1], ALU.add, ALU.max)\
                        .then_inc(q["carry"], 1)
                    dve.wait_ge(q["carry"], 5 * d + 5)
                for g in range(groups):
                    n = min(per, T - g * per)
                    dve.wait_ge(q["backturned"], g + 1)
                    if n > 0:
                        w = self.w8[:, g * per:g * per + n, 0:H]
                        m = v.tensor_tensor(w, w, psB[g % 2][:, 0:n * H].rearrange("p (t h) -> p t h", h=H), ALU.subtract)
                    else:
                        m = v.memset(edge[:], 0.0)
                    m.then_inc(q["sub"], 1)
                dve.wait_ge(q["exped"], 1)
                def turn(k):
                    t = dve.value_load(self.til[0:1, bass.ds(k + (T + U), 1)], min_val=0, max_val=T - 1)
                    v.tensor_copy(self.w8[:, bass.ds(k + T, 1), 0:H], self.w8[:, bass.ds(t, 1), 0:H])\
                        .then_inc(q["moved"], 1)
                repeat(dve, NF, turn)
                dve.wait_ge(q["moved"], NF)

    def output(self):
        nc, s, io = self.nc, self.s, self.io
        nb, H = s.nb, s.heads3
        seq, done, sent = self.sem("ou_seq"), self.sem("ou_done"), self.sem("ou_sent")
        with ExitStack() as c:
            den = self.sb("ou_den", [P, nb, H], F32, c)
            block = c.enter_context(nc.Block())

            @block.vector
            def _(dve):
                v = nc.vector
                do = Chain(dve, seq)
                do(v.tensor_scalar(den[:], self.acc[:, :, D:D + H], 1e-30, None, ALU.max))
                do(v.reciprocal(den[:], den[:]))
                for h in range(H):
                    a = self.acc[:, :, h * (D // H):(h + 1) * (D // H)]
                    do(v.tensor_tensor(a, a, den[:, :, h:h + 1].broadcast_to([P, nb, D // H]), ALU.mult))
                v.tensor_tensor(self.x[:], self.x[:], self.acc[:, :, 0:D], ALU.add).then_inc(done, 1)

            @block.sync
            def _(sp):
                sp.wait_ge(done, 1)
                sp.dma_start(io["out"].rearrange("(b p) d -> p b d", p=P), self.x[:]).then_inc(sent, 16)
                sp.wait_ge(sent, 16)

    def build(self):
        s, io = self.s, self.io
        with self.ctx:
            self.allocate()
            self.prepare()
            self.end_phase()
            self.gat_nodes()
            self.end_phase()
            self.gat_gather()
            self.end_phase()
            self.gat_softmax()
            self.end_phase()
            self.weighted_sum("gat_sum", s.heads0)
            self.end_phase()
            self.gat_output()
            self.end_phase()
            self.keep_h()
            self.end_phase()
            self.gather_sum("in_sum", self.t_h, self.src, kinds=True)
            self.end_phase()
            self.mean_in()
            self.end_phase()
            self.scatter_out()
            self.end_phase()
            self.mean_out()
            self.end_phase()
            self.plain_product("a_in", [self.acc], [io["W_in_t"]], [io["b_in"]], D, out=self.aux, gate=self.gin)
            self.end_phase()
            self.plain_product("a_out", [self.aux2], [io["W_out_t"]], [io["b_out"]], D, out=self.aux2, gate=self.gout)
            self.end_phase()
            self.gru()
            self.end_phase()
            self.norm("norm2")
            self.end_phase()
            W = s.rels * D // 2
            for k in range(2):
                self.plain_product(f"rel{k}", [self.hn], [io["rel_w_t"][:, k * W:(k + 1) * W]], [], W,
                                   table=self.t_rel.rearrange("n r d -> n (r d)"), cols=k * W)
                self.end_phase()
            self.root_nodes()
            self.end_phase()
            self.gather_sum("rel_sum", self.t_rel.rearrange("n r d -> (n r) d"), self.gidx, weight=self.w2)
            self.end_phase()
            self.norm("norm3", plus=self.acc[:, :, 0:D])
            self.end_phase()
            self.plain_product("sent", [self.hn], [io["Ws"]], [io["Ws_b"]], D, table=self.t_sent,
                               bias2=io["We_b"])
            self.end_phase()
            self.plain_product("recv", [self.hn], [io["Wr"]], [io["Wr_b"]], D, out=self.aux)
            self.end_phase()
            self.edge_rows()
            self.end_phase()
            self.merge_logits()
            self.end_phase()
            self.edge_softmax()
            self.end_phase()
            self.weighted_sum("att_sum", s.heads3)
            self.end_phase()
            self.output()
            self.end_phase()



def kernel(x, src, dst, edge_attr_128, edge_type_7, node_type_4, **w):
    import concourse.bacc as bacc
    from concourse.bass_utils import run_bass_kernel_spmd

    x, src, dst, ea, et, nt = (np.asarray(a) for a in (x, src, dst, edge_attr_128, edge_type_7, node_type_4))
    w = {k: np.asarray(a) for k, a in w.items()}
    n, e = x.shape[0], src.shape[0]
    s = Shape(n, e, w["L0_gnn_a_src"].shape[1], w["L3_gnn_Ws_k"].shape[1], w["L2_gnn_rel_w"].shape[0],
              w["L2_gnn_root_w"].shape[0])
    far = (s.blocks + 1) * P

    def by_tile(a, fill):
        return np.ascontiguousarray(np.pad(a, (0, s.tiles * P - e), constant_values=fill).reshape(s.tiles, P).T)

    flat = lambda a: np.ascontiguousarray(a.reshape(-1))
    mat = lambda a: np.ascontiguousarray(a.reshape(D, -1))
    arrays = {
        "x": np.pad(x, ((0, s.nb * P - n), (0, 0))),
        "src_t": by_tile(src, 0), "dst_t": by_tile(dst, far), "type_t": by_tile(et, 0),
        "dst_seq": np.pad(dst, (1, s.stiles * P - e + 1), constant_values=(-1, far)),
        "edge_t": np.ascontiguousarray(
            np.pad(ea, ((0, s.tiles * P - e), (0, 0))).reshape(s.tiles, P, D).transpose(0, 2, 1)),
        "node_type_t": np.ascontiguousarray(np.pad(nt, (0, s.nb * P - n)).reshape(s.nb, P).T),
        "W_proj": w["L0_gnn_W_proj"], "a_src": flat(w["L0_gnn_a_src"]), "a_trg": flat(w["L0_gnn_a_trg"]),
        "gat_bias": w["L0_gnn_bias"],
        "W_in_t": w["L1_gnn_W_in"].T, "b_in": w["L1_gnn_b_in"],
        "W_out_t": w["L1_gnn_W_out"].T, "b_out": w["L1_gnn_b_out"],
        "w_ih_t": w["L1_gnn_w_ih"].T, "w_hh_t": w["L1_gnn_w_hh"].T,
        "b_ih": w["L1_gnn_b_ih"], "b_hh": w["L1_gnn_b_hh"],
        "rel_w_t": w["L2_gnn_rel_w"].transpose(2, 0, 1).reshape(D, -1),
        "root_w_t": w["L2_gnn_root_w"].transpose(2, 0, 1).reshape(D, -1), "root_b": flat(w["L2_gnn_root_b"]),
        "Ws": mat(w["L3_gnn_Ws_k"]), "Wr": mat(w["L3_gnn_Wr_k"]), "We": mat(w["L3_gnn_We_k"]),
        "Ws_b": flat(w["L3_gnn_Ws_b"]), "Wr_b": flat(w["L3_gnn_Wr_b"]), "We_b": flat(w["L3_gnn_We_b"]),
        "attn_w": flat(w["L3_gnn_attn_w"]), "attn_b": w["L3_gnn_attn_b"],
    }
    arrays = {k: np.ascontiguousarray(a) for k, a in arrays.items()}
    nc = bacc.Bacc("TRN2", target_bir_lowering=False, num_devices=1)
    io = {k: nc.dram_tensor(f"in_{k}", a.shape, mybir.dt.from_np(a.dtype), kind="ExternalInput").ap()
          for k, a in arrays.items()}
    io["out"] = nc.dram_tensor("out", (s.nb * P, D), F32, kind="ExternalOutput").ap()
    Program(nc, s, io).build()
    r = run_bass_kernel_spmd(nc, [{f"in_{k}": a for k, a in arrays.items()}], core_ids=[0])
    return r.results[0]["out"][:n]
```

```python
from contextlib import ExitStack

import numpy as np

import concourse.bass as bass
from concourse import mybir

F32 = mybir.dt.float32
I32 = mybir.dt.int32
ALU = mybir.AluOpType
ACT = mybir.ActivationFunctionType
AX = mybir.AxisListType
DVE = mybir.EngineType.DVE
PE = mybir.EngineType.PE
SP = mybir.EngineType.SP

P = 128
D = 128
U = 16
G = 4
MOVES = 8
B = U // G
TABLES = 8
BIG = 1e30
EPS_LN = 1e-5
SCAN_CHUNKS = 32
PIECES = 5
CAP = 12.0


class Shape:
    def __init__(self, n, e, heads0, heads3, rels, types):
        self.n, self.e = n, e
        self.blocks = -(-n // P)
        self.nb = self.blocks + self.blocks % 2
        self.tiles = -(-e // P)
        self.steps = -(-(self.tiles + self.blocks - 1) // U) * U
        self.heads0, self.heads3, self.rels, self.node_types = heads0, heads3, rels, types
        self.ctiles = -(-self.tiles // SCAN_CHUNKS)
        self.stiles = self.ctiles * SCAN_CHUNKS


class Chain:

    def __init__(self, eng, sem, start=0):
        self.eng, self.sem, self.n = eng, sem, start

    def __call__(self, ins):
        self.n += 1
        ins.then_inc(self.sem, 1)
        self.eng.wait_ge(self.sem, self.n)


class Turn(Chain):

    def __init__(self, eng, sem, start, go):
        super().__init__(eng, sem)
        self.start, self.go = start, go

    def __call__(self, ins):
        self.n += 1
        ins.then_inc(self.sem, 1)
        hold(self.eng, self.sem, self.start + self.n, self.go)


def clear_ahead(pool, issued):
    pool.sem_inc(issued, 1)


def hold(eng, sem, value, go=None):
    if isinstance(value, int):
        if value > 0:
            eng.wait_ge(sem, value)
        return
    eng.wait_ge(sem, value)
    if go is not None:
        eng.wait_ge(go, 1)


def repeat(eng, n, turn):
    turn(0)
    if n > 1:
        with eng.Fori(1, n) as i:
            turn(i)


def numbered(nc, eng, row, start, n, top, work):
    def group(at, count):
        _, numbers = nc.values_load_multi_w_load_instructions(
            row[0:1, bass.ds(at + start, count)], engines=[DVE], min_val=0, max_val=top,
            skip_runtime_bounds_check_because="the numbers are bounded when made")
        for j in range(count):
            work(at + j, numbers[j])

    full = n // MOVES
    if full:
        group(0, MOVES)
    if full > 1:
        with eng.Fori(1, full) as i:
            group(i * MOVES, MOVES)
    if n % MOVES:
        group(full * MOVES, n % MOVES)


class Arena:

    def __init__(self, *arrays):
        self.parts = [[a[:].rearrange("p b d -> p (b d)"), 0] for a in arrays]

    def take(self, shape, dt=F32):
        n = int(np.prod(shape[1:]))
        n8 = -(-n // 16) * 16
        part = next(p for p in self.parts if p[1] + n8 <= p[0].shape[1])
        ap = part[0][0:shape[0], part[1]:part[1] + n]
        part[1] += n8
        if dt != F32:
            ap = ap.bitcast(dt)
        if len(shape) == 3:
            ap = ap.rearrange("p (a b) -> p a b", a=shape[1])
        if len(shape) == 4:
            ap = ap.rearrange("p (a b c) -> p a b c", a=shape[1], b=shape[2])
        return ap


class Program:
    def __init__(self, nc, shape, io):
        self.nc, self.s, self.io = nc, shape, io
        self.ctx = ExitStack()
        self.count = 0
        self.phase_sems = []

    def sb(self, name, shape, dt=F32, ctx=None):
        self.count += 1
        return (ctx or self.ctx).enter_context(self.nc.sbuf_tensor(f"{name}_{self.count}", shape, dt))

    def ps(self, name, ctx):
        return ctx.enter_context(self.nc.psum_tensor(name, [P, 512], F32))

    def sem(self, name):
        self.count += 1
        handle = self.nc.alloc_semaphore(f"{name}_{self.count}")
        self.phase_sems.append(handle)
        return handle

    def end_phase(self):
        self.nc.clear_and_free_semaphores(self.phase_sems)
        self.nc.all_engine_barrier()
        self.phase_sems = []

    def scratch(self, name, shape):
        return self.nc.dram_tensor(name, shape, F32, kind="Internal").ap()

    def bcast_row(self, ap, width):
        return ap.rearrange("(o w) -> o w", o=1).broadcast_to([P, width])

    def allocate(self):
        s = self.s
        nb, S = s.nb, s.steps
        self.x = self.sb("x_res", [P, nb, D])
        self.hn = self.sb("h_norm", [P, nb, D])
        self.acc = self.sb("acc", [P, nb, 136])
        self.aux = self.sb("aux", [P, nb, D])
        self.aux2 = self.sb("aux2", [P, nb, 136])
        self.wts = self.sb("edge_w", [P, max(S * 8, nb * 136)])
        self.w8 = self.wts[:, 0:S * 8].rearrange("p (s h) -> p s h", h=8)
        self.rel = self.sb("rel_dst", [P, S + U])
        self.srcf = self.sb("src_f", [P, S + U])
        self.src = self.sb("src_i", [P, S + U], I32)
        self.typ = self.sb("type_f", [P, S + U])
        self.blk = self.sb("step_block", [1, U + S + U], I32)
        self.til = self.sb("step_tile", [1, U + S + U], I32)
        self.strg = self.sb("target_scores", [P, nb, s.heads0])
        self.ahead = self.wts[:, 0:S + U]
        self.sidx = self.sb("scatter_rows", [P, S + U], I32)
        self.gidx = self.sb("relation_rows", [P, S + U], I32)
        self.inv = self.sb("inverse_counts", [P, nb, 8])
        self.gin = self.sb("has_in_edges", [P, nb])
        self.gout = self.sb("has_out_edges", [P, nb])
        self.mask = self.sb("mask", [P, S + U])
        self.iota = self.sb("iota_row", [P, P])
        self.ident = self.sb("ident", [P, P])
        self.pidx = self.sb("partition_index", [P, 1])
        self.ones = self.sb("ones", [P, P])
        self.issued = self.nc.alloc_semaphore("indirect_issued")
        self.setup_done = self.nc.alloc_semaphore("setup_done")
        rows = nb * P
        self.t_gat = self.scratch("t_gat", (rows, 136))
        self.t_h = self.scratch("t_h", (rows, D))
        self.t_rel = self.scratch("t_rel", (rows, s.rels, D))
        self.t_sent = self.scratch("t_sent", (rows, D))
        self.t_rows = self.scratch("t_rows", (S, P, D))
        self.t_out = [self.scratch(f"t_out{k}", (rows + P, 136)) for k in range(TABLES)]
        self.t_relrow = self.scratch("t_relrow", (S * P,))
        self.t_srcrow = self.scratch("t_srcrow", (S * P,))
        self.t_seq = self.scratch("t_seq", (s.stiles, s.heads3, P))
        self.t_max = self.scratch("t_max", (s.stiles, s.heads3, P))

    def prepare(self):
        nc, s, io = self.nc, self.s, self.io
        T, S, NF = s.tiles, s.steps, s.blocks - 1
        with ExitStack() as c:
            at = Arena(self.hn, self.acc, self.aux, self.aux2)
            raw = at.take([P, T], I32)
            rawt = at.take([P, T], I32)
            dstf = at.take([P, S + U], F32)
            base = at.take([P, S + U], F32)
            on = at.take([P, S + U], F32)
            junk = at.take([P, S + U], F32)
            below = at.take([P, NF], F32)
            bi = at.take([P, S + U], I32)
            ti = at.take([P, S + U], I32)
            fi = at.take([P, NF], I32)
            io_i = at.take([P, P], I32)
            io_p = at.take([P, 1], I32)
            io_t = at.take([P, S + U], I32)
            row0 = at.take([P, P], F32)
            thr = at.take([P, NF], F32)
            thi = at.take([P, NF], I32)
            minus = at.take([P, NF], F32)
            signs = at.take([P, NF], F32)
            junk_a = at.take([P, T], F32)
            ask, signed = self.sem("ask"), self.sem("signed")
            N1 = NF // 2
            psA = [self.ps(f"p_first{k}", c) for k in range(-(-T // 512))]
            psB = self.ps("p_below", c)
            psT = [self.ps(f"p_turned{j}", c) for j in range(2)]
            line = at.take([P, 4, P], F32)
            turned_rows, lined = self.sem("turned_rows"), self.sem("lined")
            ready = self.sem("ready")
            written = [self.sem(f"written{j}") for j in range(4)]
            parts = [(a, dst, k, min(P, S - k)) for a, dst in ((self.rel, self.t_relrow), (self.srcf, self.t_srcrow))
                     for k in range(0, S, P)]
            loaded, made, seq = self.sem("loaded"), self.sem("iotas"), self.sem("seq")
            rows_ready, counted, summed = self.sem("dst_ready"), self.sem("counted"), self.sem("summed")
            moved, load_x = self.sem("moved"), self.sem("load_x")
            block = c.enter_context(nc.Block())

            @block.sync
            def _(sp):
                sp.dma_start(raw[:], io["dst_t"]).then_inc(loaded, 16)
                sp.dma_start(rawt[:], io["type_t"]).then_inc(loaded, 16)
                sp.dma_start(self.src[:, 0:T], io["src_t"]).then_inc(loaded, 16)
                for g, (_, dst, k, n) in enumerate(parts):
                    sp.wait_ge(lined, g + 1)
                    sp.dma_start(dst[k * P:(k + n) * P].rearrange("(s e) -> s e", e=P), line[0:n, g % 4, :])\
                        .then_inc(written[g % 4], 16)
                for j in range(4):
                    sp.wait_ge(written[j], 16 * len(parts[j::4]))

            @block.scalar
            def _(act):
                act.dma_start(self.x[:], io["x"].rearrange("(b p) d -> p b d", p=P)).then_inc(load_x, 16)
                act.wait_ge(rows_ready, 1)
                act.wait_ge(ask, 1)

                def turn(k):
                    hold(act, signed, k - N1)
                    nc.scalar.activation(junk_a[:], dstf[:, 0:T], ACT.Sign, bias=minus[:, bass.ds(k, 1)],
                                         accum_out=signs[:, bass.ds(k, 1)]).then_inc(signed, 1)
                turn(N1)
                with act.Fori(N1 + 1, NF) as k:
                    turn(k)
                act.wait_ge(load_x, 16)

            @block.gpsimd
            def _(pool):
                nc.gpsimd.iota(io_i[:], pattern=[[1, P]], base=0, channel_multiplier=0).then_inc(made, 1)
                nc.gpsimd.iota(io_p[:], pattern=[[0, 1]], base=0, channel_multiplier=1).then_inc(made, 1)
                nc.gpsimd.iota(io_t[:], pattern=[[1, S + U]], base=0, channel_multiplier=0).then_inc(made, 1)
                nc.gpsimd.iota(thi[:], pattern=[[P, NF]], base=P, channel_multiplier=0).then_inc(made, 1)

            @block.tensor
            def _(pe):
                pe.wait_ge(rows_ready, 1)
                for k, p in enumerate(psA):
                    w = min(512, T - 512 * k)
                    nc.tensor.matmul(p[:, 0:w], row0[:], dstf[:, 512 * k:512 * k + w],
                                     start=True, stop=True).then_inc(summed, 1)
                pe.wait_ge(counted, 1)
                nc.tensor.matmul(psB[:, 0:NF], self.ones[:], below[:], start=True, stop=True).then_inc(summed, 1)
                pe.wait_ge(ready, 1)
                for g, (a, _, k, n) in enumerate(parts):
                    if g >= 2:
                        pe.wait_ge(lined, g - 1)
                    nc.tensor.transpose(psT[g % 2][0:n, 0:P], a[:, k:k + n], self.ident[:]).then_inc(turned_rows, 1)

            @block.vector
            def _(dve):
                v = nc.vector
                do = Chain(dve, seq)
                do(v.memset(self.ones[:], 1.0))
                do(v.memset(dstf[:], float((s.blocks + 1) * P)))
                do(v.memset(self.typ[:], 0.0))
                do(v.memset(self.srcf[:], 0.0))
                do(v.memset(on[:], 0.0))
                do(v.memset(on[:, 0:T], 1.0))
                do(v.memset(base[:], 0.0))
                do(v.memset(bi[:], 0))
                do(v.memset(self.rel[:], 0.0))
                dve.wait_ge(made, 4)
                do(v.tensor_copy(self.iota[:], io_i[:]))
                do(v.tensor_copy(self.pidx[:], io_p[:]))
                do(v.tensor_copy(thr[:], thi[:]))
                do(v.tensor_copy(ti[:], io_t[:]))
                do(v.tensor_scalar(self.ident[:], self.iota[:], self.pidx[:, 0:1], None, ALU.is_equal))
                do(v.memset(row0[:], 0.0))
                do(v.memset(row0[0:1, :], 1.0))
                dve.wait_ge(loaded, 48)
                do(v.tensor_copy(self.typ[:, 0:T], rawt[:]))
                do(v.tensor_copy(self.srcf[:, 0:T], self.src[:, 0:T]))
                v.tensor_copy(dstf[:, 0:T], raw[:]).then_inc(rows_ready, 1)
                v.tensor_scalar(minus[:], thr[:], -1.0, 0.5, ALU.mult, ALU.add).then_inc(ask, 1)
                dve.wait_ge(rows_ready, 1)
                def turn(k):
                    hold(dve, moved, k)
                    v.tensor_scalar(junk[:, 0:T], dstf[:, 0:T], thr[:, bass.ds(k, 1)], 0.0,
                                    ALU.is_lt, ALU.add, accum_out=below[:, bass.ds(k, 1)]).then_inc(moved, 1)
                repeat(dve, N1, turn)
                dve.wait_ge(moved, N1)
                dve.wait_ge(signed, NF - N1)
                do(v.tensor_scalar(below[:, N1:NF], signs[:, N1:NF], float(T), -0.5, ALU.subtract, ALU.mult))
                do(v.tensor_copy(junk[:, 0:NF], below[:]))
                v.tensor_copy(below[:], junk[:, 0:NF]).then_inc(counted, 1)
                dve.wait_ge(counted, 1)
                dve.wait_ge(summed, len(psA) + 1)
                for k, p in enumerate(psA):
                    w = min(512, T - 512 * k)
                    do(v.tensor_copy(bi[:, 512 * k:512 * k + w], p[:, 0:w]))
                do(v.tensor_single_scalar(bi[:, 0:T], bi[:, 0:T], 7, ALU.arith_shift_right))
                do(v.tensor_single_scalar(bi[:, 0:T], bi[:, 0:T], 7, ALU.logical_shift_left))
                do(v.tensor_copy(base[:, 0:T], bi[:, 0:T]))
                do(v.tensor_single_scalar(bi[:, 0:T], bi[:, 0:T], 7, ALU.arith_shift_right))
                do(v.tensor_copy(fi[:], psB[:, 0:NF]))
                do(v.tensor_single_scalar(ti[:, T:T + NF], fi[:], 7, ALU.arith_shift_right))
                do(v.tensor_single_scalar(fi[:], fi[:], P - 1, ALU.bitwise_and))
                do(v.tensor_copy(junk[:, 0:NF], fi[:]))
                do(v.tensor_scalar(on[:, T:T + NF], junk[:, 0:NF], 0.0, None, ALU.is_gt))
                do(v.tensor_copy(junk[:, 0:NF], ti[:, T:T + NF]))
                do(v.tensor_scalar(junk[:, 0:NF], junk[:, 0:NF], float(T - 1), None, ALU.min))
                do(v.tensor_copy(ti[:, T:T + NF], junk[:, 0:NF]))
                do(v.memset(ti[:, T + NF:S + U], 0))
                do(v.tensor_copy(base[:, T:T + NF], thr[:]))
                do(v.tensor_copy(bi[:, T:T + NF], io_t[:, 1:NF + 1]))
                do(v.memset(self.blk[:], 0))
                do(v.memset(self.til[:], 0))
                do(v.tensor_copy(self.blk[:, U:], bi[0:1, :]))
                do(v.tensor_copy(self.til[:, U:], ti[0:1, :]))
                def move(k, t):
                    for a in (dstf, self.srcf, self.typ):
                        v.tensor_copy(a[:, bass.ds(k + T, 1)], a[:, bass.ds(t, 1)]).then_inc(moved, 1)
                numbered(nc, dve, self.til, T + U, NF, T - 1, move)
                dve.wait_ge(moved, N1 + 3 * NF)
                do(v.tensor_copy(self.src[:], self.srcf[:]))
                do(v.tensor_scalar(on[:], on[:], 1.0, -1e6, ALU.subtract, ALU.mult))
                do(v.tensor_tensor(junk[:], dstf[:], base[:], ALU.subtract))
                do(v.tensor_tensor(self.rel[:], junk[:], on[:], ALU.add))
                do(v.tensor_scalar(junk[:], self.rel[:], 0.0, None, ALU.is_ge))
                do(v.tensor_scalar(self.mask[:], self.rel[:], float(P), None, ALU.is_lt))
                do(v.tensor_tensor(self.mask[:], self.mask[:], junk[:], ALU.mult))
                dve.sem_inc(self.setup_done, 1)
                dve.sem_inc(ready, 1)
                for g, (_, _, _, n) in enumerate(parts):
                    dve.wait_ge(turned_rows, g + 1)
                    if g >= 4:
                        dve.wait_ge(written[g % 4], 16 * (g // 4))
                    v.tensor_copy(line[0:n, g % 4, :], psT[g % 2][0:n, 0:P]).then_inc(lined, 1)

    def norm_sems(self, name):
        return {k: self.sem(f"{name}_norm_{k}") for k in ("centered", "squared", "ask", "root", "scaled", "done")}

    def halves(self):
        nb = self.s.nb
        return slice(0, nb // 2), slice(nb // 2, nb)

    def norm_vector(self, dve, do, sums, rstd, n):
        v = self.nc.vector
        wide = lambda a, b: a[:, b].rearrange("p (b o) -> p b o", o=1).broadcast_to([P, b.stop - b.start, D])
        do(v.tensor_reduce(sums[:], self.x[:], AX.X, ALU.add))
        do(v.tensor_scalar(sums[:], sums[:], 1.0 / D, None, ALU.mult))
        for b in self.halves():
            v.tensor_tensor(self.hn[:, b, :], self.x[:, b, :], wide(sums, b), ALU.subtract).then_inc(n["centered"], 1)
        dve.wait_ge(n["centered"], 2)
        for k, b in enumerate(self.halves()):
            dve.wait_ge(n["squared"], k + 1)
            do(v.tensor_reduce(sums[:, b], self.acc[:, b, 0:D], AX.X, ALU.add))
        v.tensor_scalar(sums[:], sums[:], 1.0 / D, EPS_LN, ALU.mult, ALU.add).then_inc(n["ask"], 1)
        dve.wait_ge(n["root"], 1)
        do(v.reciprocal(rstd[:], rstd[:]))
        for b in self.halves():
            v.tensor_tensor(self.hn[:, b, :], self.hn[:, b, :], wide(rstd, b), ALU.mult).then_inc(n["scaled"], 1)

    def norm_scalar(self, act, sums, rstd, n):
        a = self.nc.scalar
        for k, b in enumerate(self.halves()):
            act.wait_ge(n["centered"], k + 1)
            a.activation(self.acc[:, b, 0:D], self.hn[:, b, :], ACT.Square).then_inc(n["squared"], 1)
        act.wait_ge(n["ask"], 1)
        a.activation(rstd[:], sums[:], ACT.Sqrt).then_inc(n["root"], 1)
        for k, b in enumerate(self.halves()):
            act.wait_ge(n["scaled"], k + 1)
            a.activation(self.hn[:, b, :], self.hn[:, b, :], ACT.Relu).then_inc(n["done"], 1)

    def product_sems(self, name):
        return {k: self.sem(f"{name}_{k}") for k in
                ("loaded", "staged", "turned_ps", "turned", "product", "read", "finished", "seq")}

    def product_memory(self, name, c, k, width, at=None, banks=1):
        take = at.take if at else lambda shape: self.sb(name, shape, F32, c)
        return (take([P, width]), take([P, 2, k * D]), take([P, 2, k * D]),
                [self.ps(f"{name}_pt{j}", c) for j in range(2)],
                [self.ps(f"{name}_po{j}", c) for j in range(2 * banks)])

    def product_scalar(self, act, q, arrays, stage, turned, psT):
        go, K = self.setup_done, len(arrays)

        def rows(i, j, _):
            n = 2 * i + j
            hold(act, q["turned_ps"], (n - 1) * K, go)
            for k in range(K):
                self.nc.scalar.activation(stage[:, j, k * D:(k + 1) * D], arrays[k][:, bass.ds(n, 1), 0:D],
                                          ACT.Copy).then_inc(q["staged"], 1)

        def copy(i, j, _):
            n = 2 * i + j
            hold(act, q["product"], n - 1)
            hold(act, q["turned_ps"], n * K + K)
            self.nc.scalar.activation(turned[:, j, :], psT[j][:, 0:K * D], ACT.Copy).then_inc(q["turned"], 1)
        return rows, copy

    def product_tensor(self, pe, q, stage, turned, psT, K, loads, multiply, reads=1):
        pe.wait_ge(q["loaded"], 16 * loads)

        def turn(i, j, _):
            n = 2 * i + j
            hold(pe, q["turned"], n - 1)
            hold(pe, q["staged"], n * K + K)
            for k in range(K):
                m = self.nc.tensor.transpose(psT[j][:, k * D:k * D + D], stage[:, j, k * D:(k + 1) * D],
                                             self.ident[:])
                m.then_inc(q["turned_ps"], 1)

        def product(i, j, _):
            n = 2 * i + j
            hold(pe, q["turned"], n + 1)
            hold(pe, q["read"], (n - 1) * reads)
            multiply(j).then_inc(q["product"], 1)
        self.flow(pe, [(0, turn), (1, product)], count=self.s.nb, unit=2)

    def pieces(self, sp, table, rows, finished, sent, per=1):
        nb = self.s.nb
        tab = table.rearrange("(b p) d -> p b d", p=P)
        cuts = [nb * k // PIECES for k in range(PIECES + 1)]
        for a, b in zip(cuts, cuts[1:]):
            sp.wait_ge(finished, b * per)
            sp.dma_start(tab[:, a:b, :], rows[:, a:b, 0:table.shape[1]]).then_inc(sent, 16)
        sp.wait_ge(sent, 16 * PIECES)

    def gat_nodes(self):
        nc, s, io, go = self.nc, self.s, self.io, self.setup_done
        H = s.heads0
        F = D // H
        q = self.product_sems("gat")
        sent, seq, norm = self.sem("sent"), self.sem("seq"), self.norm_sems("gat")
        scaled_up, scored, kept = self.sem("scaled_up"), self.sem("scored"), self.sem("kept")
        with ExitStack() as c:
            w, stage, turned, psT, psO = self.product_memory("gat", c, 1, D)
            bias = self.sb("gat_bias", [P, D], F32, c)
            a_both = self.sb("a_both", [P, 2, D], F32, c)
            h = self.sb("gat_h", [P, 2, D], F32, c)
            scaled = self.sb("scaled", [P, 2, 2 * D], F32, c)
            score = self.sb("score", [P, 2, 2 * H], F32, c)
            sums, rstd = self.sb("sums", [P, s.nb], F32, c), self.sb("rstd", [P, s.nb], F32, c)
            block = c.enter_context(nc.Block())

            @block.sync
            def _(sp):
                sp.dma_start(w[:], io["W_proj"]).then_inc(q["loaded"], 16)
                sp.dma_start(a_both[:, 0, :], self.bcast_row(io["a_src"], D)).then_inc(q["loaded"], 16)
                sp.dma_start(a_both[:, 1, :], self.bcast_row(io["a_trg"], D)).then_inc(q["loaded"], 16)
                sp.dma_start(bias[:], self.bcast_row(io["gat_bias"], D)).then_inc(q["loaded"], 16)
                self.pieces(sp, self.t_gat, self.aux2, q["finished"], sent, per=3)

            @block.scalar
            def _(act):
                self.norm_scalar(act, sums, rstd, norm)
                act.wait_ge(norm["done"], 2)
                rows, copy = self.product_scalar(act, q, [self.hn], stage, turned, psT)

                def keep(i, j, _):
                    n = 2 * i + j
                    at = bass.ds(n, 1)
                    flat = lambda a: a.rearrange("p o d -> p (o d)")
                    hold(act, scored, n + 1, go)
                    for out, made in ((self.aux2[:, at, 0:D], h[:, j, :]),
                                      (self.strg[:, at, :], score[:, j, H:2 * H]),
                                      (self.aux2[:, at, D:D + H], score[:, j, 0:H])):
                        nc.scalar.activation(flat(out), made, ACT.Copy).then_inc(q["finished"], 1)
                self.flow(act, [(0, rows), (1, copy), (3, keep)], count=s.nb, unit=2)

            @block.tensor
            def _(pe):
                self.product_tensor(pe, q, stage, turned, psT, 1, 4, lambda j: nc.tensor.matmul(
                    psO[j][:, 0:D], turned[:, j, :], w[:], start=True, stop=True))

            @block.vector
            def _(dve):
                v = nc.vector
                do = Chain(dve, seq)
                self.norm_vector(dve, do, sums, rstd, norm)
                dve.wait_ge(q["loaded"], 64)

                def take(i, j, _):
                    n = 2 * i + j
                    hold(dve, q["product"], n + 1)
                    hold(dve, q["finished"], (n - 1) * 3)
                    hold(dve, kept, n - 1)
                    v.tensor_copy(h[:, j, :], psO[j][:, 0:D]).then_inc(q["read"], 1)
                    hold(dve, q["read"], n + 1)
                    v.tensor_tensor(scaled[:, j, :].rearrange("p (t d) -> p t d", t=2),
                                    h[:, j, :].rearrange("p (o d) -> p o d", o=1).broadcast_to([P, 2, D]),
                                    a_both[:], ALU.mult).then_inc(scaled_up, 1)

                def score_up(i, j, _):
                    n = 2 * i + j
                    hold(dve, scaled_up, n + 1)
                    v.tensor_reduce(score[:, j, :], scaled[:, j, :].rearrange("p (h f) -> p h f", f=F),
                                    AX.X, ALU.add).then_inc(scored, 1)
                    v.tensor_tensor(self.aux[:, bass.ds(n, 1), :].rearrange("p o d -> p (o d)"), h[:, j, :],
                                    bias[:], ALU.add).then_inc(kept, 1)
                self.flow(dve, [(0, take), (1, score_up)], count=s.nb, unit=2)

    def node_products(self, name, arrays, products):
        nc, s = self.nc, self.s
        K, N = len(arrays), len(products)
        q = self.product_sems(name)
        with ExitStack() as c:
            w, stage, turned, psT, psO = self.product_memory(name, c, K, N * D)
            biases = [(n, b) for n, product in enumerate(products) for b in product[2]]
            each = self.sb(f"{name}_biases", [P, len(biases) * D], F32, c)
            bias = self.sb(f"{name}_bias", [P, N * D], F32, c)
            tables = [(table, out) for _, _, _, _, out, table in products if table is not None]
            sent = self.sem(f"{name}_sent")
            block = c.enter_context(nc.Block())
            loads = N + len(biases)

            @block.sync
            def _(sp):
                for n, product in enumerate(products):
                    sp.dma_start(w[:, n * D:(n + 1) * D], product[1]).then_inc(q["loaded"], 16)
                for k, (_, b) in enumerate(biases):
                    sp.dma_start(each[:, k * D:(k + 1) * D], self.bcast_row(b, D)).then_inc(q["loaded"], 16)
                for table, out in tables:
                    self.pieces(sp, table, out, q["read"], sent, per=N)

            @block.scalar
            def _(act):
                rows, copy = self.product_scalar(act, q, arrays, stage, turned, psT)
                self.flow(act, [(0, rows), (1, copy)], count=s.nb, unit=2)

            @block.tensor
            def _(pe):
                def multiply(j):
                    for n, product in enumerate(products):
                        k = product[0]
                        m = nc.tensor.matmul(psO[j][:, n * D:(n + 1) * D], turned[:, j, k * D:(k + 1) * D],
                                             w[:, n * D:(n + 1) * D], start=True, stop=True)
                    return m
                self.product_tensor(pe, q, stage, turned, psT, K, loads, multiply, reads=N)

            @block.vector
            def _(dve):
                v = nc.vector
                dve.wait_ge(q["loaded"], 16 * loads)
                do = Chain(dve, q["seq"])
                do(v.memset(bias[:], 0.0))
                for k, (n, _) in enumerate(biases):
                    do(v.tensor_tensor(bias[:, n * D:(n + 1) * D], bias[:, n * D:(n + 1) * D],
                                       each[:, k * D:(k + 1) * D], ALU.add))

                def add(i, j, _):
                    n = 2 * i + j
                    at = bass.ds(n, 1)
                    hold(dve, q["product"], n + 1)
                    for p, (_, _, _, gate, out, _) in enumerate(products):
                        dst = out[:, at, 0:D].rearrange("p o d -> p (o d)")
                        cols = slice(p * D, (p + 1) * D)
                        if gate is None:
                            m = v.tensor_tensor(dst, psO[j][:, cols], bias[:, cols], ALU.add)
                        else:
                            m = v.scalar_tensor_tensor(dst, bias[:, cols], gate[:, at], psO[j][:, cols],
                                                       ALU.mult, ALU.add)
                        m.then_inc(q["read"], 1)
                self.flow(dve, [(0, add)], count=s.nb, unit=2)

    def refill(self, i, r, idx, source, idx_ready):
        k = r - r % B
        self.nc.vector.tensor_copy(idx[:, k:k + B], source[:, bass.ds(i * U + k + U, B)])\
            .then_inc(idx_ready, B)

    def four(self, row):
        return row.rearrange("p (o n) -> p o n", o=1).broadcast_to([P, B, row.shape[1]])

    def spread(self, cols, width):
        return cols.rearrange("p (s o) -> p s o", o=1).broadcast_to([P, B, width])

    def load_rows(self, sp, i, r, table, rows, used, landed):
        if r % B == 0:
            h = r // B
            hold(sp, used, i * U + r + B - U)
            sp.dma_start(rows[:, h, :], table[bass.ds((i * U + r) * P, B * P)]
                         .rearrange("(o w) -> o w", o=1).broadcast_to([P, B * P])).then_inc(landed[h], 16)

    def select_turned(self, dve, i, r, rows, landed, selT, used, made):
        if r % B == 0:
            h = r // B
            hold(dve, landed[h], i * 16 + 16)
            hold(dve, used, i * U + r + B - U)
            self.nc.vector.tensor_scalar(selT[:, h, :], rows[:, h, :], self.pidx[:, 0:1], None, ALU.is_equal)\
                .then_inc(made, B)

    def select(self, dve, i, r, q, sel, used):
        if r % B == 0:
            hold(dve, used, i * U + r + B - U)
            self.nc.vector.tensor_tensor(sel[:, r // B, :].rearrange("p (s n) -> p s n", n=P),
                                         self.four(self.iota[:]),
                                         self.spread(self.rel[:, bass.ds(i * U + r, B)], P), ALU.is_equal)\
                .then_inc(q["sel"], B)

    def matrix(self, halves, r, width=P):
        return halves[:, r // B, (r % B) * width:(r % B + 1) * width]

    def flow(self, eng, parts, blocks_for=None, tiles_for=None, count=None, unit=U):
        turns = (self.s.steps if count is None else count) // unit
        behind = -(-max(lag for lag, _ in parts) // unit)

        def turn(i):
            numbers = {}
            for f, row, top in ((blocks_for, self.blk, self.s.nb - 1), (tiles_for, self.til, self.s.tiles - 1)):
                if f is not None:
                    lag = next(g for g, h in parts if h is f)
                    if not isinstance(i, int) or i < turns + -(-lag // unit):
                        kind = {"PE": PE, "DVE": DVE, "SP": SP}[f.engine]
                        _, numbers[f] = self.nc.values_load_multi_w_load_instructions(
                            row[0:1, bass.ds(i * unit + (U - lag), unit)], engines=[kind], min_val=0, max_val=top,
                            skip_runtime_bounds_check_because="the numbers are bounded when made")
            for r in range(unit):
                for lag, f in parts:
                    k, j = (r - lag) % unit, i + (r - lag) // unit
                    if isinstance(j, int) and not 0 <= j < turns:
                        continue
                    f(j, k, numbers[f][r] if f in numbers else None)

        written_out = min(behind + 1, turns)
        for i in range(written_out):
            turn(i)
        if turns > written_out:
            with eng.Fori(written_out, turns) as i:
                turn(i)
        for i in range(turns, turns + behind):
            turn(i)

    def gat_gather(self):
        nc, s, go = self.nc, self.s, self.setup_done
        H, S, turns = s.heads0, s.steps, s.steps // U
        q = {k: self.sem(f"gg_{k}") for k in ("idx", "selT", "target", "logit", "leaky", "masked", "final")}
        gathered = [self.sem(f"gg_gathered{r}") for r in range(U)]
        stored = [self.sem(f"gg_stored{h}") for h in range(G)]
        landed = [self.sem(f"gg_landed{h}") for h in range(G)]
        with ExitStack() as c:
            at = Arena(self.aux2)
            rows = at.take([P, U, 136])
            idx = at.take([P, U], I32)
            relrow = at.take([P, G, B * P])
            selT = at.take([P, G, B * P])
            off = self.sb("gg_off", [P, S], F32, c)
            psE = [self.ps(f"gg_pe{j}", c) for j in range(4)]
            block = c.enter_context(nc.Block())

            @block.gpsimd
            def _(pool):
                def gather(i, r, _):
                    hold(pool, q["idx"], i * U + r + 1)
                    hold(pool, q["logit"], i * U + r + 1 - U)
                    hold(pool, stored[r // B], i * 16)
                    clear_ahead(pool, self.issued)
                    nc.gpsimd.indirect_dma_start(rows[:, r, :], None, self.t_gat,
                                                 bass.IndirectOffsetOnAxis(idx[:, r:r + 1], 0))\
                        .then_inc(gathered[r], 16)
                self.flow(pool, [(0, gather)])

            @block.sync
            def _(sp):
                def rel(i, r, _):
                    self.load_rows(sp, i, r, self.t_relrow, relrow, q["selT"], landed)

                def store(i, r, _):
                    hold(sp, gathered[r], i * 16 + 16)
                    if r % B == B - 1:
                        k = r - r % B
                        sp.dma_start(self.t_rows[bass.ds(i * U + k, B), :, :].rearrange("s p d -> p s d"),
                                     rows[:, k:k + B, 0:D]).then_inc(stored[r // B], 16)
                self.flow(sp, [(0, rel), (4, store)])
                for h in range(G):
                    sp.wait_ge(stored[h], 16 * turns)

            @block.tensor
            def _(pe):
                def target(i, r, b):
                    hold(pe, q["selT"], i * U + r + 1)
                    hold(pe, q["logit"], i * U + r + 1 - 4)
                    nc.tensor.matmul(psE[r % 4][:, 0:H], self.matrix(selT, r), self.strg[:, bass.ds(b, 1), :],
                                     start=True, stop=True).then_inc(q["target"], 1)
                target.engine = "PE"
                self.flow(pe, [(0, target)], blocks_for=target)

            @block.vector
            def _(dve):
                v = nc.vector
                v.tensor_copy(idx[:], self.src[:, 0:U]).then_inc(q["idx"], U)
                v.tensor_scalar(off[:], self.mask[:, 0:S], 1.0, BIG, ALU.subtract, ALU.mult).then_inc(q["final"], 1)
                dve.wait_ge(q["final"], 1)

                def select(i, r, _):
                    self.select_turned(dve, i, r, relrow, landed, selT, q["target"], q["selT"])

                def leaky(i, r, _):
                    if r % B < B - 1:
                        return
                    end, cols = i * U + r + 1, bass.ds(i * U + r + 1 - B, B)
                    w = self.w8[:, cols, 0:H]
                    hold(dve, q["logit"], end)
                    v.scalar_tensor_tensor(w, w, 0.2, w, ALU.mult, ALU.max).then_inc(q["leaky"], B)
                    hold(dve, q["leaky"], end)
                    v.tensor_tensor(w, w, self.spread(self.mask[:, cols], H), ALU.mult).then_inc(q["masked"], B)
                    hold(dve, q["masked"], end)
                    v.tensor_tensor(w, w, self.spread(off[:, cols], H), ALU.add).then_inc(q["final"], B)

                def logit(i, r, _):
                    hold(dve, gathered[r], i * 16 + 16, go if r % B == B - 1 else None)
                    if r % B == B - 1:
                        self.refill(i, r, idx, self.src, q["idx"])
                    hold(dve, q["target"], i * U + r + 1)
                    v.tensor_tensor(self.w8[:, bass.ds(i * U + r, 1), 0:H].rearrange("p o h -> p (o h)"),
                                    rows[:, r, D:D + H], psE[r % 4][:, 0:H], ALU.add).then_inc(q["logit"], 1)
                self.flow(dve, [(0, select), (4, logit), (5, leaky)])

    def gat_softmax(self):
        nc, s = self.nc, self.s
        H = s.heads0
        seq, ready, turned, top = (self.sem(f"gs_{k}") for k in ("seq", "ready", "turned", "top"))
        with ExitStack() as c:
            part = self.sb("part_max", [P, 1], F32, c)
            tops = self.sb("tops", [1, P], F32, c)
            one = self.sb("one_max", [1, 1], F32, c)
            low = self.sb("minus_max", [P, 1], F32, c)
            ps = self.ps("gs_ps", c)
            block = c.enter_context(nc.Block())
            w = self.w8[:, :, 0:H]

            @block.tensor
            def _(pe):
                pe.wait_ge(ready, 1)
                nc.tensor.transpose(ps[0:1, 0:P], part[:], self.ident[:]).then_inc(turned, 1)
                pe.wait_ge(ready, 2)
                nc.tensor.matmul(ps[:, P:P + 1], self.ones[0:1, :], one[:], start=True, stop=True).then_inc(turned, 1)

            @block.scalar
            def _(act):
                act.wait_ge(top, 1)
                nc.scalar.activation(w, w, ACT.Exp, bias=low[:, 0:1])

            @block.vector
            def _(dve):
                v = nc.vector
                do = Chain(dve, seq)
                v.tensor_reduce(part[:], w, AX.XY, ALU.max).then_inc(ready, 1)
                dve.wait_ge(turned, 1)
                do(v.tensor_copy(tops[:], ps[0:1, 0:P]))
                v.tensor_reduce(one[:], tops[:], AX.X, ALU.max).then_inc(ready, 1)
                dve.wait_ge(turned, 2)
                v.tensor_scalar(low[:], ps[:, P:P + 1], -1.0, None, ALU.mult).then_inc(top, 1)

    def weighted_sum(self, name, H):
        nc, s, go = self.nc, self.s, self.setup_done
        q = {k: self.sem(f"{name}_{k}") for k in ("sel", "scaled", "weights", "summed", "added", "cleared")}
        loaded = [self.sem(f"{name}_loaded{h}") for h in range(G)]
        with ExitStack() as c:
            at = Arena(self.hn)
            rows = at.take([P, U, D])
            vals = at.take([P, U, D + H])
            sel = at.take([P, G, B * P])
            psO = [self.ps(f"{name}_po{j}", c) for j in range(8)]
            block = c.enter_context(nc.Block())

            @block.sync
            def _(sp):
                def load(i, r, _):
                    if r % B == 0:
                        hold(sp, q["scaled"], i * U + r + B - U)
                        sp.dma_start(rows[:, r:r + B, :], self.t_rows[bass.ds(i * U + r, B), :, :]
                                     .rearrange("s p d -> p s d")).then_inc(loaded[r // B], 16)
                self.flow(sp, [(0, load)])

            @block.gpsimd
            def _(pool):
                def scale(i, r, _):
                    if r % B == 0:
                        hold(pool, loaded[r // B], i * 16 + 16, go)
                        hold(pool, q["summed"], i * U + r + B - U, go)
                        for k in range(B):
                            w = self.w8[:, bass.ds(i * U + r + k, 1), 0:H].rearrange("p o h -> p (o h)")\
                                .rearrange("p (h o) -> p h o", o=1).broadcast_to([P, H, D // H])
                            nc.gpsimd.tensor_tensor(vals[:, r + k, 0:D].rearrange("p (h f) -> p h f", h=H),
                                                    rows[:, r + k, :].rearrange("p (h f) -> p h f", h=H), w,
                                                    ALU.mult).then_inc(q["scaled"], 1)
                self.flow(pool, [(0, scale)])

            @block.scalar
            def _(act):
                def weights(i, r, _):
                    if r % B == 0:
                        hold(act, q["summed"], i * U + r + B - U, go)
                        nc.scalar.activation(vals[:, r:r + B, D:D + H], self.w8[:, bass.ds(i * U + r, B), 0:H],
                                             ACT.Copy).then_inc(q["weights"], B)
                self.flow(act, [(0, weights)])

            @block.tensor
            def _(pe):
                def total(i, r, _):
                    if r % B == 0:
                        hold(pe, q["sel"], i * U + r + B)
                        hold(pe, q["weights"], i * U + r + B)
                        hold(pe, q["scaled"], i * U + r + B)
                    self.free_bank(pe, i, r, q, psO)
                    nc.tensor.matmul(psO[r % 8][:, 0:D + H], self.matrix(sel, r), vals[:, r, :],
                                     start=True, stop=True).then_inc(q["summed"], 1)
                self.flow(pe, [(0, total)])

            @block.vector
            def _(dve):
                v = nc.vector
                v.memset(self.acc[:], 0.0).then_inc(q["cleared"], 1)
                v.memset(self.aux2[:], 0.0).then_inc(q["cleared"], 1)
                dve.wait_ge(q["cleared"], 2)

                def select(i, r, _):
                    self.select(dve, i, r, q, sel, q["summed"])

                def add(i, r, b):
                    self.add_sum(dve, i, r, b, q, psO, D + H, (self.acc, self.aux2))
                add.engine = "DVE"
                self.flow(dve, [(0, select), (B, add)], blocks_for=add)
                dve.wait_ge(q["added"], s.steps)
                v.tensor_tensor(self.acc[:], self.acc[:], self.aux2[:], ALU.add)

    def free_bank(self, pe, i, r, q, psO):
        if len(psO) < 2 * B:
            hold(pe, q["added"], i * U + r + 1 - len(psO))
        elif r % B == 0:
            hold(pe, q["added"], i * U + r + B - len(psO))

    def add_sum(self, dve, i, r, b, q, psO, width, into):
        if len(psO) < 2 * B:
            hold(dve, q["summed"], i * U + r + 1)
        elif r % B == 0:
            hold(dve, q["summed"], i * U + r + B)
        hold(dve, q["added"], i * U + r + 1 - len(into))
        a = into[r % len(into)][:, bass.ds(b, 1), 0:width].rearrange("p o d -> p (o d)")
        self.nc.vector.tensor_tensor(a, a, psO[r % len(psO)][:, 0:width], ALU.add).then_inc(q["added"], 1)

    def gat_output(self):
        nc, s = self.nc, self.s
        nb, H = s.nb, s.heads0
        seq, lowered, raised, sent = (self.sem(f"go_{k}") for k in ("seq", "lowered", "raised", "sent"))
        norm = self.norm_sems("go")
        halves = self.halves()
        with ExitStack() as c:
            den = self.sb("gat_den", [P, nb, H], F32, c)
            sums, rstd = self.sb("sums", [P, nb], F32, c), self.sb("rstd", [P, nb], F32, c)
            block = c.enter_context(nc.Block())
            neg = self.aux2[:, :, 0:D]

            @block.sync
            def _(sp):
                table = self.t_h.rearrange("(b p) d -> p b d", p=P)
                for k, b in enumerate(halves):
                    sp.wait_ge(norm["done"], k + 1)
                    sp.dma_start(table[:, b, :], self.hn[:, b, :]).then_inc(sent, 16)
                sp.wait_ge(sent, 32)

            @block.scalar
            def _(act):
                for k, b in enumerate(halves):
                    act.wait_ge(lowered, k + 1)
                    nc.scalar.activation(neg[:, b, :], neg[:, b, :], ACT.Exp).then_inc(raised, 1)
                self.norm_scalar(act, sums, rstd, norm)

            @block.vector
            def _(dve):
                v = nc.vector
                do = Chain(dve, seq)
                do(v.tensor_scalar(den[:], self.acc[:, :, D:D + H], 1e-16, None, ALU.add))
                do(v.reciprocal(den[:], den[:]))
                for h in range(H):
                    a = self.acc[:, :, h * (D // H):(h + 1) * (D // H)]
                    do(v.tensor_tensor(a, a, den[:, :, h:h + 1].broadcast_to([P, nb, D // H]), ALU.mult))
                out = self.acc[:, :, 0:D]
                do(v.tensor_tensor(out, out, self.aux[:], ALU.add))
                for b in halves:
                    v.tensor_scalar(neg[:, b, :], out[:, b, :], 0.0, None, ALU.min).then_inc(lowered, 1)
                for k, b in enumerate(halves):
                    dve.wait_ge(raised, k + 1)
                    do(v.scalar_tensor_tensor(out[:, b, :], out[:, b, :], 0.0, neg[:, b, :], ALU.max, ALU.add))
                    do(v.scalar_tensor_tensor(self.x[:, b, :], out[:, b, :], -1.0, self.x[:, b, :],
                                              ALU.add, ALU.add))
                self.norm_vector(dve, do, sums, rstd, norm)

    def gather_sum(self, name, table, source, kinds=False, means=False):
        nc, s = self.nc, self.s
        R = s.rels
        q = {k: self.sem(f"{name}_{k}") for k in
             ("idx", "sel", "summed", "added", "cleared", "onehot", "ahead", "selT", "picked",
              "own", "weight", "weighed")}
        gathered = [self.sem(f"{name}_gathered{r}") for r in range(U)]
        landed = [self.sem(f"{name}_landed{h}") for h in range(G)]
        zeroed = self.sem(f"{name}_zeroed")
        width = D + R if kinds else D
        with ExitStack() as c:
            at = Arena(self.aux, self.aux2)
            rows = at.take([P, U, D])
            idx = at.take([P, U], I32)
            sel = at.take([P, G, B * P])
            hot = at.take([P, G, B * 8])
            same = at.take([P, B, P])
            lower = at.take([P, P])
            row = at.take([P, G, B * P])
            selT = at.take([P, G, B * P])
            own = at.take([P, G, B * 8])
            w2 = at.take([P, G, B])
            nought = at.take([P, 136])
            banks = [self.ps(f"{name}_p{j}", c) for j in range(8)]
            psO, psW = (banks[0:4], banks[4:8]) if means else (banks, None)
            block = c.enter_context(nc.Block())

            @block.gpsimd
            def _(pool):
                def gather(i, r, _):
                    hold(pool, q["idx"], i * U + r + 1)
                    hold(pool, q["summed"], i * U + r + 1 - U)
                    clear_ahead(pool, self.issued)
                    nc.gpsimd.indirect_dma_start(rows[:, r, :], None, table,
                                                 bass.IndirectOffsetOnAxis(idx[:, r:r + 1], 0))\
                        .then_inc(gathered[r], 16)
                self.flow(pool, [(0, gather)])

            if kinds:
                @block.scalar
                def _(act):
                    act.wait_ge(q["cleared"], 1)
                    pieces = [(k, a, b) for k in range(TABLES)
                              for a, b in ((0, s.nb // 2), (s.nb // 2, s.nb + 1))]
                    for n, (k, a, b) in enumerate(pieces):
                        if n:
                            act.wait_ge(q["summed"], n * s.steps // (len(pieces) + 1))
                        act.dma_start(self.t_out[k].rearrange("(b p) d -> p b d", p=P)[:, a:b, :],
                                      nought[:].rearrange("p (o d) -> p o d", o=1)
                                      .broadcast_to([P, b - a, 136])).then_inc(zeroed, 16)
                    act.wait_ge(zeroed, 16 * len(pieces))

            @block.sync
            def _(sp):
                def numbers(i, r, _):
                    table, used = (self.t_srcrow, q["ahead"]) if kinds else (self.t_relrow, q["selT"])
                    self.load_rows(sp, i, r, table, row, used, landed)
                self.flow(sp, [(0, numbers)])

            @block.tensor
            def _(pe):
                def total(i, r, _):
                    made = q["weighed"] if means else q["sel"]
                    if r % B == 0:
                        hold(pe, made, i * U + r + B)
                    hold(pe, gathered[r], i * 16 + 16)
                    self.free_bank(pe, i, r, q, psO)
                    m = nc.tensor.matmul(psO[r % len(psO)][:, 0:D], self.matrix(sel, r), rows[:, r, :],
                                         start=True, stop=True)
                    if kinds:
                        if r % B == 0:
                            hold(pe, q["onehot"], i * U + r + B)
                        m = nc.tensor.matmul(psO[r % len(psO)][:, D:D + R], self.matrix(sel, r),
                                             self.matrix(hot, r, 8)[:, 0:R],
                                             start=True, stop=True)
                    m.then_inc(q["summed"], 1)

                def pick(i, r, b):
                    if r % B == 0:
                        hold(pe, q["selT"], i * U + r + B)
                        hold(pe, q["own"], i * U + r + B - U)
                    nc.tensor.matmul(psW[r // B][:, (r % B) * 8:(r % B + 1) * 8], self.matrix(selT, r),
                                     self.inv[:, bass.ds(b, 1), :], start=True, stop=True).then_inc(q["picked"], 1)
                pick.engine = "PE"
                if means:
                    self.flow(pe, [(0, pick), (8, total)], blocks_for=pick)
                else:
                    self.flow(pe, [(0, total)])

            @block.vector
            def _(dve):
                v = nc.vector
                v.tensor_copy(idx[:], source[:, 0:U]).then_inc(q["idx"], U)
                if kinds:
                    v.memset(nought[:], 0.0).then_inc(q["cleared"], 1)
                v.memset(self.acc[:], 0.0).then_inc(q["cleared"], 1)
                if kinds:
                    v.tensor_scalar(lower[:], self.iota[:], self.pidx[:, 0:1], None, ALU.is_lt)\
                        .then_inc(q["cleared"], 1)
                dve.wait_ge(q["cleared"], 3 if kinds else 1)

                def front(i, r, _):
                    self.select(dve, i, r, q, sel, q["summed"])
                    if r % B == 0:
                        v.tensor_tensor(hot[:, r // B, :].rearrange("p (s n) -> p s n", n=8),
                                        self.four(self.iota[:, 0:8]),
                                        self.spread(self.typ[:, bass.ds(i * U + r, B)], 8), ALU.is_equal)\
                            .then_inc(q["onehot"], B)
                    if means:
                        self.select_turned(dve, i, r, row, landed, selT, q["picked"], q["selT"])
                    if kinds:
                        if r % B == 0:
                            hold(dve, landed[r // B], i * 16 + 16)
                        hold(dve, q["ahead"], i * U + r + 1 - B)
                        col = bass.ds(i * U + r, 1)
                        v.scalar_tensor_tensor(same[:, r % B, :], self.matrix(row, r), self.srcf[:, col],
                                               lower[:], ALU.is_equal, ALU.mult, accum_out=self.ahead[:, col])\
                            .then_inc(q["ahead"], 1)

                def weigh(i, r, _):
                    if r % B < B - 1:
                        return
                    h, end = r // B, i * U + r + 1
                    m = sel[:, h, :].rearrange("p (s n) -> p s n", n=P)
                    hold(dve, q["picked"], end)
                    hold(dve, q["onehot"], end)
                    v.tensor_tensor(own[:, h, :], psW[h][:, 0:B * 8], hot[:, h, :], ALU.mult).then_inc(q["own"], B)
                    hold(dve, q["own"], end)
                    v.tensor_reduce(w2[:, h, :], own[:, h, :].rearrange("p (s n) -> p s n", n=8), AX.X, ALU.add)\
                        .then_inc(q["weight"], B)
                    hold(dve, q["weight"], end)
                    v.tensor_tensor(m, m, self.spread(w2[:, h, :], P), ALU.mult).then_inc(q["weighed"], B)

                def add(i, r, b):
                    self.add_sum(dve, i, r, b, q, psO, width, (self.acc,))
                    if r % B == B - 1:
                        self.refill(i, r, idx, source, q["idx"])
                add.engine = "DVE"
                if means:
                    self.flow(dve, [(0, front), (2, weigh), (10, add)], blocks_for=add)
                else:
                    self.flow(dve, [(0, front), (B, add)], blocks_for=add)

    def mean_in(self):
        nc, s = self.nc, self.s
        nb, R, S = s.nb, s.rels, s.steps + U
        seq = self.sem("mi_seq")
        with ExitStack() as c:
            at = Arena(self.aux)
            cnt = at.take([P, nb], F32)
            inv = at.take([P, nb], F32)
            dump = at.take([P, 1], F32)
            t = at.take([P, S], F32)
            f = at.take([P, S], F32)
            block = c.enter_context(nc.Block())

            @block.vector
            def _(dve):
                v = nc.vector
                do = Chain(dve, seq)
                do(v.tensor_scalar(self.inv[:, :, 0:R], self.acc[:, :, D:D + R], 1.0, None, ALU.max))
                do(v.reciprocal(self.inv[:, :, 0:R], self.inv[:, :, 0:R]))
                do(v.memset(self.inv[:, :, R:8], 1.0))
                do(v.tensor_reduce(cnt[:], self.acc[:, :, D:D + R], AX.X, ALU.add))
                do(v.tensor_scalar(self.gin[:], cnt[:], 1.0, None, ALU.min))
                do(v.tensor_scalar(cnt[:], cnt[:], 1.0, None, ALU.max))
                do(v.reciprocal(inv[:], cnt[:]))
                a = self.acc[:, :, 0:D]
                do(v.tensor_tensor(a, a, inv[:].rearrange("p (b o) -> p b o", o=1).broadcast_to([P, nb, D]), ALU.mult))
                do(v.tensor_scalar(dump[:], self.pidx[:], float(nb * P), None, ALU.add))
                do(v.tensor_scalar(f[:, 0:s.steps], self.ahead[:, 0:s.steps], 0.0, None, ALU.is_equal))
                do(v.tensor_scalar(t[:, 0:s.steps], self.srcf[:, 0:s.steps], dump[:, 0:1], None, ALU.subtract))
                do(v.tensor_tensor(t[:, 0:s.steps], t[:, 0:s.steps], f[:, 0:s.steps], ALU.mult))
                do(v.tensor_scalar(t[:, 0:s.steps], t[:, 0:s.steps], dump[:, 0:1], None, ALU.add))
                do(v.tensor_copy(self.sidx[:, 0:s.steps], t[:, 0:s.steps]))
                do(v.tensor_scalar(t[:], self.srcf[:], float(R), None, ALU.mult))
                do(v.tensor_tensor(t[:], t[:], self.typ[:], ALU.add))
                do(v.tensor_copy(self.gidx[:], t[:]))

    def scatter_out(self):
        nc, s, go = self.nc, self.s, self.setup_done
        turns = s.steps // U
        q = {k: self.sem(f"so_{k}") for k in ("idx", "selT", "same", "taken", "vals", "counts", "joined", "sums")}
        scattered = [self.sem(f"so_scattered{r}") for r in range(U)]
        landed = [self.sem(f"so_landed{h}") for h in range(G)]
        landed_src = [self.sem(f"so_landed_src{h}") for h in range(G)]
        with ExitStack() as c:
            at = Arena(self.aux, self.aux2)
            idx = at.take([P, U], I32)
            relrow = at.take([P, G, B * P])
            srcrow = at.take([P, G, B * P])
            selT = at.take([P, G, B * P])
            same = at.take([P, G, B * P])
            vals = at.take([P, U, 136])
            sums = at.take([P, U, 136])
            psE = [self.ps(f"so_pe{h}", c) for h in range(G)]
            psC = [self.ps(f"so_pc{j}", c) for j in range(4)]
            block = c.enter_context(nc.Block())

            @block.gpsimd
            def _(pool):
                def scatter(i, r, _):
                    hold(pool, q["idx"], i * U + r + 1)
                    hold(pool, q["sums"], i * U + r + 1)
                    before = r - TABLES
                    if before < 0:
                        before, j = before + U, i - 1
                    else:
                        j = i
                    if not isinstance(j, int) or j >= 0:
                        hold(pool, scattered[before], j * 16 + 16)
                    clear_ahead(pool, self.issued)
                    nc.gpsimd.indirect_dma_start(self.t_out[r % TABLES], bass.IndirectOffsetOnAxis(idx[:, r:r + 1], 0),
                                                 sums[:, r, :], None, compute_op=ALU.add)\
                        .then_inc(scattered[r], 16)
                self.flow(pool, [(0, scatter)])
                for r in range(U):
                    pool.wait_ge(scattered[r], 16 * turns)

            @block.sync
            def _(sp):
                def rel(i, r, _):
                    self.load_rows(sp, i, r, self.t_relrow, relrow, q["selT"], landed)
                    self.load_rows(sp, i, r, self.t_srcrow, srcrow, q["same"], landed_src)
                self.flow(sp, [(0, rel)])

            @block.scalar
            def _(act):
                a = nc.scalar

                def taken(i, r, _):
                    if r % B == B - 1:
                        k = r - r % B
                        hold(act, q["taken"], i * U + r + 1, go)
                        hold(act, q["joined"], i * U + r + 1 - U, go)
                        a.activation(vals[:, k:k + B, 0:D], psE[r // B][:].rearrange("p (s d) -> p s d", d=D),
                                     ACT.Copy).then_inc(q["vals"], B)
                        a.activation(vals[:, k:k + B, D:136], self.spread(self.mask[:, bass.ds(i * U + k, B)], 8),
                                     ACT.Copy).then_inc(q["counts"], B)

                def joined(i, r, _):
                    hold(act, q["joined"], i * U + r + 1, go)
                    hold(act, scattered[r], i * 16, go)
                    a.activation(sums[:, r, :], psC[r % 4][:, 0:136], ACT.Copy).then_inc(q["sums"], 1)
                self.flow(act, [(0, taken), (6, joined)])

            @block.tensor
            def _(pe):
                def take(i, r, b):
                    if r % B == 0:
                        hold(pe, q["selT"], i * U + r + B)
                        hold(pe, q["vals"], i * U + r + B - U)
                    nc.tensor.matmul(psE[r // B][:, (r % B) * D:(r % B + 1) * D], self.matrix(selT, r),
                                     self.hn[:, bass.ds(b, 1), :], start=True, stop=True).then_inc(q["taken"], 1)
                take.engine = "PE"

                def join(i, r, _):
                    if r % B == 0:
                        hold(pe, q["vals"], i * U + r + B)
                        hold(pe, q["counts"], i * U + r + B)
                        hold(pe, q["same"], i * U + r + B)
                    hold(pe, q["sums"], i * U + r + 1 - 4)
                    nc.tensor.matmul(psC[r % 4][:, 0:136], self.matrix(same, r), vals[:, r, :],
                                     start=True, stop=True).then_inc(q["joined"], 1)
                self.flow(pe, [(0, take), (6, join)], blocks_for=take)

            @block.vector
            def _(dve):
                v = nc.vector

                def front(i, r, _):
                    self.select_turned(dve, i, r, relrow, landed, selT, q["taken"], q["selT"])
                    if r % B == 0:
                        h = r // B
                        hold(dve, landed_src[h], i * 16 + 16)
                        hold(dve, q["joined"], i * U + r + B - U)
                        v.tensor_tensor(same[:, h, :].rearrange("p (s n) -> p s n", n=P),
                                        srcrow[:, h, :].rearrange("p (s n) -> p s n", n=P),
                                        self.spread(self.srcf[:, bass.ds(i * U + r, B)], P), ALU.is_equal)\
                            .then_inc(q["same"], B)

                def back(i, r, _):
                    hold(dve, scattered[r], i * 16, go if r % B == B - 1 else None)
                    if r % B == B - 1:
                        k = r - r % B
                        cols = bass.ds(i * U + k, B)
                        v.tensor_copy(idx[:, k:k + B], self.sidx[:, cols]).then_inc(q["idx"], B)

                self.flow(dve, [(0, front), (4, back)])

    def mean_out(self):
        nc, s = self.nc, self.s
        nb = s.nb
        half = nb // 2
        seq = self.sem("mo_seq")
        loaded = [self.sem(f"mo_loaded{j}") for j in range(2)]
        added = [self.sem(f"mo_added{j}") for j in range(2)]
        buf = self.wts[:, 0:nb * 136].rearrange("p (b d) -> p b d", d=136)
        with ExitStack() as c:
            at = Arena(self.aux)
            cnt = at.take([P, nb], F32)
            block = c.enter_context(nc.Block())

            @block.sync
            def _(sp):
                for k in range(TABLES):
                    for j in range(2):
                        if k:
                            sp.wait_ge(added[j], k)
                        sp.dma_start(buf[:, j * half:(j + 1) * half, :],
                                     self.t_out[k][j * half * P:(j + 1) * half * P, :]
                                     .rearrange("(b p) d -> p b d", p=P)).then_inc(loaded[j], 16)

            @block.vector
            def _(dve):
                v = nc.vector
                do = Chain(dve, seq)
                for k in range(TABLES):
                    for j in range(2):
                        a = self.aux2[:, j * half:(j + 1) * half, :]
                        dve.wait_ge(loaded[j], 16 * (k + 1))
                        if k == 0:
                            m = v.tensor_copy(a, buf[:, j * half:(j + 1) * half, :])
                        else:
                            dve.wait_ge(added[j], k)
                            m = v.tensor_tensor(a, a, buf[:, j * half:(j + 1) * half, :], ALU.add)
                        m.then_inc(added[j], 1)
                for j in range(2):
                    dve.wait_ge(added[j], TABLES)
                flag = self.aux2[:, :, 135:136].rearrange("p b o -> p (b o)")
                do(v.tensor_scalar(self.gout[:], flag, 1.0, None, ALU.min))
                do(v.tensor_scalar(cnt[:], flag, 1.0, None, ALU.max))
                do(v.reciprocal(cnt[:], cnt[:]))
                a = self.aux2[:, :, 0:D]
                do(v.tensor_tensor(a, a, cnt[:].rearrange("p (b o) -> p b o", o=1).broadcast_to([P, nb, D]), ALU.mult))

    def gru(self):
        nc, s, io = self.nc, self.s, self.io
        q = self.product_sems("gru")
        arrays = [self.aux, self.aux2, self.hn]
        blank, gates_made, asked, n_made = (self.sem(f"gru_{k}") for k in ("blank", "gates_made", "asked", "n_made"))
        steps = [self.sem(f"gru_step{k}") for k in range(4)]
        with ExitStack() as c:
            at = Arena(self.acc)
            w, stage, turned, psT, psO = self.product_memory("gru", c, 3, 3 * 4 * D, at)
            wk = w.rearrange("p (k n) -> p k n", k=3)
            bi = at.take([P, 4 * D], F32)
            bh = at.take([P, 4 * D], F32)
            g = self.sb("gru_sums", [P, 2, 4 * D], F32, c)
            rz = self.sb("gru_gates", [P, 2, 2 * D], F32, c)
            t = self.sb("gru_t", [P, 2, D], F32, c)
            n = self.sb("gru_n", [P, 2, D], F32, c)
            block = c.enter_context(nc.Block())

            @block.sync
            def _(sp):
                wi, wh = io["w_ih_t"], io["w_hh_t"]
                sp.wait_ge(blank, 1)
                for k in range(2):
                    sp.dma_start(wk[:, k, 0:3 * D], wi[k * D:(k + 1) * D, :]).then_inc(q["loaded"], 16)
                sp.dma_start(wk[:, 2, 0:2 * D], wh[:, 0:2 * D]).then_inc(q["loaded"], 16)
                sp.dma_start(wk[:, 2, 3 * D:4 * D], wh[:, 2 * D:3 * D]).then_inc(q["loaded"], 16)
                sp.dma_start(bi[:, 0:3 * D], self.bcast_row(io["b_ih"], 3 * D)).then_inc(q["loaded"], 16)
                sp.dma_start(bh[:, 0:2 * D], self.bcast_row(io["b_hh"][0:2 * D], 2 * D)).then_inc(q["loaded"], 16)
                sp.dma_start(bh[:, 3 * D:4 * D], self.bcast_row(io["b_hh"][2 * D:3 * D], D)).then_inc(q["loaded"], 16)

            @block.scalar
            def _(act):
                a = nc.scalar
                rows, copy = self.product_scalar(act, q, arrays, stage, turned, psT)

                def gates(i, j, _):
                    b = 2 * i + j
                    hold(act, q["read"], b + 1)
                    hold(act, q["finished"], b - 1)
                    a.activation(rz[:, j, :], g[:, j, 0:2 * D], ACT.Sigmoid).then_inc(gates_made, 1)

                def candidate(i, j, _):
                    hold(act, asked, 2 * i + j + 1)
                    a.activation(n[:, j, :], t[:, j, :], ACT.Tanh).then_inc(n_made, 1)
                self.flow(act, [(0, rows), (1, copy), (2, gates), (3, candidate)], count=s.nb, unit=2)

            @block.tensor
            def _(pe):
                def multiply(j):
                    for k in range(3):
                        m = nc.tensor.matmul(psO[j][:], turned[:, j, k * D:(k + 1) * D], wk[:, k, :],
                                             start=(k == 0), stop=(k == 2))
                    return m
                self.product_tensor(pe, q, stage, turned, psT, 3, 7, multiply)

            @block.vector
            def _(dve):
                v = nc.vector
                do = Chain(dve, q["seq"])
                do(v.memset(bi[:], 0.0))
                do(v.memset(bh[:], 0.0))
                v.memset(w[:], 0.0).then_inc(blank, 1)
                dve.wait_ge(q["loaded"], 16 * 7)
                do(v.tensor_tensor(bi[:], bi[:], bh[:], ALU.add))

                def bias(i, j, _):
                    hold(dve, q["product"], 2 * i + j + 1)
                    hold(dve, asked, 2 * i + j - 1)
                    v.tensor_tensor(g[:, j, :], psO[j][:], bi[:], ALU.add).then_inc(q["read"], 1)

                def ask(i, j, _):
                    b = 2 * i + j
                    hold(dve, gates_made, b + 1)
                    hold(dve, q["finished"], b - 1)
                    v.tensor_tensor(t[:, j, :], rz[:, j, 0:D], g[:, j, 3 * D:4 * D], ALU.mult).then_inc(steps[0], 1)
                    hold(dve, steps[0], b + 1)
                    v.tensor_tensor(t[:, j, :], t[:, j, :], g[:, j, 2 * D:3 * D], ALU.add).then_inc(asked, 1)

                def finish(i, j, _):
                    b = 2 * i + j
                    one = bass.ds(b, 1)
                    h = self.hn[:, one, :].rearrange("p o d -> p (o d)")
                    x = self.x[:, one, :].rearrange("p o d -> p (o d)")
                    hold(dve, n_made, b + 1)
                    v.tensor_tensor(t[:, j, :], h, n[:, j, :], ALU.subtract).then_inc(steps[1], 1)
                    v.tensor_tensor(x, x, n[:, j, :], ALU.add).then_inc(steps[3], 1)
                    hold(dve, steps[1], b + 1)
                    v.tensor_tensor(t[:, j, :], t[:, j, :], rz[:, j, D:2 * D], ALU.mult).then_inc(steps[2], 1)
                    hold(dve, steps[2], b + 1)
                    hold(dve, steps[3], b + 1)
                    v.tensor_tensor(x, x, t[:, j, :], ALU.add).then_inc(q["finished"], 1)
                self.flow(dve, [(0, bias), (1, ask), (2, finish)], count=s.nb, unit=2)

    def norm(self, name, plus=None):
        nc, s = self.nc, self.s
        seq, n = self.sem(f"{name}_seq"), self.norm_sems(name)
        with ExitStack() as c:
            sums, rstd = self.sb("sums", [P, s.nb], F32, c), self.sb("rstd", [P, s.nb], F32, c)
            block = c.enter_context(nc.Block())

            @block.scalar
            def _(act):
                self.norm_scalar(act, sums, rstd, n)

            @block.vector
            def _(dve):
                do = Chain(dve, seq)
                if plus is not None:
                    do(nc.vector.tensor_tensor(self.x[:], self.x[:], plus, ALU.add))
                self.norm_vector(dve, do, sums, rstd, n)

    def relation_nodes(self):
        nc, s, io = self.nc, self.s, self.io
        K, W, R = s.node_types, s.node_types * D, s.rels * D
        q = self.product_sems("rel")
        cuts = [R * k // 2 for k in range(3)]
        assert R % 2 == 0 and cuts[1] <= 512 and W <= 512
        kept = self.sem("rel_kept")
        stored = [self.sem(f"rel_stored{j}") for j in range(2)]
        steps = [self.sem(f"root_step{k}") for k in range(K)]
        with ExitStack() as c:
            at = Arena(self.aux)
            w, stage, turned, psT, psO = self.product_memory("rel", c, 1, R + W, at, banks=3)
            b = at.take([P, W])
            g = self.sb("root_g", [P, 2, W], F32, c)
            rows = at.take([P, 2, R])
            typ = self.sb("node_type", [P, s.nb], I32, c)
            own = self.sb("own_type", [P, K, s.nb], F32, c)
            block = c.enter_context(nc.Block())

            @block.sync
            def _(sp):
                sp.dma_start(w[:, 0:R], io["rel_w_t"]).then_inc(q["loaded"], 16)
                sp.dma_start(w[:, R:R + W], io["root_w_t"]).then_inc(q["loaded"], 16)
                sp.dma_start(b[:], self.bcast_row(io["root_b"], W)).then_inc(q["loaded"], 16)
                sp.dma_start(typ[:], io["node_type_t"]).then_inc(q["loaded"], 16)
                table = self.t_rel.rearrange("(b p) r d -> b p (r d)", p=P)

                def send(i, j, _):
                    n = 2 * i + j
                    hold(sp, kept, (n + 1) * 2)
                    sp.dma_start(table[bass.ds(n, 1), :, :].rearrange("o p d -> p (o d)"), rows[:, j, :])\
                        .then_inc(stored[j], 16)
                self.flow(sp, [(0, send)], count=s.nb, unit=2)
                for j in range(2):
                    sp.wait_ge(stored[j], 16 * (s.nb // 2))

            @block.scalar
            def _(act):
                front, copy = self.product_scalar(act, q, [self.hn], stage, turned, psT)

                def keep(i, j, _):
                    hold(act, q["product"], 2 * i + j + 1)
                    hold(act, stored[j], i * 16)
                    for k in range(2):
                        nc.scalar.activation(rows[:, j, cuts[k]:cuts[k + 1]], psO[3 * j + k][:, 0:cuts[1]],
                                             ACT.Copy).then_inc(kept, 1)
                self.flow(act, [(0, front), (1, copy), (2, keep)], count=s.nb, unit=2)

            @block.tensor
            def _(pe):
                pe.wait_ge(q["loaded"], 64)

                def turn(i, j, _):
                    n = 2 * i + j
                    hold(pe, q["turned"], n - 1)
                    hold(pe, q["staged"], n + 1)
                    nc.tensor.transpose(psT[j][:, 0:D], stage[:, j, :], self.ident[:]).then_inc(q["turned_ps"], 1)

                def product(i, j, _):
                    n = 2 * i + j
                    hold(pe, q["turned"], n + 1)
                    hold(pe, kept, (n - 1) * 2)
                    hold(pe, q["read"], n - 1)
                    for k, (first, last) in enumerate(((0, cuts[1]), (cuts[1], R), (R, R + W))):
                        m = nc.tensor.matmul(psO[3 * j + k][:, 0:last - first], turned[:, j, :], w[:, first:last],
                                             start=True, stop=True)
                    m.then_inc(q["product"], 1)
                self.flow(pe, [(0, turn), (1, product)], count=s.nb, unit=2)

            @block.vector
            def _(dve):
                v = nc.vector
                do = Chain(dve, q["seq"])
                dve.wait_ge(q["loaded"], 64)
                for k in range(K):
                    do(v.tensor_scalar(own[:, k, :], typ[:], float(k), None, ALU.is_equal))

                def bias(i, j, _):
                    n = 2 * i + j
                    hold(dve, q["product"], n + 1)
                    hold(dve, steps[K - 1], n - 1)
                    v.tensor_tensor(g[:, j, :], psO[3 * j + 2][:, 0:W], b[:], ALU.add).then_inc(q["read"], 1)

                def add(i, j, _):
                    n = 2 * i + j
                    one = bass.ds(n, 1)
                    x = self.x[:, one, :].rearrange("p o d -> p (o d)")
                    hold(dve, q["read"], n + 1)
                    for k in range(K):
                        v.scalar_tensor_tensor(x, g[:, j, k * D:(k + 1) * D], own[:, k, one], x,
                                               ALU.mult, ALU.add).then_inc(steps[k], 1)
                        hold(dve, steps[k], n + 1)
                self.flow(dve, [(0, bias), (1, add)], count=s.nb, unit=2)

    def edge_rows(self):
        nc, s, io, go = self.nc, self.s, self.io, self.setup_done
        H, turns = s.heads3, s.steps // U
        q = {k: self.sem(f"er_{k}") for k in ("idx", "selT", "projected", "target", "z", 
                                              "inverse", "weighed", "part", "part2", "reduced", "logits", "consts", "att")}
        gathered = [self.sem(f"er_gathered{r}") for r in range(U)]
        stored = [self.sem(f"er_stored{h}") for h in range(G)]
        loaded = [self.sem(f"er_loaded{r}") for r in range(U)]
        landed = [self.sem(f"er_landed{h}") for h in range(G)]
        with ExitStack() as c:
            at = Arena(self.hn, self.acc, self.aux2)
            rows = at.take([P, U, D])
            att = at.take([P, U, D])
            ea = at.take([P, U, D])
            idx = at.take([P, U], I32)
            relrow = at.take([P, G, B * P])
            selT = at.take([P, G, B * P])
            z = at.take([P, G, B * D])
            u = at.take([P, G, B * D])
            zw = at.take([P, G, B * D])
            limit = at.take([P, 1])
            we = at.take([P, D])
            attn = at.take([P, D // H])
            attn4 = at.take([P, B * D])
            attn_b = at.take([P, 1])
            psA = [self.ps(f"er_pa{h}", c) for h in range(G)]
            psE = [self.ps(f"er_pe{h}", c) for h in range(G)]
            block = c.enter_context(nc.Block())

            @block.gpsimd
            def _(pool):
                def gather(i, r, _):
                    hold(pool, q["idx"], i * U + r + 1)
                    hold(pool, q["att"], i * U + r + 1 - U)
                    clear_ahead(pool, self.issued)
                    nc.gpsimd.indirect_dma_start(rows[:, r, :], None, self.t_sent,
                                                 bass.IndirectOffsetOnAxis(idx[:, r:r + 1], 0))\
                        .then_inc(gathered[r], 16)
                self.flow(pool, [(0, gather)])

            @block.sync
            def _(sp):
                sp.dma_start(we[:], io["We"]).then_inc(q["consts"], 16)
                sp.dma_start(attn[:], self.bcast_row(io["attn_w"], D // H)).then_inc(q["consts"], 16)
                sp.dma_start(attn_b[:], self.bcast_row(io["attn_b"], 1)).then_inc(q["consts"], 16)

                def load(i, r, t):
                    self.load_rows(sp, i, r, self.t_relrow, relrow, q["selT"], landed)
                    hold(sp, q["projected"], i * U + r + 1 - U)
                    sp.dma_start(ea[:, r, :], io["edge_t"][bass.ds(t, 1), :, :]
                                 .rearrange("o p d -> p (o d)")).then_inc(loaded[r], 16)
                load.engine = "SP"

                def send(i, r, _):
                    if r % B == B - 1:
                        k = r - r % B
                        hold(sp, q["att"], i * U + r + 1)
                        sp.dma_start(self.t_rows[bass.ds(i * U + k, B), :, :].rearrange("s p d -> p s d"),
                                     att[:, k:k + B, :]).then_inc(stored[r // B], 16)
                self.flow(sp, [(0, load), (14, send)], tiles_for=load)
                for h in range(G):
                    sp.wait_ge(stored[h], 16 * turns)

            @block.scalar
            def _(act):
                def inverse(i, r, _):
                    if r % B:
                        return
                    k = r // B
                    uk = u[:, k, :]
                    hold(act, q["z"], i * U + r + B, go)
                    hold(act, q["part2"], G * i + k + 1 - G, go)
                    then = Turn(act, q["part"], (G * i + k) * 4, go)
                    then(nc.scalar.activation(uk, z[:, k, :], ACT.Relu, scale=-1.0, bias=limit[:, 0:1]))
                    then(nc.scalar.activation(uk, uk, ACT.Exp, scale=-1.0, bias=limit[:, 0:1]))
                    then(nc.scalar.activation(uk, uk, ACT.Square, bias=1.0))
                    then(nc.scalar.activation(uk, uk, ACT.Ln, bias=1.0))
                    nc.scalar.activation(uk, uk, ACT.Exp, scale=-1.0).then_inc(q["inverse"], 1)
                act.preload_act_table_set("natural_log_exp_and_others")
                act.wait_ge(q["consts"], 50)
                self.flow(act, [(0, inverse)])

            @block.tensor
            def _(pe):
                pe.wait_ge(q["consts"], 48)

                def project(i, r, _):
                    hold(pe, loaded[r], i * 16 + 16)
                    if r % B == 0:
                        hold(pe, q["att"], i * U + r + B - U)
                    nc.tensor.matmul(psA[r // B][:, (r % B) * D:(r % B + 1) * D], ea[:, r, :], we[:], start=True, stop=True)\
                        .then_inc(q["projected"], 1)

                def target(i, r, b):
                    hold(pe, q["selT"], i * U + r + 1)
                    if r % B == 0:
                        hold(pe, q["z"], i * U + r + B - U)
                    nc.tensor.matmul(psE[r // B][:, (r % B) * D:(r % B + 1) * D], self.matrix(selT, r),
                                     self.aux[:, bass.ds(b, 1), :], start=True, stop=True)\
                        .then_inc(q["target"], 1)
                target.engine = "PE"
                self.flow(pe, [(0, project), (0, target)], blocks_for=target)

            @block.vector
            def _(dve):
                v = nc.vector
                v.tensor_copy(idx[:], self.src[:, 0:U]).then_inc(q["idx"], U)
                dve.wait_ge(q["consts"], 48)
                v.tensor_copy(attn4[:].rearrange("p (b f) -> p b f", f=D // H),
                              attn[:].rearrange("p (o f) -> p o f", o=1).broadcast_to([P, B * H, D // H]))\
                    .then_inc(q["consts"], 1)
                v.memset(limit[:], CAP).then_inc(q["consts"], 1)
                dve.wait_ge(q["consts"], 50)

                def select(i, r, _):
                    self.select_turned(dve, i, r, relrow, landed, selT, q["target"], q["selT"])

                def add(i, r, _):
                    hold(dve, gathered[r], i * 16 + 16, go if r % B == B - 1 else None)
                    if r % B < B - 1:
                        return
                    k, h = r - r % B, r // B
                    self.refill(i, r, idx, self.src, q["idx"])
                    hold(dve, q["projected"], i * U + r + 1)
                    hold(dve, stored[h], i * 16)
                    v.tensor_tensor(att[:, k:k + B, :], rows[:, k:k + B, :],
                                    psA[h][:].rearrange("p (s d) -> p s d", d=D), ALU.add)\
                        .then_inc(q["att"], B)
                    hold(dve, q["target"], i * U + r + 1)
                    hold(dve, q["reduced"], G * i + h + 1 - G)
                    hold(dve, q["att"], i * U + r + 1)
                    v.tensor_tensor(z[:, h, :], att[:, k:k + B, :].rearrange("p s d -> p (s d)"), psE[h][:],
                                    ALU.add).then_inc(q["z"], B)

                def weigh(i, r, _):
                    if r % B == B - 1:
                        h = r // B
                        hold(dve, q["z"], i * U + r + 1)
                        v.tensor_tensor(zw[:, h, :], z[:, h, :], attn4[:], ALU.mult).then_inc(q["weighed"], 1)

                def mish(i, r, _):
                    if r % B < B - 1:
                        return
                    k = r // B
                    hold(dve, q["inverse"], G * i + k + 1)
                    hold(dve, q["weighed"], G * i + k + 1)
                    v.scalar_tensor_tensor(zw[:, k, :], u[:, k, :], 0.5, zw[:, k, :], ALU.subtract, ALU.mult)\
                        .then_inc(q["part2"], 1)
                    hold(dve, q["part2"], G * i + k + 1, go)
                    v.tensor_reduce(self.w8[:, bass.ds(i * U + k * B, B), 0:H],
                                    zw[:, k, :].rearrange("p (b h f) -> p b h f", h=H, f=D // H),
                                    AX.X, ALU.add).then_inc(q["reduced"], 1)
                self.flow(dve, [(0, select), (5, add), (7, weigh), (13, mish)])
                dve.wait_ge(q["reduced"], G * turns)
                v.tensor_scalar(self.w8[:, :, 0:H], self.w8[:, :, 0:H], -2.0, attn_b[:, 0:1], ALU.mult, ALU.add)\
                    .then_inc(q["logits"], 1)
                dve.wait_ge(q["logits"], 1)

    def merge_logits(self):
        nc, s, go = self.nc, self.s, self.setup_done
        T, NF, S, H = s.tiles, s.blocks - 1, s.steps, s.heads3
        seq, moved = self.sem("ml_seq"), self.sem("ml_moved")
        with nc.Block() as block:
            @block.vector
            def _(dve):
                v = nc.vector
                do = Chain(dve, seq)
                w = self.w8[:, :, 0:H]
                do(v.tensor_tensor(w, w, self.mask[:, 0:S].rearrange("p (s o) -> p s o", o=1)
                                   .broadcast_to([P, S, H]), ALU.mult))
                def move(k, t):
                    a = self.w8[:, bass.ds(t, 1), 0:H]
                    hold(dve, moved, k, go)
                    v.tensor_tensor(a, a, self.w8[:, bass.ds(k + T, 1), 0:H], ALU.add).then_inc(moved, 1)
                numbered(nc, dve, self.til, T + U, NF, T - 1, move)
                dve.wait_ge(moved, NF)

    def edge_softmax(self):
        nc, s = self.nc, self.s
        T, H, C, CT, ST = s.tiles, s.heads3, SCAN_CHUNKS, s.ctiles, s.stiles
        L, NF = CT * P, s.blocks - 1
        per = P // H
        groups = -(-ST // per)
        names = ("seq", "compact", "turned", "copied", "written", "loaded", "rows", "carry", "back",
                 "backturned", "sub", "exped", "moved")
        q = {k: self.sem(f"es_{k}") for k in names}
        RING = 8
        stage_free = [self.sem(f"es_stage{j}") for j in range(RING)]
        arrived = [self.sem(f"es_arrived{j}") for j in range(RING)]
        flat = lambda a: a[:].rearrange("p b d -> p (b d)")
        accf, auxf, aux2f, hnf = flat(self.acc), flat(self.aux), flat(self.aux2), flat(self.hn)
        assert 2 * L <= self.s.nb * 136 and L <= self.s.nb * D and ST * H <= L and H * C == P
        logits = accf[:, 0:ST * H]
        run = accf[:, L:2 * L]
        seqd = aux2f[:, 0:L]
        here, other = aux2f[:, L:2 * L].bitcast(I32), hnf[:, 0:L].bitcast(I32)
        reset = auxf[:, 0:L]
        with ExitStack() as c:
            stage = self.sb("es_stage", [P, RING, P], F32, c)
            edge = self.sb("es_edge", [P, 2], F32, c)
            row = self.sb("es_row", [1, 2 * P], F32, c)
            chain = self.sb("es_chain", [1, H * (C + 1)], F32, c)
            first = self.sb("es_first", [1, P], F32, c)
            start = self.sb("es_start", [P, 1], F32, c)
            ps = [self.ps(f"es_ps{j}", c) for j in range(2)]
            psR = self.ps("es_pr", c)
            psB = [self.ps(f"es_pb{j}", c) for j in range(2)]
            block = c.enter_context(nc.Block())
            dseq = self.io["dst_seq"]
            tseq = self.t_seq.rearrange("t h e -> (t h) e")
            tmax = self.t_max.rearrange("t h e -> (t h) e")

            def chunked(t, h):
                return t[:, h, :].rearrange("(c j) e -> c j e", c=C)

            @block.sync
            def _(sp):
                for h in range(H):
                    for off, dst in ((1, here), (0, other)):
                        sp.dma_start(dst[h * C:(h + 1) * C, :], dseq[off:off + C * L].rearrange("(c l) -> c l", c=C))\
                            .then_inc(q["loaded"], 16)
                for g in range(groups):
                    sp.wait_ge(q["copied"], g + 1)
                    sp.dma_start(tseq[g * P:(g + 1) * P, :], stage[:, g % RING, :]).then_inc(stage_free[g % RING], 16)
                for j in range(RING):
                    sp.wait_ge(stage_free[j], 16 * len(range(j, groups, RING)))
                for h in range(H):
                    sp.dma_start(seqd[h * C:(h + 1) * C, :].rearrange("p (j e) -> p j e", e=P), chunked(self.t_seq, h))\
                        .then_inc(q["written"], 16)
                sp.wait_ge(q["carry"], 5)
                for h in range(H):
                    sp.dma_start(other[h * C:(h + 1) * C, :], dseq[2:2 + C * L].rearrange("(c l) -> c l", c=C))\
                        .then_inc(q["loaded"], 16)
                sp.wait_ge(q["carry"], 10)
                for h in range(H):
                    sp.dma_start(chunked(self.t_max, h), run[h * C:(h + 1) * C, :].rearrange("p (j e) -> p j e", e=P))\
                        .then_inc(q["back"], 16)
                sp.wait_ge(q["back"], 16 * H)
                for g in range(groups):
                    if g >= RING:
                        sp.wait_ge(q["backturned"], g + 1 - RING)
                    sp.dma_start(stage[:, g % RING, :], tmax[g * P:(g + 1) * P, :]).then_inc(arrived[g % RING], 16)

            @block.tensor
            def _(pe):
                pe.wait_ge(q["compact"], 1)
                for g in range(groups):
                    if g >= 2:
                        pe.wait_ge(q["copied"], g - 1)
                    nc.tensor.transpose(ps[g % 2][:, 0:P], logits[:, g * P:(g + 1) * P], self.ident[:])\
                        .then_inc(q["turned"], 1)
                for d in range(2):
                    pe.wait_ge(q["carry"], 5 * d + 1)
                    for k in range(2):
                        nc.tensor.transpose(psR[0:1, k * P:(k + 1) * P], edge[:, k:k + 1], self.ident[:])\
                            .then_inc(q["rows"], 1)
                    pe.wait_ge(q["carry"], 5 * d + 4)
                    nc.tensor.matmul(psR[:, 2 * P:2 * P + 1], first[:], self.ones[0:1, 0:1], start=True, stop=True)\
                        .then_inc(q["rows"], 1)
                for g in range(groups):
                    pe.wait_ge(arrived[g % RING], 16 * (g // RING + 1))
                    if g >= 2:
                        pe.wait_ge(q["sub"], g - 1)
                    nc.tensor.transpose(psB[g % 2][:, 0:P], stage[:, g % RING, :], self.ident[:])\
                        .then_inc(q["backturned"], 1)

            @block.scalar
            def _(act):
                for g in range(groups):
                    act.wait_ge(q["turned"], g + 1)
                    if g >= RING:
                        act.wait_ge(stage_free[g % RING], 16 * (g // RING))
                    nc.scalar.activation(stage[:, g % RING, :], ps[g % 2][:, 0:P], ACT.Copy).then_inc(q["copied"], 1)
                act.wait_ge(q["sub"], groups)
                nc.scalar.activation(self.w8[:, 0:T, 0:H], self.w8[:, 0:T, 0:H], ACT.Exp).then_inc(q["exped"], 1)

            @block.vector
            def _(dve):
                v = nc.vector
                do = Chain(dve, q["seq"])
                do(v.memset(logits, 0.0))
                v.tensor_copy(logits[:, 0:T * H].rearrange("p (t h) -> p t h", h=H), self.w8[:, 0:T, 0:H])\
                    .then_inc(q["compact"], 1)
                dve.wait_ge(q["loaded"], 32 * H)
                for d in range(2):
                    if d == 1:
                        dve.wait_ge(q["loaded"], 48 * H)
                    do(v.tensor_tensor(reset, here, other, ALU.not_equal))
                    do(v.tensor_scalar(reset, reset, -BIG, None, ALU.mult))
                    if d == 0:
                        dve.wait_ge(q["written"], 16 * H)
                    way = (lambda a: a) if d == 0 else (lambda a: a[:, ::-1])
                    data = seqd if d == 0 else run
                    out = run if d == 0 else seqd
                    do(v.tensor_tensor_scan(way(out), way(reset), way(data), -BIG, ALU.add, ALU.max))
                    end = L - 1 if d == 0 else 0
                    do(v.tensor_copy(edge[:, 0:1], out[:, end:end + 1]))
                    do(v.memset(chain[:], -BIG))
                    v.tensor_reduce(edge[:, 1:2], reset, AX.X, ALU.min).then_inc(q["carry"], 1)
                    dve.wait_ge(q["rows"], 3 * d + 2)
                    v.tensor_copy(row[:], psR[0:1, 0:2 * P]).then_inc(q["carry"], 1)
                    dve.wait_ge(q["carry"], 5 * d + 2)
                    for h in range(H):
                        a = row[0:1, h * C:(h + 1) * C]
                        r = row[0:1, P + h * C:P + (h + 1) * C]
                        at = h * (C + 1)
                        if d == 0:
                            o = chain[0:1, at + 1:at + 1 + C]
                        else:
                            a, r, o = a[:, ::-1], r[:, ::-1], chain[0:1, at:at + C][:, ::-1]
                        do(v.tensor_tensor_scan(o, r, a, -BIG, ALU.add, ALU.max))
                    dve.sem_inc(q["carry"], 1)
                    off = 0 if d == 0 else 1
                    v.tensor_copy(first[:].rearrange("p (h c) -> p h c", h=H),
                                  chain[:].rearrange("p (h c) -> p h c", h=H)[:, :, off:off + C])\
                        .then_inc(q["carry"], 1)
                    dve.wait_ge(q["rows"], 3 * d + 3)
                    do(v.tensor_copy(start[:], psR[:, 2 * P:2 * P + 1]))
                    final = run
                    v.tensor_tensor_scan(way(final), way(reset), way(data), start[:, 0:1], ALU.add, ALU.max)\
                        .then_inc(q["carry"], 1)
                    dve.wait_ge(q["carry"], 5 * d + 5)
                for g in range(groups):
                    n = min(per, T - g * per)
                    dve.wait_ge(q["backturned"], g + 1)
                    if n > 0:
                        w = self.w8[:, g * per:g * per + n, 0:H]
                        m = v.tensor_tensor(w, w, psB[g % 2][:, 0:n * H].rearrange("p (t h) -> p t h", h=H), ALU.subtract)
                    else:
                        m = v.memset(edge[:], 0.0)
                    m.then_inc(q["sub"], 1)
                dve.wait_ge(q["exped"], 1)
                def move(k, t):
                    v.tensor_copy(self.w8[:, bass.ds(k + T, 1), 0:H], self.w8[:, bass.ds(t, 1), 0:H])\
                        .then_inc(q["moved"], 1)
                numbered(nc, dve, self.til, T + U, NF, T - 1, move)
                dve.wait_ge(q["moved"], NF)

    def output(self):
        nc, s, io = self.nc, self.s, self.io
        nb, H = s.nb, s.heads3
        seq, done, sent = self.sem("ou_seq"), self.sem("ou_done"), self.sem("ou_sent")
        with ExitStack() as c:
            den = self.sb("ou_den", [P, nb, H], F32, c)
            block = c.enter_context(nc.Block())

            @block.vector
            def _(dve):
                v = nc.vector
                do = Chain(dve, seq)
                do(v.tensor_scalar(den[:], self.acc[:, :, D:D + H], 1e-30, None, ALU.max))
                do(v.reciprocal(den[:], den[:]))
                for b in self.halves():
                    for h in range(H):
                        a = self.acc[:, b, h * (D // H):(h + 1) * (D // H)]
                        do(v.tensor_tensor(a, a, den[:, b, h:h + 1].broadcast_to([P, nb // 2, D // H]), ALU.mult))
                    v.tensor_tensor(self.x[:, b, :], self.x[:, b, :], self.acc[:, b, 0:D], ALU.add).then_inc(done, 1)

            @block.sync
            def _(sp):
                for k, b in enumerate(self.halves()):
                    sp.wait_ge(done, k + 1)
                    sp.dma_start(io["out"].rearrange("(b p) d -> p b d", p=P)[:, b, :], self.x[:, b, :])\
                        .then_inc(sent, 16)
                sp.wait_ge(sent, 32)

    def build(self):
        s, io = self.s, self.io
        with self.ctx:
            self.allocate()
            self.prepare()
            self.end_phase()
            self.gat_nodes()
            self.end_phase()
            self.gat_gather()
            self.end_phase()
            self.gat_softmax()
            self.end_phase()
            self.weighted_sum("gat_sum", s.heads0)
            self.end_phase()
            self.gat_output()
            self.end_phase()
            self.gather_sum("in_sum", self.t_h, self.src, kinds=True)
            self.end_phase()
            self.mean_in()
            self.end_phase()
            self.scatter_out()
            self.end_phase()
            self.mean_out()
            self.end_phase()
            self.node_products("a", [self.acc, self.aux2],
                               [(0, io["W_in_t"], [io["b_in"]], self.gin, self.aux, None),
                                (1, io["W_out_t"], [io["b_out"]], self.gout, self.aux2, None)])
            self.end_phase()
            self.gru()
            self.end_phase()
            self.norm("norm2")
            self.end_phase()
            self.relation_nodes()
            self.end_phase()
            self.gather_sum("rel_sum", self.t_rel.rearrange("n r d -> (n r) d"), self.gidx, means=True)
            self.end_phase()
            self.norm("norm3", plus=self.acc[:, :, 0:D])
            self.end_phase()
            self.node_products("ends", [self.hn],
                               [(0, io["Ws"], [io["Ws_b"], io["We_b"]], None, self.acc, self.t_sent),
                                (0, io["Wr"], [io["Wr_b"]], None, self.aux, None)])
            self.end_phase()
            self.edge_rows()
            self.end_phase()
            self.merge_logits()
            self.end_phase()
            self.edge_softmax()
            self.end_phase()
            self.weighted_sum("att_sum", s.heads3)
            self.end_phase()
            self.output()
            self.end_phase()



def kernel(x, src, dst, edge_attr_128, edge_type_7, node_type_4, **w):
    import concourse.bacc as bacc
    from concourse.bass_utils import run_bass_kernel_spmd

    x, src, dst, ea, et, nt = (np.asarray(a) for a in (x, src, dst, edge_attr_128, edge_type_7, node_type_4))
    w = {k: np.asarray(a) for k, a in w.items()}
    n, e = x.shape[0], src.shape[0]
    s = Shape(n, e, w["L0_gnn_a_src"].shape[1], w["L3_gnn_Ws_k"].shape[1], w["L2_gnn_rel_w"].shape[0],
              w["L2_gnn_root_w"].shape[0])
    far = (s.blocks + 1) * P

    def by_tile(a, fill):
        return np.ascontiguousarray(np.pad(a, (0, s.tiles * P - e), constant_values=fill).reshape(s.tiles, P).T)

    flat = lambda a: np.ascontiguousarray(a.reshape(-1))
    mat = lambda a: np.ascontiguousarray(a.reshape(D, -1))
    arrays = {
        "x": np.pad(x, ((0, s.nb * P - n), (0, 0))),
        "src_t": by_tile(src, 0), "dst_t": by_tile(dst, far), "type_t": by_tile(et, 0),
        "dst_seq": np.pad(dst, (1, s.stiles * P - e + 1), constant_values=(-1, far)),
        "edge_t": np.ascontiguousarray(
            np.pad(ea, ((0, s.tiles * P - e), (0, 0))).reshape(s.tiles, P, D).transpose(0, 2, 1)),
        "node_type_t": np.ascontiguousarray(np.pad(nt, (0, s.nb * P - n)).reshape(s.nb, P).T),
        "W_proj": w["L0_gnn_W_proj"], "a_src": flat(w["L0_gnn_a_src"]), "a_trg": flat(w["L0_gnn_a_trg"]),
        "gat_bias": w["L0_gnn_bias"],
        "W_in_t": w["L1_gnn_W_in"].T, "b_in": w["L1_gnn_b_in"],
        "W_out_t": w["L1_gnn_W_out"].T, "b_out": w["L1_gnn_b_out"],
        "w_ih_t": w["L1_gnn_w_ih"].T, "w_hh_t": w["L1_gnn_w_hh"].T,
        "b_ih": w["L1_gnn_b_ih"], "b_hh": w["L1_gnn_b_hh"],
        "rel_w_t": w["L2_gnn_rel_w"].transpose(2, 0, 1).reshape(D, -1),
        "root_w_t": w["L2_gnn_root_w"].transpose(2, 0, 1).reshape(D, -1), "root_b": flat(w["L2_gnn_root_b"]),
        "Ws": mat(w["L3_gnn_Ws_k"]), "Wr": mat(w["L3_gnn_Wr_k"]), "We": mat(w["L3_gnn_We_k"]),
        "Ws_b": flat(w["L3_gnn_Ws_b"]), "Wr_b": flat(w["L3_gnn_Wr_b"]), "We_b": flat(w["L3_gnn_We_b"]),
        "attn_w": flat(w["L3_gnn_attn_w"]), "attn_b": w["L3_gnn_attn_b"],
    }
    arrays = {k: np.ascontiguousarray(a) for k, a in arrays.items()}
    nc = bacc.Bacc("TRN2", target_bir_lowering=False, num_devices=1)
    io = {k: nc.dram_tensor(f"in_{k}", a.shape, mybir.dt.from_np(a.dtype), kind="ExternalInput").ap()
          for k, a in arrays.items()}
    io["out"] = nc.dram_tensor("out", (s.nb * P, D), F32, kind="ExternalOutput").ap()
    Program(nc, s, io).build()
    r = run_bass_kernel_spmd(nc, [{f"in_{k}": a for k, a in arrays.items()}], core_ids=[0])
    return r.results[0]["out"][:n]
```
